# Optimizing a Trainium2 kernel written in Bass

```python
import numpy as np
import jax
import jax.numpy as jnp

def _softmax(x, axis=-1):
    return jax.nn.softmax(x, axis=axis)

def _gelu(x):
    return jax.nn.gelu(x, approximate=True)

def _silu(x):
    return jax.nn.silu(x)

def _sigmoid(x):
    return jax.nn.sigmoid(x)

def _layernorm(x, axis=-1, eps=1e-05):
    m = jnp.mean(x, axis=axis, keepdims=True)
    v = jnp.var(x, axis=axis, keepdims=True)
    return (x - m) / jnp.sqrt(v + eps)

def _scatter_add(tgt, idx, src, axis=0):
    return tgt.at[idx].add(src)

def _segment_sum(src, seg, n):
    return jax.ops.segment_sum(src, seg, n)
kernel_name = 'mk_vit_tower_d1_tok_img512_r4_cc0452'

def setup_inputs(seed: int=0):
    np.random.seed(seed)
    _w = jnp.asarray

    def _rec_inputs():
        import jax
        import jax.numpy as jnp
        _rk = jax.random.key(seed)
        x = -0.000147625 + 0.999875 * jax.random.normal(jax.random.fold_in(_rk, 1), (64, 3, 224, 224), jnp.float32)
        return x
    x = _rec_inputs()

    def _L0_tok_setup():
        import jax, jax.numpy as jnp
        import numpy as np
        N_PATCHES = 8
        PATCH = 28
        C = 3
        IN_D = C * PATCH * PATCH
        HID = 128
        SEQ = N_PATCHES * N_PATCHES + 1

        def _positional_embedding(seq_len, dim):
            i = np.arange(seq_len)[:, None].astype(np.float32)
            j = np.arange(dim)[None, :].astype(np.float32)
            ang = i / np.power(100000.0, j / dim)
            pe = np.where(j % 2 == 0, np.sin(ang), np.cos(ang))
            return jnp.asarray(pe, dtype=jnp.float32)
        key = jax.random.key(seed)
        k1, k2, k3, k4 = jax.random.split(key, 4)
        B = 64
        X = jax.random.normal(k1, (B, C, 224, 224), dtype=jnp.float32)
        bound = 1.0 / np.sqrt(IN_D)
        W = jax.random.uniform(k2, (HID, IN_D), minval=-bound, maxval=bound, dtype=jnp.float32)
        b = jax.random.uniform(k3, (HID,), minval=-bound, maxval=bound, dtype=jnp.float32)
        class_token = jax.random.uniform(k4, (1, HID), dtype=jnp.float32)
        pos_embed = _positional_embedding(SEQ, HID)
        return {'X': X, 'W': W, 'b': b, 'class_token': class_token, 'pos_embed': pos_embed}
    _L0_tok_all = _L0_tok_setup()
    _L0_tok_in = {k: v for k, v in _L0_tok_all.items() if k in ('W', 'b', 'class_token', 'pos_embed')}
    del _L0_tok_all

    def _L0_attn_setup():
        import jax, jax.numpy as jnp
        import numpy as np
        STAGES = 3
        CAUSAL = True

        def _positional_encoding(T, W):
            half = W // 2
            t = jnp.arange(T, dtype=jnp.float32)
            freqs = 10000.0 ** (-jnp.arange(half, dtype=jnp.float32) / half)
            phi = t[:, None] * freqs[None, :]
            return jnp.concatenate([jnp.sin(phi), jnp.cos(phi)], axis=-1)
        key = jax.random.key(seed)
        k1, k2, k3 = jax.random.split(key, 3)
        B, T, W = (4, 512, 128)
        X = jax.random.normal(k1, (B, T, W), dtype=jnp.float32)
        W_proj = jax.random.normal(k2, (W, W, STAGES + 1), dtype=jnp.float32) * 0.02
        W_filt = jax.random.normal(k3, (W, W, STAGES), dtype=jnp.float32) * 0.02
        return {'X': X, 'W_proj': W_proj, 'W_filt': W_filt}
    _L0_attn_all = _L0_attn_setup()
    _L0_attn_in = {k: v for k, v in _L0_attn_all.items() if k in ('W_proj', 'W_filt')}
    del _L0_attn_all

    def _L0_ffn_setup():
        import jax, jax.numpy as jnp
        import numpy as np
        CAPACITY_FACTOR = 1.2
        key = jax.random.key(seed)
        k1, k2, k3 = jax.random.split(key, 3)
        B, S, D, E = (8, 1024, 128, 16)
        x = jax.random.normal(k1, (B, S, D), dtype=jnp.float32)
        switch_w = jax.random.normal(k2, (E, D), dtype=jnp.float32) * 0.02
        switch_b = jnp.zeros((E,), dtype=jnp.float32)
        expert_w = jax.random.normal(k3, (E, D, D), dtype=jnp.float32) * 0.02
        expert_b = jnp.zeros((E, D), dtype=jnp.float32)
        return {'x': x, 'switch_w': switch_w, 'switch_b': switch_b, 'expert_w': expert_w, 'expert_b': expert_b}
    _L0_ffn_all = _L0_ffn_setup()
    _L0_ffn_in = {k: v for k, v in _L0_ffn_all.items() if k in ('switch_w', 'switch_b', 'expert_w', 'expert_b')}
    del _L0_ffn_all
    return {'x': x, 'L0_tok_W': _L0_tok_in['W'], 'L0_tok_b': _L0_tok_in['b'], 'L0_tok_class_token': _L0_tok_in['class_token'], 'L0_tok_pos_embed': _L0_tok_in['pos_embed'], 'L0_attn_W_proj': _L0_attn_in['W_proj'], 'L0_attn_W_filt': _L0_attn_in['W_filt'], 'L0_ffn_switch_w': _L0_ffn_in['switch_w'], 'L0_ffn_switch_b': _L0_ffn_in['switch_b'], 'L0_ffn_expert_w': _L0_ffn_in['expert_w'], 'L0_ffn_expert_b': _L0_ffn_in['expert_b']}

def reference(x, L0_tok_W, L0_tok_b, L0_tok_class_token, L0_tok_pos_embed, L0_attn_W_proj, L0_attn_W_filt, L0_ffn_switch_w, L0_ffn_switch_b, L0_ffn_expert_w, L0_ffn_expert_b):
    import jax
    import jax.numpy as jnp

    def _L0_tok_ref(X, W, b, class_token, pos_embed):
        import jax, jax.numpy as jnp
        import numpy as np
        N_PATCHES = 8
        PATCH = 28
        C = 3
        IN_D = C * PATCH * PATCH
        HID = 128
        SEQ = N_PATCHES * N_PATCHES + 1

        def _positional_embedding(seq_len, dim):
            i = np.arange(seq_len)[:, None].astype(np.float32)
            j = np.arange(dim)[None, :].astype(np.float32)
            ang = i / np.power(100000.0, j / dim)
            pe = np.where(j % 2 == 0, np.sin(ang), np.cos(ang))
            return jnp.asarray(pe, dtype=jnp.float32)
        B = X.shape[0]
        patches = X.reshape(B, C, N_PATCHES, PATCH, N_PATCHES, PATCH)
        patches = patches.transpose(0, 2, 4, 1, 3, 5).reshape(B, N_PATCHES * N_PATCHES, IN_D)
        tokens = jnp.einsum('bpi,hi->bph', patches, W) + b
        cls = jnp.broadcast_to(class_token[None, :, :], (B, 1, HID))
        tokens = jnp.concatenate([cls, tokens], axis=1)
        return tokens * pos_embed[None, :, :]

    def _L0_attn_ref(X, W_proj, W_filt):
        import jax, jax.numpy as jnp
        import numpy as np
        STAGES = 3
        CAUSAL = True

        def _positional_encoding(T, W):
            half = W // 2
            t = jnp.arange(T, dtype=jnp.float32)
            freqs = 10000.0 ** (-jnp.arange(half, dtype=jnp.float32) / half)
            phi = t[:, None] * freqs[None, :]
            return jnp.concatenate([jnp.sin(phi), jnp.cos(phi)], axis=-1)
        B, T, W = X.shape
        x = jnp.einsum('btw,wvs->btvs', X, W_proj)
        pe = _positional_encoding(T, W)
        f = jnp.einsum('tw,wvs->tvs', pe, W_filt)
        if CAUSAL:
            x = jnp.concatenate([x, jnp.zeros_like(x)], axis=1)
            f = jnp.concatenate([f, jnp.zeros_like(f)], axis=0)
        n = x.shape[1]
        Ff = jnp.fft.rfft(f, axis=0)
        y = x[..., 0]
        for i in range(STAGES):
            Fy = jnp.fft.rfft(y, axis=1)
            y = jnp.fft.irfft(Fy * Ff[None, :, :, i], n=n, axis=1) * x[..., i + 1]
        if CAUSAL:
            y = y[:, :T]
        return y

    def _L0_ffn_ref(x, switch_w, switch_b, expert_w, expert_b):
        import jax, jax.numpy as jnp
        import numpy as np
        CAPACITY_FACTOR = 1.2
        B, S, D = x.shape
        E = switch_w.shape[0]
        N = B * S
        xf = x.reshape(N, D)
        logits = xf @ switch_w.T + switch_b
        probs = jax.nn.softmax(logits, axis=-1)
        route_probs = jnp.max(probs, axis=-1)
        routes = jnp.argmax(probs, axis=-1)
        oh = jax.nn.one_hot(routes, E, dtype=jnp.int32)
        pos = jnp.take_along_axis(jnp.cumsum(oh, axis=0), routes[:, None], axis=1)[:, 0] - 1
        capacity = int(CAPACITY_FACTOR * N / E)
        keep = pos < capacity
        buf = jnp.zeros((E, capacity, D), dtype=xf.dtype).at[routes, pos].set(xf)
        y = jnp.einsum('ecd,efd->ecf', buf, expert_w) + expert_b[:, None, :]
        gathered = y[routes, jnp.minimum(pos, capacity - 1)]
        out = jnp.where(keep[:, None], gathered, xf) * route_probs[:, None]
        return out.reshape(B, S, D)
    h = _L0_tok_ref(x, L0_tok_W, L0_tok_b, L0_tok_class_token, L0_tok_pos_embed)
    h = h + _L0_attn_ref(_layernorm(h, axis=-1), L0_attn_W_proj, L0_attn_W_filt)
    h = h + _L0_ffn_ref(_layernorm(h, axis=-1), L0_ffn_switch_w, L0_ffn_switch_b, L0_ffn_expert_w, L0_ffn_expert_b)
    return h

_drawn_inputs = setup_inputs


def setup_inputs(seed=0):
    import zlib

    import numpy as np

    out = dict(_drawn_inputs(seed))
    spreads = {'L0_ffn_switch_b': (0.0, 0.1), 'L0_ffn_expert_b': (0.0, 0.1)}
    factors = {}
    for name, (base, spread) in spreads.items():
        noise = np.random.default_rng([zlib.crc32(name.encode()), seed]).standard_normal(out[name].shape)
        drawn = base * np.exp(spread * noise) if base else spread * noise
        out[name] = jnp.asarray(drawn.astype(out[name].dtype))
    for name, factor in factors.items():
        out[name] = (out[name] * factor).astype(out[name].dtype)
    return out
```

```python
from contextlib import ExitStack

import numpy as np

import concourse.bass as bass
from concourse import mybir

P = 128
B, C, IMG, PATCH, HID = 64, 3, 224, 28, 128
NP = IMG // PATCH
TOK = NP * NP
SEQ = TOK + 1
ROWS = C * PATCH
GI = 8
GT = GI * TOK
NG = B // GI
XI = NP * IMG
XG = GI * XI
CK = 4
NCK = PATCH // CK
NB = GT // P
NT = B * TOK // P + 1
ST = 3
HV = HID // 2
CQ = 16
NQ = HV // CQ
G8 = 8
NS8 = HV // G8
E = 16
EG = 4
CAP = int(1.2 * (B * SEQ) / E)
EPS = 1e-5
COPIES = 16
RHO = 128

F32 = mybir.dt.float32
F32R = mybir.dt.float32r
BF16 = mybir.dt.bfloat16
I32 = mybir.dt.int32
ALU = mybir.AluOpType
ACT = mybir.ActivationFunctionType
AX = mybir.AxisListType

CONST_COLS = {}


def constants():
    p = np.arange(P)
    parts = [
        ("ident", np.eye(P)),
        ("select", (p[:, None] % HV == np.arange(HV)[None, :])),
        ("before", (p[:, None] < p[None, :])),
        ("image_half", (p[:, None] // TOK == np.arange(2)[None, :])),
        ("even_before", (2 * p[:, None] < p[None, :]) & (p[:, None] < B // 2)),
        ("odd_before", (2 * p[:, None] + 1 < p[None, :]) & (p[:, None] < B // 2)),
        ("priority", np.broadcast_to(E - np.arange(E)[None, :], (P, E))),
        ("classes_before", 2 * np.arange(B // 2)[None, :] + p[:, None] // TOK + 1),
        ("row", p[:, None]),
    ]
    at = 0
    for name, a in parts:
        CONST_COLS[name] = (at, at + a.shape[1])
        at += a.shape[1]
    return np.concatenate([a.astype(np.float32) for _, a in parts], axis=1)


def positions_t():
    half = HID // 2
    freqs = np.power(np.float32(10000.0), -np.arange(half, dtype=np.float32) / np.float32(half)).astype(np.float32)
    phi = np.arange(SEQ, dtype=np.float32)[:, None] * freqs[None, :]
    return np.ascontiguousarray(np.concatenate([np.sin(phi), np.cos(phi)], axis=-1).astype(np.float32).T)


CONSTS = constants()


def build(nc, x, tok_w, tok_b, class_token, pos_embed, w_proj, w_filt, switch_w, switch_b, expert_w, expert_b,
          consts, filt_pos_t, out):
    with ExitStack() as ctx:
        def sb(name, shape, dt=F32):
            return ctx.enter_context(nc.sbuf_tensor(name, shape, dt))

        def sem(name):
            return ctx.enter_context(nc.semaphore(name))

        ps = ctx.enter_context(nc.psum_tensor("ps", [P, 8, 512], F32))

        arena = sb("arena", [P, 2 * XG + E * HID + HID])
        ring_hi = sb("ring_hi", [P, 2, CK * GT], F32R)
        ring_lo = sb("ring_lo", [P, 2, CK * GT], F32R)
        w_hi = sb("w_hi", [P, PATCH * HID + 4 * HID], F32R)
        w_lo = sb("w_lo", [P, PATCH * HID + 4 * HID], F32R)
        h = sb("h", [P, NT * HID])
        con = sb("con", [P, CONSTS.shape[1]])
        pos_t = sb("pos_t", [P, TOK])
        select = sb("select", [P, HV], BF16)
        carry_ab = sb("carry_ab", [P, ST, P], BF16)
        carry_c = sb("carry_c", [P, ST, P], BF16)
        cols = sb("cols", [P, 8])
        stat = sb("stat", [P, 176])

        def c_(name):
            a, b = CONST_COLS[name]
            return con[:, a:b]

        ident = c_("ident")
        b_col, ct_col, p0_col, hc_col, eps_col = (cols[:, i:i + 1] for i in range(5))
        WP0 = PATCH * HID

        x_raw = arena[:, 0:2 * XG].rearrange("p (s n) -> p s n", s=2)
        a0 = XG
        w_raw = arena[:, a0:a0 + ROWS * PATCH]; a0 += ROWS * PATCH
        wp_raw = arena[:, a0:a0 + 4 * HID]; a0 += 4 * HID
        wp_mid = arena[:, a0:a0 + 4 * HID]; a0 += 4 * HID
        wf_raw = arena[:, a0:a0 + ST * HID]; a0 += ST * HID
        wf_two = arena[:, a0:a0 + ST * 2 * HID]; a0 += ST * 2 * HID
        fp_t = arena[:, a0:a0 + SEQ]; a0 += SEQ
        fp0 = arena[:, a0:a0 + P]; a0 += P
        mean_w = arena[:, a0:a0 + P]; a0 += P
        pos_raw = arena[0:TOK, a0:a0 + HID]; a0 += HID
        f_rest = arena[0:TOK, a0:a0 + ST * HID]; a0 += ST * HID
        f_parts = arena[0:TOK, a0:a0 + ST * 3 * HID // 2].bitcast(BF16).rearrange("p (n k c) -> p n k c", k=3, c=CQ)
        a0 += ST * 3 * HID // 2
        f_zero = arena[0:ST * 2 * NQ, a0:a0 + (TOK - 1) * 3 * CQ // 2].bitcast(BF16); a0 += (TOK - 1) * 3 * CQ // 2
        assert a0 <= 2 * XG
        ew_raw = arena[:, 2 * XG:2 * XG + E * HID]
        sw_raw = arena[0:E, 2 * XG + E * HID:2 * XG + E * HID + HID]
        TW = 3 * P * CQ
        toep = arena[:, 0:NQ * TW // 2].bitcast(BF16).rearrange("p (q n) -> p q n", q=NQ)
        XO = 8192
        xs = arena[:, XO:XO + ST * HV * B]
        xs_q = xs.rearrange("p (s v b) -> p s v b", s=ST, v=HV)
        xs_m = xs.rearrange("p (m n) -> p m n", n=G8 * B)
        X3 = XO + ST * HV * B
        x3 = arena[:, X3:X3 + NT * HID].rearrange("p (j v) -> p j v", v=HID)
        PO = X3 + NT * HID
        parts = arena[:, PO:PO + 3 * HV * B // 2].bitcast(BF16).rearrange("p (k g n) -> p k g n", k=3, g=NS8)
        assert PO + 3 * HV * B // 2 <= arena.shape[1]
        a0 = PO
        cls_x = arena[:, a0:a0 + 4 * HID].rearrange("p (s v) -> p s v", s=4); a0 += 4 * HID
        cls_y = arena[:, a0:a0 + 3 * HID].rearrange("p (s v) -> p s v", s=3); a0 += 3 * HID
        cls_t = arena[:, a0:a0 + HID]; a0 += HID
        cls_two = arena[:, a0:a0 + ST * 2 * HID].rearrange("p (i a d v) -> p i a d v", i=ST, a=2, d=2)
        a0 += ST * 2 * HID
        cls_col = arena[:, a0:a0 + 6]; a0 += 6
        cls_f = arena[:, a0:a0 + ST * P].rearrange("p (i n) -> p i n", i=ST); a0 += ST * P
        cls_a = arena[:, a0:a0 + ST * P // 2].bitcast(BF16).rearrange("p (i n) -> p i n", i=ST); a0 += ST * P // 2
        assert a0 <= 2 * XG

        toep_rows = nc.dram_tensor("toeplitz_rows", [ST, 2, NQ, RHO, 3, CQ], BF16, kind="Internal").ap()

        toep_copies = nc.dram_tensor("toeplitz_copies", [ST, 2, NQ, COPIES, RHO, 3, CQ], BF16, kind="Internal").ap()

        s_small = sem("small_loaded"); s_wraw = sem("patch_weights_loaded"); s_exp = sem("expert_weights_loaded")
        s_x = [sem("images_loaded_even"), sem("images_loaded_odd")]
        s_zero = sem("rings_zeroed"); s_prep = sem("prepared_by_vector"); s_prep_a = sem("prepared_by_scalar")
        s_prep_t = sem("prepared_by_tensor")
        s_wt = sem("patch_weights_turned"); s_wt_hi = sem("patch_weights_high"); s_wt_lo = sem("patch_weights_low")
        s_rows = sem("toeplitz_rows_stored"); s_copies = sem("toeplitz_copies_stored")
        s_hi = sem("high_parts_ready"); s_lo = sem("low_parts_ready")
        s_hi_used = sem("high_parts_used"); s_lo_used = sem("low_parts_used")
        s_tok = sem("tokens_ready")
        s_ew_t = sem("expert_weights_turned"); s_ew_hi = sem("expert_weights_high"); s_ew_lo = sem("expert_weights_low")
        s_n_hi = sem("token_high_ready"); s_n_lo = sem("token_low_ready"); s_n_tr = sem("tokens_turned")
        s_n_nat = sem("tokens_stored_by_row"); s_n_var = sem("variances_ready"); s_n_std = sem("deviations_ready")
        s_n_r = sem("scales_ready"); s_n_pr = sem("projected"); s_n_pa = sem("projections_moved_by_scalar")
        s_n_pv = sem("projections_moved_by_vector")
        s_dv = sem("vector_steps")
        s_cls = sem("class_token_vector"); s_cls_t = sem("class_token_tensor"); s_cls_p = sem("class_token_gpsimd")
        s_t = [sem(f"toeplitz_loaded_{q}") for q in range(NQ)]
        s_tz = sem("toeplitz_slots_zeroed")
        s_ya = sem("part_a_ready"); s_yr = sem("rest_ready"); s_yb = sem("part_b_ready"); s_yc = sem("part_c_ready")
        s_cv = sem("convolved"); s_y = sem("stage_output_ready")

        block = ctx.enter_context(nc.Block())

        x_src = x.rearrange("b c (h r) w -> b c r h w", r=PATCH)
        N_SMALL = 8
        V_MEAN, V_FZERO, V_EPS, V_SELECT, V_HC, V_TWO, V_FP0, V_CLS, V_POS, V_MID, V_WPLO, V_FREST, V_FC = (
            1, 2, 3, 4, 5, 11, 12, 13, 14, 15, 16, 17, 18)
        A_WPHI, A_FA, A_FB = 1, 2, 3
        T_POS, T_MEAN, T_F, T_FT, T_F0 = 1, 2, 3, 4, 5
        WT_BANKS = 3
        MEAN_BANK, F_BANK, FT_BANK, F0_BANK, POS_BANK = 3, 4, 5, 6, 7
        BATCHES = NG + 1
        PR_BANKS = [0, 1, 4, 7]
        CV_BANKS = [0, 1, 4, 7]

        def load_images(eng, g, slot):
            for i in range(GI):
                for c in range(C):
                    eng.dma_start(
                        x_raw[c * PATCH:(c + 1) * PATCH, slot, i * XI:(i + 1) * XI].rearrange("p (h w) -> p h w", h=NP),
                        x_src[g * GI + i, c]).then_inc(s_x[slot], 16)

        X_LOADED = GI * C * 16

        def load_toeplitz(eng, i, q):
            for half in range(2):
                for w in range(TOK // COPIES):
                    s0 = half * TOK + w * COPIES
                    src = toep_copies[i, half, q]
                    eng.dma_start(
                        toep[s0:s0 + COPIES, q, half * TOK * 3 * CQ:(half + 1) * TOK * 3 * CQ],
                        bass.AP(src.tensor, offset=src.offset + (TOK - 1 - w * COPIES) * 3 * CQ,
                                ap=[[(RHO - 1) * 3 * CQ, COPIES], [1, TOK * 3 * CQ]])).then_inc(s_t[q], 16)

        T_LOADED = 2 * (TOK // COPIES) * 16

        x_chunk = x_raw.rearrange("p s (t j) -> p s t j", j=PATCH)
        hi_chunk = ring_hi[:].rearrange("p r (j t) -> p r t j", j=CK)
        lo_chunk = ring_lo[:].rearrange("p r (j t) -> p r t j", j=CK)
        h_b = h[:, 0:NG * GT].rearrange("p (n t) -> p n t", t=GT)
        h_cls = h[:, NG * GT:]
        f_view = wf_raw.rearrange("p (v i) -> p i v", i=ST)
        f_sums = ps[0:TOK, F_BANK, 0:ST * HID].rearrange("p (n c) -> p n c", c=CQ)
        f_rest_n = f_rest.rearrange("p (n c) -> p n c", c=CQ)
        w_view = w_raw.rearrange("p (r j) -> p r j", j=PATCH)
        TR_BANKS = [2, 3]
        LAST = NG * NCK

        bs = stat[:, 0:24].rearrange("p (k n) -> p k n", k=NB)
        mv = stat[:, 24:32].rearrange("p (k n) -> p k n", k=NB)
        std, ve, tt = stat[:, 32:36], stat[:, 36:40], stat[:, 40:44]
        rs = stat[:, 44:52].rearrange("p (r k) -> p r k", r=2)
        CLS_X, CLS_Y3, CLS_TWO, CLS_COL, CLS_F = 1, 6, 9, 10, 16

        def pool_parts_c(pool, st, g0, g1):
            for g in range(g0, g1):
                n = st * NS8 + g
                pool.wait_ge(s_yb, n + 1)
                pool.tensor_tensor(parts[:, 2, g], xs_m[:, n], parts[:, 1, g], ALU.subtract).then_inc(s_yc, 1)

        def pool_carry(pool):
            pool.wait_ge(s_cls, CLS_F)
            pool.tensor_copy(cls_a, cls_f).then_inc(s_cls_p, 1)
            pool.wait_ge(s_cls_p, 1)
            pool.tensor_copy(carry_ab[0:HV], cls_a[0:HV]).then_inc(s_cls_p, 1)
            pool.wait_ge(s_cls_p, 2)
            pool.tensor_tensor(cls_f, cls_f, cls_a, ALU.subtract).then_inc(s_cls_p, 1)
            pool.wait_ge(s_cls_p, 3)
            pool.tensor_copy(cls_a, cls_f).then_inc(s_cls_p, 1)
            pool.wait_ge(s_cls_p, 4)
            pool.memset(carry_c[HV:P], 0.0).then_inc(s_cls_p, 1)
            pool.wait_ge(s_cls_p, 5)
            pool.tensor_copy(carry_ab[HV:P], cls_a[HV:P]).then_inc(s_cls_p, 1)
            pool.wait_ge(s_cls_p, 6)
            pool.tensor_tensor(carry_c[0:HV], cls_f[0:HV], cls_a[0:HV], ALU.subtract).then_inc(s_cls_p, 1)
            pool.wait_ge(s_cls_p, 7)

        def tile0(n):
            return 0 if n == 0 else 1 + (n - 1) * NB

        def tiles(n):
            return 1 if n == 0 else NB

        def span(n):
            return slice(tile0(n), tile0(n) + tiles(n))

        def h_tiles(n):
            a = (NT - 1) * HID if n == 0 else (n - 1) * GT
            return h[:, a:a + tiles(n) * HID].rearrange("p (k v) -> p k v", v=HID)

        def wide(col, n):
            return col[:, span(n)].unsqueeze(2).to_broadcast([P, tiles(n), HID])

        SEL = 8
        PAD = 32
        a0 = 0

        def by_tile(width, dt=F32):
            nonlocal a0
            cols_ = NT * width if dt == F32 else NT * width // 2
            v = arena[:, a0:a0 + cols_]
            a0 += cols_
            v = v if dt == F32 else v.bitcast(dt)
            return v.rearrange("p (j e) -> p j e", e=width)

        xf, total, gated = by_tile(HID), by_tile(HID), by_tile(HID)
        picked = arena[:, a0:a0 + SEL * EG * HID].rearrange("p (s i f) -> p s i f", s=SEL, i=EG)
        a0 += SEL * EG * HID
        logit, below, expo, key, chosen, counts, chosen_count = (by_tile(E) for _ in range(7))
        assert a0 <= X3
        eb_raw, eb_rest = gated[:, 0:EG], gated[:, EG:2 * EG]
        a0 = PO
        chosen_bf = by_tile(PAD, BF16)
        chosen_t = arena[:, a0:a0 + (NG + 1) * P // 2].bitcast(BF16).rearrange("p (n m) -> p n m", m=P)
        a0 += (NG + 1) * P // 2
        cls_share = arena[:, a0:a0 + (NT - 1) * E].rearrange("p (j e) -> p j e", e=E); a0 += (NT - 1) * E
        eb = arena[:, a0:a0 + 3 * NB * HID // 2].bitcast(BF16).rearrange("p (k n) -> p k n", k=3)
        a0 += 3 * NB * HID // 2
        ident_bf, before_bf, ones_bf = (arena[:, a0 + k * HV:a0 + (k + 1) * HV].bitcast(BF16) for k in range(3))
        a0 += 3 * HV
        sum_before = arena[:, a0:a0 + (NG + 1) * PAD // 2].bitcast(BF16).rearrange("p (n e) -> p n e", e=PAD)
        a0 += (NG + 1) * PAD // 2
        sum_two = arena[:, a0:a0 + PAD].bitcast(BF16).rearrange("p (k e) -> p k e", k=2); a0 += PAD
        sum_one = arena[:, a0:a0 + PAD // 2].bitcast(BF16); a0 += PAD // 2
        bs2 = arena[:, a0:a0 + NT * 6].rearrange("p (j n) -> p j n", n=6); a0 += NT * 6
        mv2 = arena[:, a0:a0 + NT * 2].rearrange("p (j n) -> p j n", n=2); a0 += NT * 2
        std2, rs2, ve2, tt2, shift2, top, key_top, denom, prob, place, p_keep, p_drop, as_cls = (
            arena[:, a0 + k * NT:a0 + (k + 1) * NT] for k in range(13))
        a0 += 13 * NT
        cls_seen = arena[:, a0:a0 + 2]; a0 += 2
        assert a0 <= arena.shape[1]
        swb = stat[:, 64:64 + E]
        TR4, OHT_BANK, LG_BANK, BI_BANK = 4, 5, 6, 7
        CNT0 = P
        POOL_H = 3

        s_h1 = sem("residual_sums_by_gpsimd"); s_eb = sem("expert_bias_steps"); s_ebl = sem("expert_bias_loaded")
        s_l2 = sem("second_norm_steps"); s_var = sem("second_variances_ready"); s_dev = sem("second_deviations_ready")
        s_norm = sem("second_norm_ready"); s_xf = sem("normed_tokens_ready"); s_tr = sem("normed_tokens_turned")
        s_eh = sem("normed_high_ready"); s_el = sem("normed_low_ready"); s_lg = sem("logits_ready")
        s_rt = sem("routing_steps"); s_bel = sem("logits_below_top_ready"); s_ex = sem("exponentials_ready")
        s_oh = sem("experts_chosen"); s_cnt = sem("counts_ready"); s_gate = sem("gates_ready")
        s_oht = sem("chosen_turned_stored"); s_sum = sem("chosen_summed"); s_bi = sem("biases_ready")
        s_e = sem("expert_groups_computed"); s_p0 = sem("first_group_picked"); s_pk = sem("later_groups_picked")
        s_tot = sem("picked_summed"); s_bt = sem("biases_added"); s_g = sem("dropped_shares_ready"); s_fin = sem("batches_finished")
        s_ps = sem("gpsimd_sum_steps"); s_cs = sem("class_seen"); s_cc = sem("class_counts_ready"); s_out = sem("outputs_stored")
        A_STEPS, G_STEPS = 9, 3

        def experts_sync(sp):
            sp.wait_ge(s_eb, 1)
            for k in range(NB):
                sp.dma_start(eb_raw[PAD * k:PAD * k + E, k], expert_b).then_inc(s_ebl, 16)
            for n in range(1, NG + 1):
                if n == NG:
                    sp.wait_ge(s_fin, NG)
                    sp.dma_start(out[:, 0], h_tiles(0)[0:B, 0]).then_inc(s_out, 16)
                sp.wait_ge(s_fin, n if n < NG else NG + 1)
                for par in range(2):
                    sp.dma_start(
                        out[(n - 1) * GI:n * GI, 1:SEQ].rearrange("(k u) t v -> u t k v", u=2)[par],
                        h_tiles(n)[par * TOK:(par + 1) * TOK]).then_inc(s_out, 16)
            sp.wait_ge(s_out, 16 * (2 * NG + 1))

        def experts_pool(pool):
            pool.wait_ge(s_y, ST * NS8)
            for g in range(NG - POOL_H, NG):
                pool.tensor_tensor(h_b[:, g], h_b[:, g], x3[:, g * NB:(g + 1) * NB].rearrange("p j v -> p (j v)"), ALU.add
                                   ).then_inc(s_h1, 1)
            pool.memset(eb_raw, 0.0).then_inc(s_eb, 1)
            pool.memset(chosen_bf, 0.0).then_inc(s_eb, 1)
            pool.memset(ones_bf, 1.0).then_inc(s_eb, 1)
            pool.tensor_copy(before_bf, c_("before")).then_inc(s_eb, 1)
            pool.tensor_copy(ident_bf, ident).then_inc(s_eb, 1)
            flat = eb_raw.rearrange("p k f -> p (k f)")
            rest_ = eb_rest.rearrange("p k f -> p (k f)")
            pool.wait_ge(s_ebl, 16 * NB)
            pool.tensor_copy(eb[:, 0], flat).then_inc(s_eb, 1)
            pool.wait_ge(s_eb, 6)
            pool.tensor_tensor(rest_, flat, eb[:, 0], ALU.subtract).then_inc(s_eb, 1)
            pool.wait_ge(s_eb, 7)
            pool.tensor_copy(eb[:, 1], rest_).then_inc(s_eb, 1)
            pool.wait_ge(s_eb, 8)
            pool.tensor_tensor(eb[:, 2], rest_, eb[:, 1], ALU.subtract).then_inc(s_eb, 1)
            pool.wait_ge(s_eb, 9)

            def summed(n):
                pool.wait_ge(s_oh, n + 1)
                o = chosen_bf[:, span(n)]
                b = 3 * (n - 1)
                if n > 1:
                    pool.wait_ge(s_sum, b)
                pool.tensor_tensor(sum_two, o[:, 0:2], o[:, 2:4], ALU.add).then_inc(s_sum, 1)
                pool.wait_ge(s_sum, b + 1)
                pool.tensor_tensor(sum_one, sum_two[:, 0], sum_two[:, 1], ALU.add).then_inc(s_sum, 1)
                pool.wait_ge(s_sum, b + 2)
                if n == 1:
                    pool.tensor_copy(sum_before[:, n + 1], sum_one).then_inc(s_sum, 1)
                else:
                    pool.tensor_tensor(sum_before[:, n + 1], sum_before[:, n], sum_one, ALU.add).then_inc(s_sum, 1)

            ps_steps = 0

            def dropped(n):
                nonlocal ps_steps
                pool.wait_ge(s_gate, n if n else NG + 1)
                pool.tensor_tensor(gated[:, span(n)], xf[:, span(n)], wide(p_drop, n), ALU.mult).then_inc(s_ps, 1)
                ps_steps += 1
                pool.wait_ge(s_ps, ps_steps)
                pool.tensor_tensor(gated[:, span(n)], gated[:, span(n)], h_tiles(n), ALU.add).then_inc(s_g, 1)

            def sum_picked(t):
                nonlocal ps_steps
                s = picked[:, t % SEL]
                pool.wait_ge(s_pk, (EG - 1) * (t + 1))
                pool.tensor_tensor(s[:, 0:2], s[:, 0:2], s[:, 2:4], ALU.add).then_inc(s_ps, 1)
                ps_steps += 1
                pool.wait_ge(s_ps, ps_steps)
                pool.tensor_tensor(total[:, t], s[:, 0], s[:, 1], ALU.add).then_inc(s_tot, 1)

            def finish(n, done):
                nonlocal ps_steps
                pool.wait_ge(s_bt, n + 1)
                pool.wait_ge(s_g, done)
                pool.tensor_tensor(total[:, span(n)], total[:, span(n)], wide(p_keep, n), ALU.mult).then_inc(s_ps, 1)
                ps_steps += 1
                pool.wait_ge(s_ps, ps_steps)
                pool.tensor_tensor(h_tiles(n), total[:, span(n)], gated[:, span(n)], ALU.add).then_inc(s_fin, 1)

            sum_picked(0)
            for n in range(1, NG + 1):
                dropped(n)
                for k in range(NB):
                    sum_picked(tile0(n) + k)
                    if k == 0 and n < NG:
                        summed(n)
                    if k == 1 and n > 1:
                        finish(n - 1, n - 1)
                    if k == 2 and n == NG:
                        dropped(0)
                        finish(0, NG + 1)
            finish(NG, NG)

        def experts_scalar(act):
            act.wait_ge(s_var, 1)
            act.activation(std2, mv2[:, :, 1], ACT.Sqrt, bias=eps_col).then_inc(s_dev, 1)

            def normed(n):
                for k in range(tiles(n)):
                    t = tile0(n) + k
                    ins = act.activation(xf[:, t], h_tiles(n)[:, k], ACT.Identity, bias=shift2[:, t:t + 1], scale=rs2[:, t:t + 1])
                ins.then_inc(s_xf, 1)

            def high(n):
                act.wait_ge(s_tr, n + 1)
                if n >= 2:
                    act.wait_ge(s_e, EG * tile0(n - 1))
                w = tiles(n) * P
                act.activation(ring_hi[:, n % 2, 0:w], ps[:, TR4, 0:w], ACT.Copy).then_inc(s_eh, 1)

            def exponentials(n):
                act.wait_ge(s_bel, n + 1)
                act.activation(expo[:, span(n)], below[:, span(n)], ACT.Exp).then_inc(s_ex, 1)

            def store_turned(n):
                act.wait_ge(s_cnt, n + 1)
                w = tiles(n) * PAD
                act.activation(chosen_t[0:w, n], turned_bf[0:w], ACT.Copy).then_inc(s_oht, 1)

            def first_group(t):
                if t >= SEL:
                    act.wait_ge(s_tot, t - SEL + 1)
                act.wait_ge(s_e, EG * t + 1)
                for e in range(EG):
                    ins = act.activation(picked[:, t % SEL, e], ps[:, 0, e * HID:(e + 1) * HID], ACT.Copy,
                                         scale=chosen[:, t, e:e + 1])
                ins.then_inc(s_p0, 1)

            act.wait_ge(s_norm, 1)
            act.wait_ge(s_h1, POOL_H)
            normed(0)
            normed(1)
            high(0)
            exponentials(0)
            high(1)
            normed(2)
            store_turned(0)
            exponentials(1)
            act.wait_ge(s_oh, 1)
            first_group(0)
            store_turned(1)
            for n in range(1, NG + 1):
                act.wait_ge(s_oh, n + 1)
                for k in range(NB):
                    first_group(tile0(n) + k)
                    if n < NG:
                        if k == 0:
                            high(n + 1)
                        if k == 1 and n + 2 <= NG:
                            normed(n + 2)
                        if k == 1:
                            exponentials(n + 1)
                        if k == 2:
                            store_turned(n + 1)

        def experts_vector(dve):
            dve.wait_ge(s_y, ST * NS8)
            dve.tensor_tensor(h_cls, h_cls, x3[:, NT - 1], ALU.add).then_inc(s_l2, 1)
            for g in range(NG - POOL_H):
                dve.tensor_tensor(h_b[:, g], h_b[:, g], x3[:, g * NB:(g + 1) * NB].rearrange("p j v -> p (j v)"), ALU.add
                                  ).then_inc(s_l2, 1)
            for n in range(NG + 1):
                if n == 0:
                    dve.wait_ge(s_l2, NG - POOL_H + 1)
                if n > NG - POOL_H:
                    dve.wait_ge(s_h1, n - (NG - POOL_H))
                for k in range(tiles(n)):
                    dve.bn_stats(bs2[:, tile0(n) + k], h_tiles(n)[:, k]).then_inc(s_l2, 1)
            L = NG - POOL_H + 1 + NT
            dve.wait_ge(s_l2, L)
            for t in range(NT):
                ins = dve.bn_aggr(mv2[:, t], bs2[:, t])
            ins.then_inc(s_var, 1)
            dve.wait_ge(s_var, 1)
            dve.tensor_scalar(ve2, mv2[:, :, 1], EPS, None, ALU.add).then_inc(s_l2, 1)
            dve.wait_ge(s_dev, 1)
            dve.reciprocal(rs2, std2).then_inc(s_l2, 1)
            dve.wait_ge(s_l2, L + 2)
            dve.tensor_tensor(tt2, rs2, rs2, ALU.mult).then_inc(s_l2, 1)
            dve.wait_ge(s_l2, L + 3)
            dve.tensor_tensor(tt2, tt2, ve2, ALU.mult).then_inc(s_l2, 1)
            dve.wait_ge(s_l2, L + 4)
            dve.tensor_scalar(tt2, tt2, -0.5, 1.5, ALU.mult, ALU.add).then_inc(s_l2, 1)
            dve.wait_ge(s_l2, L + 5)
            dve.tensor_tensor(rs2, rs2, tt2, ALU.mult).then_inc(s_l2, 1)
            dve.wait_ge(s_l2, L + 6)
            dve.scalar_tensor_tensor(out=shift2, in0=mv2[:, :, 0], scalar=-1.0, in1=rs2, op0=ALU.mult, op1=ALU.mult
                                     ).then_inc(s_norm, 1)

            def low_parts(n):
                w = tiles(n) * P
                dve.wait_ge(s_eh, n + 1)
                dve.tensor_tensor(ring_lo[:, n % 2, 0:w], ps[:, TR4, 0:w], ring_hi[:, n % 2, 0:w].bitcast(F32), ALU.subtract
                                  ).then_inc(s_el, 1)

            steps = 0

            def choose(n):
                nonlocal steps
                nt, s = tiles(n), span(n)
                by = lambda col: col[:, s].unsqueeze(2).to_broadcast([P, nt, E])
                dve.wait_ge(s_lg, n + 1)
                dve.tensor_tensor(logit[:, s], ps[:, LG_BANK, 0:nt * E].rearrange("p (k e) -> p k e", e=E),
                                  swb.unsqueeze(1).to_broadcast([P, nt, E]), ALU.add).then_inc(s_rt, 1)
                dve.wait_ge(s_rt, steps + 1)
                dve.tensor_reduce(top[:, s], logit[:, s], AX.X, ALU.max).then_inc(s_rt, 1)
                dve.wait_ge(s_rt, steps + 2)
                dve.tensor_tensor(below[:, s], logit[:, s], by(top), ALU.subtract).then_inc(s_bel, 1)
                dve.wait_ge(s_bel, n + 1)
                dve.scalar_tensor_tensor(out=key[:, s], in0=below[:, s], scalar=0.0,
                                         in1=c_("priority").unsqueeze(1).to_broadcast([P, nt, E]),
                                         op0=ALU.is_ge, op1=ALU.mult).then_inc(s_rt, 1)
                dve.wait_ge(s_rt, steps + 3)
                dve.tensor_reduce(key_top[:, s], key[:, s], AX.X, ALU.max).then_inc(s_rt, 1)
                dve.wait_ge(s_rt, steps + 4)
                dve.tensor_tensor(chosen[:, s], key[:, s], by(key_top), ALU.is_equal).then_inc(s_rt, 1)
                if n == 0:
                    dve.wait_ge(s_eb, 9)
                dve.tensor_tensor(chosen_bf[:, s, 0:E], key[:, s], by(key_top), ALU.is_equal).then_inc(s_oh, 1)
                dve.wait_ge(s_rt, steps + 5)
                if n == 0:
                    dve.tensor_tensor(cls_share, c_("classes_before").unsqueeze(2).to_broadcast([P, NT - 1, E]),
                                      chosen[:, 0:1].to_broadcast([P, NT - 1, E]), ALU.mult).then_inc(s_rt, 1)
                else:
                    dve.tensor_tensor(chosen_count[:, s], chosen[:, s], chosen[:, 0:1].to_broadcast([P, nt, E]), ALU.mult
                                      ).then_inc(s_rt, 1)
                dve.wait_ge(s_ex, n + 1)
                dve.tensor_reduce(denom[:, s], expo[:, s], AX.X, ALU.add).then_inc(s_rt, 1)
                dve.wait_ge(s_rt, steps + 7)
                if n == 0:
                    dve.reciprocal(prob[:, s], denom[:, s]).then_inc(s_rt, 2)
                else:
                    dve.reciprocal(prob[:, s], denom[:, s]).then_inc(s_rt, 1)
                    dve.tensor_reduce(as_cls[:, s], chosen_count[:, s], AX.X, ALU.add).then_inc(s_rt, 1)
                dve.wait_ge(s_rt, steps + A_STEPS)
                steps += A_STEPS

            def gates(n):
                nonlocal steps
                s = span(n)
                dve.wait_ge(s_cnt, n + 1)
                dve.tensor_tensor(
                    counts[:, s], ps[:, LG_BANK, CNT0:CNT0 + NB * PAD].rearrange("p (k e) -> p k e", e=PAD)[:, :, 0:E],
                    cls_share[:, (n - 1) * NB:n * NB], ALU.add).then_inc(s_rt, 1)
                dve.wait_ge(s_rt, steps + 1)
                dve.tensor_tensor(counts[:, s], counts[:, s], chosen[:, s], ALU.mult).then_inc(s_rt, 1)
                dve.wait_ge(s_rt, steps + 2)
                dve.tensor_reduce(place[:, s], counts[:, s], AX.X, ALU.add).then_inc(s_rt, 1)
                dve.wait_ge(s_rt, steps + 3)
                steps += 3
                split(s)

            def split(s):
                nonlocal steps
                dve.scalar_tensor_tensor(out=p_keep[:, s], in0=place[:, s], scalar=float(CAP), in1=prob[:, s],
                                         op0=ALU.is_lt, op1=ALU.mult).then_inc(s_rt, 1)
                dve.wait_ge(s_rt, steps + 1)
                steps += 1
                dve.tensor_tensor(p_drop[:, s], prob[:, s], p_keep[:, s], ALU.subtract).then_inc(s_gate, 1)

            def later_groups(t):
                for g in range(1, EG):
                    dve.wait_ge(s_e, EG * t + g + 1)
                    if g == 1:
                        dve.wait_ge(s_p0, t + 1)
                    else:
                        dve.wait_ge(s_pk, (EG - 1) * t + g - 1)
                    dve.copy_predicated(
                        picked[:, t % SEL], chosen[:, t, g * EG:(g + 1) * EG].bitcast(I32).unsqueeze(2).to_broadcast([P, EG, HID]),
                        ps[:, g, :].rearrange("p (e f) -> p e f", e=EG)).then_inc(s_pk, 1)

            def add_bias(n):
                dve.wait_ge(s_bi, n + 1)
                dve.wait_ge(s_tot, tile0(n) + tiles(n))
                dve.tensor_tensor(total[:, span(n)], total[:, span(n)],
                                  ps[:, BI_BANK, 0:tiles(n) * HID].rearrange("p (k f) -> p k f", f=HID), ALU.add
                                  ).then_inc(s_bt, 1)

            def class_gates():
                nonlocal steps
                dve.wait_ge(s_cs, 1)
                dve.tensor_copy(cls_seen[0:NT - 1], ps[0:NT - 1, OHT_BANK, P:P + 2]).then_inc(s_rt, 1)
                dve.wait_ge(s_cc, 1)
                dve.tensor_tensor(place[:, 0:1], ps[:, OHT_BANK, P + 4:P + 5], c_("row"), ALU.add).then_inc(s_rt, 1)
                dve.wait_ge(s_rt, steps + 2)
                steps += 2
                split(slice(0, 1))

            low_parts(0)
            choose(0)
            low_parts(1)
            choose(1)
            later_groups(0)
            gates(1)
            for n in range(1, NG + 1):
                for k in range(NB):
                    later_groups(tile0(n) + k)
                    if n < NG:
                        if k == 0:
                            low_parts(n + 1)
                            add_bias(n - 1)
                        if k == 1:
                            choose(n + 1)
                        if k == 3:
                            gates(n + 1)
                    else:
                        if k == 0:
                            add_bias(n - 1)
                            class_gates()
            add_bias(NG)

        def experts_tensor(pe):
            def turn(n):
                pe.wait_ge(s_xf, n + 1)
                if n:
                    pe.wait_ge(s_eh, n)
                    pe.wait_ge(s_el, n)
                for k in range(tiles(n)):
                    ins = pe.transpose(ps[:, TR4, k * P:(k + 1) * P], xf[:, tile0(n) + k], ident)
                ins.then_inc(s_tr, 1)

            def logits(n):
                pe.wait_ge(s_eh, n + 1)
                pe.wait_ge(s_el, n + 1)
                if n >= 2:
                    pe.wait_ge(s_gate, n - 1)
                if n == 1:
                    pe.wait_ge(s_bel, 1)
                a = E * HID
                for k in range(tiles(n)):
                    x_h, x_l = (q[:, n % 2, k * P:(k + 1) * P] for q in (ring_hi, ring_lo))
                    o = ps[:, LG_BANK, k * E:(k + 1) * E]
                    pe.matmul(o, x_h, w_hi[:, a:a + E], start=True, stop=False)
                    pe.matmul(o, x_h, w_lo[:, a:a + E], start=False, stop=False)
                    ins = pe.matmul(o, x_l, w_hi[:, a:a + E], start=False, stop=True)
                ins.then_inc(s_lg, 1)

            turned_in = ps[:, OHT_BANK, 0:HV].bitcast(BF16)

            def count(n):
                pe.wait_ge(s_oh, n + 1)
                if n:
                    pe.wait_ge(s_oht, n)
                w = tiles(n) * PAD
                ins = pe.transpose(turned_in[0:w], chosen_bf[:, span(n)].rearrange("p k e -> p (k e)"), ident_bf)
                if n:
                    cnt = lambda k: ps[:, LG_BANK, CNT0 + k * PAD:CNT0 + NB * PAD]
                    pe.matmul(cnt(0), before_bf, chosen_bf[:, span(n)].rearrange("p k e -> p (k e)"), start=True, stop=False,
                              skip_group_check=True)
                    if n > 1:
                        pe.wait_ge(s_sum, 3 * (n - 1))
                        pe.matmul(cnt(0).rearrange("p (k e) -> p k e", e=PAD), ones_bf,
                                  sum_before[:, n:n + 1].to_broadcast([P, NB, PAD]), start=False, stop=False,
                                  skip_group_check=True)
                    for k in range(NB - 1):
                        ins = pe.matmul(cnt(k + 1).rearrange("p (k e) -> p k e", e=PAD), ones_bf,
                                        chosen_bf[:, tile0(n) + k:tile0(n) + k + 1].to_broadcast([P, NB - 1 - k, PAD]),
                                        start=False, stop=(k == NB - 2), skip_group_check=True)
                ins.then_inc(s_cnt, 1)

            def bias(n):
                pe.wait_ge(s_oht, n + 1)
                if n:
                    pe.wait_ge(s_bt, n)
                w, f = tiles(n) * PAD, tiles(n) * HID
                for k in range(3):
                    ins = pe.matmul(ps[:, BI_BANK, 0:f], chosen_t[0:w, n], eb[0:w, k, 0:f], start=(k == 0), stop=(k == 2))
                ins.then_inc(s_bi, 1)

            def experts(n, k):
                t = tile0(n) + k
                x_h, x_l = (q[:, n % 2, k * P:(k + 1) * P] for q in (ring_hi, ring_lo))
                for g in range(EG):
                    if t:
                        if g == 0:
                            pe.wait_ge(s_p0, t)
                        else:
                            pe.wait_ge(s_pk, (EG - 1) * (t - 1) + g)
                    o, a = ps[:, g, :], g * EG * HID
                    pe.matmul(o, x_h, w_hi[:, a:a + EG * HID], start=True, stop=False)
                    pe.matmul(o, x_h, w_lo[:, a:a + EG * HID], start=False, stop=False)
                    pe.matmul(o, x_l, w_hi[:, a:a + EG * HID], start=False, stop=True).then_inc(s_e, 1)

            def class_counts():
                pe.wait_ge(s_rt, CLASS_STEPS)
                pe.wait_ge(s_oht, NG + 1)
                pe.matmul(ps[0:NT - 1, OHT_BANK, P:P + 2], as_cls[:, 1:NT], c_("image_half"), start=True, stop=True
                          ).then_inc(s_cs, 1)
                pe.wait_ge(s_rt, CLASS_STEPS + 1)
                for k, name in enumerate(("even_before", "odd_before")):
                    ins = pe.matmul(ps[:, OHT_BANK, P + 4:P + 5], c_(name)[0:NT - 1], cls_seen[0:NT - 1, k:k + 1],
                                    start=(k == 0), stop=(k == 1))
                ins.then_inc(s_cc, 1)

            pe.wait_ge(s_y, ST * NS8)
            turn(0)
            logits(0)
            turn(1)
            pe.wait_ge(s_eb, 9)
            count(0)
            logits(1)
            experts(0, 0)
            count(1)
            bias(0)
            for n in range(1, NG + 1):
                for k in range(NB):
                    experts(n, k)
                    if k == 0 and n < NG:
                        turn(n + 1)
                    if k == 1:
                        if n < NG:
                            logits(n + 1)
                        bias(n)
                    if k == 2 and n < NG:
                        count(n + 1)
                    if k == 0 and n == NG:
                        class_counts()

        turned_bf = ps[:, OHT_BANK, 0:HV].bitcast(BF16)
        CLASS_STEPS = (NG + 1) * A_STEPS + NG * 4

        @block.sync
        def _(sp):
            sp.dma_start(w_raw, tok_w).then_inc(s_wraw, 16)
            load_images(sp, 0, 0)
            sp.wait_ge(s_prep, V_FC)
            sp.wait_ge(s_prep_a, A_FB)
            sp.wait_ge(s_prep_t, T_F0)
            sp.wait_ge(s_wt_lo, NCK)
            sp.wait_ge(s_rows, 16 * (1 + ST))
            used = (RHO - 1) * 3 * CQ
            sp.dma_start(
                toep_copies.rearrange("i a q z r k c -> (i a q) z (r k c)")[:, :, 0:used],
                toep_rows.rearrange("i a q r k c -> (i a q) (r k c)")[:, 0:used].unsqueeze(1).to_broadcast(
                    [ST * 2 * NQ, COPIES, used])).then_inc(s_copies, 16)
            load_images(sp, 1, 1)
            with sp.Fori(1, NG // 2) as i:
                for u in range(2):
                    sp.wait_ge(s_lo, (i * 2 + u - 1) * NCK)
                    load_images(sp, i * 2 + u, u)
            sp.wait_ge(s_copies, 16)
            for q in range(NQ):
                sp.wait_ge(s_tz, 2 * q + 2)
                load_toeplitz(sp, 0, q)
            for i in range(1, ST):
                for q in range(NQ):
                    sp.wait_ge(s_cv, NS8 * (i - 1) + 2 * q + 2)
                    load_toeplitz(sp, i, q)
            experts_sync(sp)

        @block.gpsimd
        def _(pool):
            for ring in (ring_hi, ring_lo):
                for r in range(2):
                    pool.memset(ring[HV:P, r].bitcast(F32), 0.0).then_inc(s_zero, 1)
            def zero_slot(q):
                for half in range(2):
                    other = 1 - half
                    pool.memset(toep[half * TOK:(half + 1) * TOK, q, other * TOK * 3 * CQ:(other + 1) * TOK * 3 * CQ], 0.0
                                ).then_inc(s_tz, 1)

            pool.wait_ge(s_lo, LAST)
            zero_slot(0)
            zero_slot(1)
            pool.wait_ge(s_tz, 4)
            pool_carry(pool)
            pool_parts_c(pool, 0, 0, 2)
            pool.wait_ge(s_yc, 2)
            zero_slot(2)
            pool.wait_ge(s_tz, 6)
            pool_parts_c(pool, 0, 2, NS8)
            pool.wait_ge(s_yc, NS8)
            zero_slot(3)
            pool.wait_ge(s_tz, 8)
            for st in range(1, ST):
                pool_parts_c(pool, st, 0, NS8)
            experts_pool(pool)

        @block.scalar
        def _(act):
            for dst, src in ((con[:], consts), (fp_t, filt_pos_t), (wp_raw, w_proj.rearrange("w v s -> w (v s)")),
                             (wf_raw, w_filt.rearrange("w v s -> w (v s)")), (pos_raw, pos_embed[1:SEQ]),
                             (b_col, tok_b.rearrange("(p o) -> p o", o=1)),
                             (ct_col, class_token.rearrange("o p -> p o")),
                             (p0_col, pos_embed[0:1].rearrange("o p -> p o"))):
                act.dma_start(dst, src).then_inc(s_small, 16)
            act.dma_start(ew_raw.rearrange("p (e d) -> p e d", e=E), expert_w.rearrange("e f d -> f e d")).then_inc(s_exp, 16)
            act.dma_start(sw_raw, switch_w).then_inc(s_exp, 16)
            act.dma_start(stat[:, 64:64 + E], bass.AP(switch_b.tensor, offset=switch_b.offset, ap=[[0, P], [1, E]])
                          ).then_inc(s_exp, 16)

            act.wait_ge(s_prep, V_MID)
            act.activation(w_hi[:, WP0:], wp_mid, ACT.Copy).then_inc(s_prep_a, 1)
            act.wait_ge(s_prep_t, T_F)
            act.activation(f_parts[:, :, 0], f_sums, ACT.Copy).then_inc(s_prep_a, 1)
            act.wait_ge(s_prep, V_FREST)
            act.activation(f_parts[:, :, 1], f_rest_n, ACT.Copy).then_inc(s_prep_a, 1)
            act.wait_ge(s_prep, V_FC)
            with nc.allow_non_contiguous_dma(reason="padded filter rows of 16 channels"):
                act.dma_start(toep_rows.rearrange("i a q r k c -> (i a q) (r k c)")[:, 0:(TOK - 1) * 3 * CQ], f_zero
                              ).then_inc(s_rows, 16)
                act.wait_ge(s_prep_a, A_FB)
                for i in range(ST):
                    act.dma_start(
                        toep_rows[i, :, :, TOK - 1:2 * TOK - 1].rearrange("a q r k c -> r (a q) (k c)"),
                        f_parts[:, i * 2 * NQ:(i + 1) * 2 * NQ].rearrange("p n k c -> p n (k c)")).then_inc(s_rows, 16)

            act.wait_ge(s_zero, 6)
            for b in range(NCK):
                act.wait_ge(s_wt, b + 1)
                act.activation(w_hi[0:ROWS, b * GT:(b + 1) * GT], ps[0:ROWS, b % WT_BANKS, :], ACT.Copy
                               ).then_inc(s_wt_hi, 1)

            for u in range(2):
                for k in range(NCK):
                    n = u * NCK + k
                    if k == 0:
                        act.wait_ge(s_x[u], X_LOADED)
                    if n >= 2:
                        act.wait_ge(s_hi_used, n - 1)
                        act.wait_ge(s_lo, n - 1)
                    act.activation(hi_chunk[0:ROWS, n % 2], x_chunk[0:ROWS, u, :, k * CK:(k + 1) * CK], ACT.Copy
                                   ).then_inc(s_hi, 1)
            with act.Fori(1, NG // 2) as i:
                for u in range(2):
                    for k in range(NCK):
                        n0 = i * (2 * NCK) + (u * NCK + k)
                        r = (u * NCK + k) % 2
                        if k == 0:
                            act.wait_ge(s_x[u], i * X_LOADED + X_LOADED)
                        act.wait_ge(s_hi_used, n0 - 1)
                        act.wait_ge(s_lo, n0 - 1)
                        act.activation(hi_chunk[0:ROWS, r], x_chunk[0:ROWS, u, :, k * CK:(k + 1) * CK], ACT.Copy
                                       ).then_inc(s_hi, 1)

            act.wait_ge(s_hi_used, LAST)
            act.wait_ge(s_lo_used, LAST)
            for k in range(5):
                act.wait_ge(s_ew_t, k + 1)
                if k < 4:
                    act.activation(w_hi[:, k * GT:(k + 1) * GT], ps[:, PR_BANKS[k], :], ACT.Copy).then_inc(s_ew_hi, 1)
                else:
                    act.activation(w_hi[:, E * HID:E * HID + E], ps[:, TR_BANKS[1], 0:E], ACT.Copy).then_inc(s_ew_hi, 1)

            def batch(n, r, src, width, first):
                if not first:
                    act.wait_ge(s_n_pr, n * NB - 7)
                act.activation(ring_hi[:, r, 0:width], src, ACT.Copy).then_inc(s_n_hi, 1)
                act.wait_ge(s_n_tr, n + 1)
                act.wait_ge(s_n_lo, n + 1)
                act.activation(src, ps[:, TR_BANKS[r], 0:width], ACT.Copy).then_inc(s_n_nat, 1)
                act.wait_ge(s_n_var, n + 1)
                nt = width // P
                act.activation(std[:, 0:nt], mv[:, 0:nt, 1], ACT.Sqrt, bias=eps_col).then_inc(s_n_std, 1)

            def moves(m, r):
                act.wait_ge(s_n_r, m + 2)
                for k in range(NB):
                    act.wait_ge(s_n_pr, m * NB + (k + 2))
                    src = ps[:, PR_BANKS[k], :].rearrange("p (s v) -> p s v", s=4)
                    sc = rs[:, r, k:k + 1]
                    for half in range(2):
                        act.activation(xs_q[half * HV:(half + 1) * HV, :, :, 2 * (m * NB + k):2 * (m * NB + k) + 1],
                                       src[0:TOK, 0:ST, half * HV:(half + 1) * HV].unsqueeze(3), ACT.Copy, scale=sc[0:TOK])
                    act.activation(x3[0:TOK, m * NB + k:m * NB + k + 1, :], src[0:TOK, ST:ST + 1, :], ACT.Copy,
                                   scale=sc[0:TOK]).then_inc(s_n_pa, 1)

            act.wait_ge(s_prep, V_CLS)
            batch(0, 0, h_cls, P, True)
            act.wait_ge(s_tok, NG)
            for m in range(NG):
                batch(m + 1, (m + 1) % 2, h_b[:, m], GT, m == 0)
                moves(m, (m + 1) % 2)

            act.wait_ge(s_n_pv, NT)
            act.wait_ge(s_n_pa, NT - 1)
            for st in range(ST):
                for g in range(NS8 + 1):
                    n = st * NS8 + g
                    if g < NS8:
                        if st:
                            act.wait_ge(s_y, n - NS8 + 1)
                        elif g == 0:
                            act.wait_ge(s_cls_p, 7)
                        act.activation(parts[:, 0, g], xs_m[:, n], ACT.Copy).then_inc(s_ya, 1)
                    if g:
                        act.wait_ge(s_yr, n)
                        act.activation(parts[:, 1, g - 1], xs_m[:, n - 1], ACT.Copy).then_inc(s_yb, 1)
            experts_scalar(act)

        @block.vector
        def _(dve):
            def prep(ins):
                ins.then_inc(s_prep, 1)

            prep(dve.memset(mean_w, 1.0 / HID))
            prep(dve.memset(f_zero, 0.0))
            prep(dve.memset(eps_col, EPS))
            for w in (w_hi, w_lo):
                dve.memset(w[HV:P, 0:WP0].bitcast(F32), 0.0).then_inc(s_zero, 1)
            dve.wait_ge(s_small, 16 * N_SMALL)
            prep(dve.tensor_copy(select[:], c_("select")))
            prep(dve.tensor_tensor(hc_col, ct_col, p0_col, ALU.mult))
            two = wf_two.rearrange("p (i a d v) -> p i a d v", i=ST, a=2, d=2)
            for i in range(ST):
                for d in range(2):
                    prep(dve.tensor_copy(two[:, i, :, d], f_view[:, i].rearrange("p (a v) -> p a v", a=2)))
            prep(dve.tensor_copy(fp0, fp_t[:, 0:1].to_broadcast([P, P])))
            dve.wait_ge(s_prep, V_HC)
            prep(dve.tensor_copy(h_cls, hc_col.to_broadcast([P, P])))
            dve.wait_ge(s_prep_t, T_POS)
            prep(dve.tensor_copy(pos_t[:], ps[:, POS_BANK, 0:TOK]))
            dve.wait_ge(s_prep_t, T_MEAN)
            prep(dve.tensor_tensor(
                wp_mid.rearrange("p (s v) -> p s v", s=4), wp_raw.rearrange("p (v s) -> p s v", s=4),
                ps[:, MEAN_BANK, :].rearrange("p (v s) -> p s v", s=4), ALU.subtract))
            dve.wait_ge(s_prep, V_MID)
            dve.wait_ge(s_prep_a, A_WPHI)
            prep(dve.tensor_tensor(w_lo[:, WP0:], wp_mid, w_hi[:, WP0:].bitcast(F32), ALU.subtract))
            dve.wait_ge(s_prep_a, A_FA)
            prep(dve.tensor_tensor(f_rest_n, f_sums, f_parts[:, :, 0], ALU.subtract))
            dve.wait_ge(s_prep_a, A_FB)
            dve.wait_ge(s_prep, V_FREST)
            prep(dve.tensor_tensor(f_parts[:, :, 2], f_rest_n, f_parts[:, :, 1], ALU.subtract))
            dve.wait_ge(s_zero, 6)
            for b in range(NCK):
                dve.wait_ge(s_wt_hi, b + 1)
                dve.tensor_tensor(w_lo[0:ROWS, b * GT:(b + 1) * GT], ps[0:ROWS, b % WT_BANKS, :],
                                  w_hi[0:ROWS, b * GT:(b + 1) * GT].bitcast(F32), ALU.subtract).then_inc(s_wt_lo, 1)

            def low(u, k):
                r = (u * NCK + k) % 2
                dve.tensor_tensor(lo_chunk[0:ROWS, r], x_chunk[0:ROWS, u, :, k * CK:(k + 1) * CK],
                                  hi_chunk[0:ROWS, r].bitcast(F32), ALU.subtract).then_inc(s_lo, 1)

            def tokens(g, bank):
                dve.wait_ge(s_lo_used, g * NCK + NCK)
                dve.scalar_tensor_tensor(
                    out=h_b[:, g].rearrange("p (b t) -> p b t", b=GI), in0=ps[:, bank, :].rearrange("p (b t) -> p b t", b=GI),
                    scalar=b_col, in1=pos_t[:].unsqueeze(1).to_broadcast([P, GI, TOK]),
                    op0=ALU.add, op1=ALU.mult).then_inc(s_tok, 1)

            dve.wait_ge(s_prep, V_POS)
            for u in range(2):
                for k in range(NCK):
                    n = u * NCK + k
                    dve.wait_ge(s_hi, n + 1)
                    if n >= 2:
                        dve.wait_ge(s_lo_used, n - 1)
                    low(u, k)
                    if u and k == 1:
                        tokens(0, 0)
            with dve.Fori(1, NG // 2) as i:
                for u in range(2):
                    for k in range(NCK):
                        n = i * (2 * NCK) + (u * NCK + k)
                        dve.wait_ge(s_hi, n + 1)
                        dve.wait_ge(s_lo_used, n - 1)
                        low(u, k)
                        if k == 1:
                            tokens(i * 2 + (u - 1), 1 - u)
            tokens(NG - 1, 1)

            for k in range(5):
                dve.wait_ge(s_ew_hi, k + 1)
                a, w, bank = (k * GT, GT, PR_BANKS[k]) if k < 4 else (E * HID, E, TR_BANKS[1])
                dve.tensor_tensor(w_lo[:, a:a + w], ps[:, bank, 0:w], w_hi[:, a:a + w].bitcast(F32), ALU.subtract
                                  ).then_inc(s_ew_lo, 1)

            def batch(n, r, src, width, steps):
                nt = width // P
                dve.wait_ge(s_n_hi, n + 1)
                dve.tensor_tensor(ring_lo[:, r, 0:width], src, ring_hi[:, r, 0:width].bitcast(F32), ALU.subtract
                                  ).then_inc(s_n_lo, 1)
                dve.wait_ge(s_n_nat, n + 1)
                for k in range(nt):
                    dve.bn_stats(bs[:, k], src[:, k * P:(k + 1) * P]).then_inc(s_dv, 1)
                dve.wait_ge(s_dv, steps + nt)
                for k in range(nt):
                    ins = dve.bn_aggr(mv[:, k], bs[:, k])
                ins.then_inc(s_n_var, 1)
                r_ = rs[:, r, 0:nt]
                dve.wait_ge(s_n_std, n + 1)
                dve.wait_ge(s_n_var, n + 1)
                dve.reciprocal(r_, std[:, 0:nt]).then_inc(s_dv, 1)
                dve.tensor_scalar(ve[:, 0:nt], mv[:, 0:nt, 1], EPS, None, ALU.add).then_inc(s_dv, 1)
                dve.wait_ge(s_dv, steps + (nt + 2))
                dve.tensor_tensor(tt[:, 0:nt], r_, r_, ALU.mult).then_inc(s_dv, 1)
                dve.wait_ge(s_dv, steps + (nt + 3))
                dve.tensor_tensor(tt[:, 0:nt], tt[:, 0:nt], ve[:, 0:nt], ALU.mult).then_inc(s_dv, 1)
                dve.wait_ge(s_dv, steps + (nt + 4))
                dve.tensor_scalar(tt[:, 0:nt], tt[:, 0:nt], -0.5, 1.5, ALU.mult, ALU.add).then_inc(s_dv, 1)
                dve.wait_ge(s_dv, steps + (nt + 5))
                dve.tensor_tensor(r_, r_, tt[:, 0:nt], ALU.mult).then_inc(s_n_r, 1)
                dve.wait_ge(s_n_r, n + 1)

            def moves(m, r):
                for k in range(NB):
                    dve.wait_ge(s_n_pr, m * NB + (k + 2))
                    src = ps[:, PR_BANKS[k], :].rearrange("p (s v) -> p s v", s=4)
                    sc = rs[:, r, k:k + 1]
                    for half in range(2):
                        dve.tensor_scalar(xs_q[half * HV:(half + 1) * HV, :, :, 2 * (m * NB + k) + 1:2 * (m * NB + k) + 2],
                                          src[TOK:P, 0:ST, half * HV:(half + 1) * HV].unsqueeze(3), sc[TOK:P], None, ALU.mult)
                    dve.tensor_scalar(x3[TOK:P, m * NB + k:m * NB + k + 1, :], src[TOK:P, ST:ST + 1, :], sc[TOK:P], None,
                                      ALU.mult).then_inc(s_n_pv, 1)

            STEPS = NB + 5
            batch(0, 0, h_cls, P, 0)
            dve.wait_ge(s_n_pr, 1)
            dve.tensor_scalar(cls_x.rearrange("p s v -> p (s v)"), ps[:, PR_BANKS[0], :], rs[:, 0, 0:1], None, ALU.mult
                              ).then_inc(s_n_pv, 1)
            dve.wait_ge(s_n_pv, 1)
            y = cls_x[:, 0]
            for i in range(ST):
                dve.tensor_tensor(cls_t, y, ps[:, F0_BANK, i * HID:(i + 1) * HID], ALU.mult).then_inc(s_cls, 1)
                dve.wait_ge(s_cls, 2 * i + 1)
                to = x3[:, NT - 1] if i == ST - 1 else cls_y[:, i + 1]
                dve.tensor_tensor(to, cls_t, cls_x[:, i + 1], ALU.mult).then_inc(s_cls, 1)
                dve.wait_ge(s_cls, 2 * i + 2)
                y = to
            for i in range(ST):
                src = (cls_x[:, 0] if i == 0 else cls_y[:, i]).rearrange("p (a v) -> p a v", a=2)
                dve.tensor_copy(cls_two[:, i], src.unsqueeze(2).to_broadcast([P, 2, 2, HV])).then_inc(s_cls, 1)
            dve.wait_ge(s_cls_t, 1)
            dve.tensor_copy(cls_col, ps[:, F0_BANK, ST * HID:ST * HID + 6]).then_inc(s_cls, 1)
            dve.wait_ge(s_cls, 10)
            for i in range(ST):
                for a in range(2):
                    dve.tensor_scalar(cls_f[:, i, a * TOK:(a + 1) * TOK], ps[:, FT_BANK, (2 * i + a) * TOK:(2 * i + a + 1) * TOK],
                                      cls_col[:, 2 * i + a:2 * i + a + 1], None, ALU.mult).then_inc(s_cls, 1)
            for m in range(NG):
                batch(m + 1, (m + 1) % 2, h_b[:, m], GT, 6 + m * STEPS)
                moves(m, (m + 1) % 2)

            def rest(n, g):
                dve.wait_ge(s_ya, n + 1)
                dve.tensor_tensor(xs_m[:, n], xs_m[:, n], parts[:, 0, g], ALU.subtract).then_inc(s_yr, 1)

            dve.wait_ge(s_n_pv, NT)
            dve.wait_ge(s_n_pa, NT - 1)
            for g in range(NS8):
                rest(g, g)
            for st in range(1, ST):
                for g in range(NS8):
                    n = st * NS8 + g
                    dve.wait_ge(s_cv, n - NS8 + 1)
                    dve.tensor_tensor(xs_m[:, n], ps[:, g, :], xs_m[:, n], ALU.mult).then_inc(s_y, 1)
                    if g:
                        dve.wait_ge(s_y, n - NS8)
                        rest(n - 1, g - 1)
                dve.wait_ge(s_y, st * NS8)
                rest(st * NS8 + NS8 - 1, NS8 - 1)
            x3_q = x3[:, 0:NT - 1].rearrange("p j v -> p v j")
            for g in range(NS8):
                dve.wait_ge(s_cv, (ST - 1) * NS8 + g + 1)
                src = ps[:, g, :].rearrange("p (v j u) -> p v j u", v=G8, u=2)
                for half in range(2):
                    for par in range(2):
                        to = x3_q[par * TOK:(par + 1) * TOK, half * HV + g * G8:half * HV + (g + 1) * G8]
                        ins = dve.tensor_tensor(to, src[half * HV:(half + 1) * HV, :, :, par], to, ALU.mult)
                ins.then_inc(s_y, 1)
            experts_vector(dve)

        @block.tensor
        def _(pe):
            pe.wait_ge(s_small, 16 * N_SMALL)
            pe.transpose(ps[:, POS_BANK, 0:TOK], pos_raw, ident[0:TOK, 0:TOK]).then_inc(s_prep_t, 1)
            pe.wait_ge(s_prep, V_MEAN)
            pe.matmul(ps[:, MEAN_BANK, :], mean_w, wp_raw, start=True, stop=True).then_inc(s_prep_t, 1)
            pe.matmul(ps[0:TOK, F_BANK, 0:ST * HID], fp_t[:, 0:TOK], f_view, start=True, stop=True).then_inc(s_prep_t, 1)
            pe.wait_ge(s_prep, V_FP0)
            for k in range(2 * ST):
                ins = pe.matmul(ps[:, FT_BANK, k * TOK:(k + 1) * TOK], wf_two[:, k * P:(k + 1) * P], fp_t[:, 1:SEQ],
                                start=True, stop=True)
            ins.then_inc(s_prep_t, 1)
            pe.matmul(ps[:, F0_BANK, 0:ST * HID], fp0, f_view, start=True, stop=True).then_inc(s_prep_t, 1)
            pe.wait_ge(s_wraw, 16)
            for b in range(NCK):
                if b >= WT_BANKS:
                    pe.wait_ge(s_wt_lo, b - WT_BANKS + 1)
                for k in range(CK):
                    ins = pe.transpose(ps[0:ROWS, b % WT_BANKS, k * HID:(k + 1) * HID], w_view[:, :, b * CK + k], ident)
                ins.then_inc(s_wt, 1)

            pe.wait_ge(s_wt_lo, NCK)
            pe.wait_ge(s_wt_hi, NCK)
            with pe.Fori(0, NG // 2) as i:
                for u in range(2):
                    for k in range(NCK):
                        r = (u * NCK + k) % 2
                        n = i * (2 * NCK) + (u * NCK + k)
                        pe.wait_ge(s_hi, n + 1)
                        for j in range(CK):
                            for w in (w_hi, w_lo):
                                a = (k * CK + j) * HID
                                ins = pe.matmul(ps[:, u, :], w[:, a:a + HID], ring_hi[:, r, j * GT:(j + 1) * GT],
                                                start=(k == 0 and j == 0 and w is w_hi), stop=False)
                        ins.then_inc(s_hi_used, 1)
                        pe.wait_ge(s_lo, n + 1)
                        for j in range(CK):
                            a = (k * CK + j) * HID
                            ins = pe.matmul(ps[:, u, :], w_hi[:, a:a + HID], ring_lo[:, r, j * GT:(j + 1) * GT],
                                            start=False, stop=(k == NCK - 1 and j == CK - 1))
                        ins.then_inc(s_lo_used, 1)

            pe.wait_ge(s_exp, 48)
            pe.wait_ge(s_tok, NG)
            for k in range(4):
                for j in range(EG):
                    e = k * EG + j
                    ins = pe.transpose(ps[:, PR_BANKS[k], j * HID:(j + 1) * HID], ew_raw[:, e * HID:(e + 1) * HID], ident)
                ins.then_inc(s_ew_t, 1)
            pe.transpose(ps[:, TR_BANKS[1], 0:E], sw_raw, ident[0:E, 0:E]).then_inc(s_ew_t, 1)

            def batch(n, r, src, width):
                nt = width // P
                for k in range(nt):
                    ins = pe.transpose(ps[:, TR_BANKS[r], k * P:(k + 1) * P], src[:, k * P:(k + 1) * P], ident)
                ins.then_inc(s_n_tr, 1)
                pe.wait_ge(s_n_hi, n + 1)
                pe.wait_ge(s_n_lo, n + 1)
                for k in range(nt):
                    x_h, x_l = (q[:, r, k * P:(k + 1) * P] for q in (ring_hi, ring_lo))
                    yield k
                    out_ = ps[:, PR_BANKS[k], :]
                    pe.matmul(out_, x_h, w_hi[:, WP0:], start=True, stop=False)
                    pe.matmul(out_, x_h, w_lo[:, WP0:], start=False, stop=False)
                    pe.matmul(out_, x_l, w_hi[:, WP0:], start=False, stop=True).then_inc(s_n_pr, 1)

            pe.wait_ge(s_prep, V_WPLO)
            for k in batch(0, 0, h_cls, P):
                pe.wait_ge(s_ew_lo, 1)
            pe.wait_ge(s_cls, 9)
            for k in range(6):
                ins = pe.matmul(ps[:, F0_BANK, ST * HID + k:ST * HID + k + 1],
                                cls_two[:, k // 2, k % 2].rearrange("p d v -> p (d v)"), ident[:, 0:1], start=True, stop=True)
            ins.then_inc(s_cls_t, 1)
            pe.wait_ge(s_ew_lo, 5)
            for m in range(NG):
                if m:
                    pe.wait_ge(s_n_nat, m)
                for k in batch(m + 1, (m + 1) % 2, h_b[:, m], GT):
                    pe.wait_ge(s_n_pv, m * NB + k - 2 if m else 1)
                    if m:
                        pe.wait_ge(s_n_pa, m * NB + k - 3)

            pe.wait_ge(s_cls_p, 7)
            pe.wait_ge(s_n_pv, NT)
            pe.wait_ge(s_n_pa, NT - 1)
            pe.wait_ge(s_prep, V_SELECT)
            toep_v = toep.rearrange("p q (t k c) -> p q t k c", k=3, c=CQ)
            with pe.Fori(0, ST) as st:
                for g in range(NS8):
                    q = g // 2
                    if g % 2 == 0:
                        pe.wait_ge(s_t[q], st * T_LOADED + T_LOADED)
                    pe.wait_ge(s_yc, st * NS8 + (g + 1))
                    rows = select[:, g * G8:(g + 1) * G8].unsqueeze(2).to_broadcast([P, G8, B])
                    bank = ps[:, g, :].rearrange("p (c b) -> p c b", c=G8)
                    pe.matmul(bank, carry_ab[:, bass.ds(st, 1), :].rearrange("p o n -> p (o n)"), rows, start=True, stop=False, skip_group_check=True)
                    pe.matmul(bank, carry_c[:, bass.ds(st, 1), :].rearrange("p o n -> p (o n)"), rows, start=False, stop=False, skip_group_check=True)
                    for c in range(G8):
                        for k in range(3):
                            for j in range(3 - k):
                                ins = pe.matmul(ps[:, g, c * B:(c + 1) * B], toep_v[:, q, :, k, (g % 2) * G8 + c],
                                                parts[:, j, g, c * B:(c + 1) * B], start=False,
                                                stop=(c == G8 - 1 and k == 2), skip_group_check=True)
                    ins.then_inc(s_cv, 1)
            experts_tensor(pe)


_INS = ["x", "L0_tok_W", "L0_tok_b", "L0_tok_class_token", "L0_tok_pos_embed", "L0_attn_W_proj", "L0_attn_W_filt",
        "L0_ffn_switch_w", "L0_ffn_switch_b", "L0_ffn_expert_w", "L0_ffn_expert_b"]
_OUTS = [((B, SEQ, HID), "float32")]


def kernel(**inputs):
    import numpy as _np
    import concourse.bacc as _bacc
    from concourse import mybir as _mybir
    from concourse.bass_utils import run_bass_kernel_spmd as _run

    nc = _bacc.Bacc("TRN2", target_bir_lowering=False, num_devices=1)
    arrays, args = {}, []
    given = {name: _np.ascontiguousarray(inputs[name]) for name in _INS}
    given["constants"] = CONSTS
    given["filter_positions"] = positions_t()
    for name, a in given.items():
        arrays[f"in_{name}_dram"] = a
        args.append(nc.dram_tensor(f"in_{name}_dram", a.shape, _mybir.dt.from_np(a.dtype), kind="ExternalInput").ap())
    for i, (shape, dtype) in enumerate(_OUTS):
        args.append(nc.dram_tensor(f"out_{i}_dram", shape, _mybir.dt.from_np(_np.dtype(dtype)), kind="ExternalOutput").ap())
    build(nc, *args)
    r = _run(nc, [arrays], core_ids=[0])
    return r.results[0]["out_0_dram"]
```

```python
from contextlib import ExitStack

import numpy as np

import concourse.bass as bass
from concourse import mybir

P = 128
B, C, IMG, PATCH, HID = 64, 3, 224, 28, 128
NP = IMG // PATCH
TOK = NP * NP
SEQ = TOK + 1
ROWS = C * PATCH
GI = 8
GT = GI * TOK
NG = B // GI
XI = NP * IMG
XG = GI * XI
CK = 4
NCK = PATCH // CK
NB = GT // P
NT = B * TOK // P + 1
ST = 3
HV = HID // 2
VB = 32
CQ = 16
NQ = HV // CQ
G8 = 8
NS8 = HV // G8
PARTS = 4
E = 16
EG = 4
CAP = int(1.2 * (B * SEQ) / E)
EPS = 1e-5
COPIES = 16
RHO = 128

F32 = mybir.dt.float32
F32R = mybir.dt.float32r
BF16 = mybir.dt.bfloat16
I32 = mybir.dt.int32
ALU = mybir.AluOpType
ACT = mybir.ActivationFunctionType
AX = mybir.AxisListType

CONST_COLS = {}


def constants():
    p = np.arange(P)
    parts = [
        ("ident", np.eye(P)),
        ("select", (p[:, None] % VB == np.arange(VB)[None, :])),
        ("before", (p[:, None] < p[None, :])),
        ("image_half", (p[:, None] // TOK == np.arange(2)[None, :])),
        ("even_before", (2 * p[:, None] < p[None, :]) & (p[:, None] < B // 2)),
        ("odd_before", (2 * p[:, None] + 1 < p[None, :]) & (p[:, None] < B // 2)),
        ("priority", np.broadcast_to(E - np.arange(E)[None, :], (P, E))),
        ("classes_before", 2 * np.arange(B // 2)[None, :] + p[:, None] // TOK + 1),
        ("row", p[:, None]),
    ]
    at = 0
    for name, a in parts:
        CONST_COLS[name] = (at, at + a.shape[1])
        at += a.shape[1]
    return np.concatenate([a.astype(np.float32) for _, a in parts], axis=1)


def positions_t():
    half = HID // 2
    freqs = np.power(np.float32(10000.0), -np.arange(half, dtype=np.float32) / np.float32(half)).astype(np.float32)
    phi = np.arange(SEQ, dtype=np.float32)[:, None] * freqs[None, :]
    return np.ascontiguousarray(np.concatenate([np.sin(phi), np.cos(phi)], axis=-1).astype(np.float32).T)


CONSTS = constants()


def build(nc, x, tok_w, tok_b, class_token, pos_embed, w_proj, w_filt, switch_w, switch_b, expert_w, expert_b,
          consts, filt_pos_t, out):
    with ExitStack() as ctx:
        def sb(name, shape, dt=F32):
            return ctx.enter_context(nc.sbuf_tensor(name, shape, dt))

        def sem(name):
            return ctx.enter_context(nc.semaphore(name))

        ps = ctx.enter_context(nc.psum_tensor("ps", [P, 8, 512], F32))

        arena = sb("arena", [P, 2 * XG + E * HID + HID])
        ring_hi = sb("ring_hi", [P, 2, CK * GT], F32R)
        ring_lo = sb("ring_lo", [P, 2, CK * GT], F32R)
        w_hi = sb("w_hi", [P, PATCH * HID + 4 * HID], F32R)
        w_lo = sb("w_lo", [P, PATCH * HID + 4 * HID], F32R)
        h = sb("h", [P, NT * HID])
        con = sb("con", [P, CONSTS.shape[1]])
        pos_t = sb("pos_t", [P, TOK])
        select = sb("select", [P, VB], BF16)
        carry = sb("carry", [P, ST, HV // VB, P], BF16)
        ident_bf, before_bf, ones_bf = (sb(name, [P, P], BF16)[:] for name in ("ident_bf", "before_bf", "ones_bf"))
        cols = sb("cols", [P, 8])
        stat = sb("stat", [P, 176])

        def c_(name):
            a, b = CONST_COLS[name]
            return con[:, a:b]

        ident = c_("ident")
        b_col, ct_col, p0_col, hc_col, eps_col = (cols[:, i:i + 1] for i in range(5))
        WP0 = PATCH * HID

        x_raw = arena[:, 0:2 * XG].rearrange("p (s n) -> p s n", s=2)
        a0 = XG
        w_raw = arena[:, a0:a0 + ROWS * PATCH]; a0 += ROWS * PATCH
        wp_raw = arena[:, a0:a0 + 4 * HID]; a0 += 4 * HID
        wp_mid = arena[:, a0:a0 + 4 * HID]; a0 += 4 * HID
        wf_raw = arena[:, a0:a0 + ST * HID]; a0 += ST * HID
        wf_two = arena[:, a0:a0 + ST * 2 * HID]; a0 += ST * 2 * HID
        fp_t = arena[:, a0:a0 + SEQ]; a0 += SEQ
        fp0 = arena[:, a0:a0 + P]; a0 += P
        mean_w = arena[:, a0:a0 + P]; a0 += P
        pos_raw = arena[0:TOK, a0:a0 + HID]; a0 += HID
        f_rest = arena[0:TOK, a0:a0 + ST * HID]; a0 += ST * HID
        f_parts = arena[0:TOK, a0:a0 + ST * 3 * HID // 2].bitcast(BF16).rearrange("p (n k c) -> p n k c", k=3, c=CQ)
        a0 += ST * 3 * HID // 2
        f_zero = arena[0:ST * 2 * NQ, a0:a0 + (TOK - 1) * 3 * CQ // 2].bitcast(BF16); a0 += (TOK - 1) * 3 * CQ // 2
        assert a0 <= 2 * XG
        ew_raw = arena[:, 2 * XG:2 * XG + E * HID]
        sw_raw = arena[0:E, 2 * XG + E * HID:2 * XG + E * HID + HID]
        TW = 3 * P * CQ
        toep = arena[:, 0:NQ * TW // 2].bitcast(BF16).rearrange("p (q n) -> p q n", q=NQ)
        XO = NQ * TW // 2 - 2 * G8 * B
        xs = arena[:, XO:XO + ST * HV * B]
        xs_q = xs.rearrange("p (s v b) -> p s v b", s=ST, v=HV)
        xs_m = xs.rearrange("p (m n) -> p m n", n=G8 * B)
        X3 = XO + ST * HV * B
        x3 = arena[:, X3:X3 + NT * HID].rearrange("p (j v) -> p j v", v=HID)
        PO = X3 + NT * HID
        parts = arena[:, PO:PO + 3 * PARTS * G8 * B // 2].bitcast(BF16).rearrange("p (k g n) -> p k g n", k=3, g=PARTS)
        assert PO + 3 * PARTS * G8 * B // 2 <= arena.shape[1]
        a0 = PO
        cls_x = arena[:, a0:a0 + 4 * HID].rearrange("p (s v) -> p s v", s=4); a0 += 4 * HID
        cls_y = arena[:, a0:a0 + 3 * HID].rearrange("p (s v) -> p s v", s=3); a0 += 3 * HID
        cls_t = arena[:, a0:a0 + HID]; a0 += HID
        cls_two = arena[:, a0:a0 + ST * 2 * HID].rearrange("p (i a d v) -> p i a d v", i=ST, a=2, d=2)
        a0 += ST * 2 * HID
        cls_col = arena[:, a0:a0 + 6]; a0 += 6
        cls_f = arena[:, a0:a0 + ST * P].rearrange("p (i n) -> p i n", i=ST); a0 += ST * P
        cls_a = arena[:, a0:a0 + ST * P // 2].bitcast(BF16).rearrange("p (i n) -> p i n", i=ST); a0 += ST * P // 2
        assert a0 <= PO + 3 * PARTS * G8 * B // 2

        toep_rows = nc.dram_tensor("toeplitz_rows", [ST, 2, NQ, RHO, 3, CQ], BF16, kind="Internal").ap()

        toep_copies = nc.dram_tensor("toeplitz_copies", [ST, 2, NQ, COPIES, RHO, 3, CQ], BF16, kind="Internal").ap()

        s_const = sem("constants_loaded"); s_small = sem("small_loaded"); s_wraw = sem("patch_weights_loaded"); s_exp = sem("expert_weights_loaded")
        s_x = [sem("images_loaded_even"), sem("images_loaded_odd")]
        s_zero = sem("rings_zeroed"); s_prep = sem("prepared_by_vector"); s_prep_a = sem("prepared_by_scalar")
        s_prep_t = sem("prepared_by_tensor")
        s_wt = sem("patch_weights_turned"); s_wt_hi = sem("patch_weights_high"); s_wt_lo = sem("patch_weights_low")
        s_rows = sem("toeplitz_rows_stored"); s_copies = sem("toeplitz_copies_stored")
        s_hi = sem("high_parts_ready"); s_lo = sem("low_parts_ready")
        s_hi_used = sem("high_parts_used"); s_lo_used = sem("low_parts_used")
        s_tok = sem("tokens_ready")
        s_ew_t = sem("expert_weights_turned"); s_ew_hi = sem("expert_weights_high"); s_ew_lo = sem("expert_weights_low")
        s_n_hi = sem("token_high_ready"); s_n_lo = sem("token_low_ready"); s_n_tr = sem("tokens_turned")
        s_n_nat = sem("tokens_stored_by_row"); s_n_var = sem("variances_ready"); s_n_std = sem("deviations_ready")
        s_n_r = sem("scales_ready"); s_n_pr = sem("projected"); s_n_pa = sem("projections_moved_by_scalar")
        s_n_pv = sem("projections_moved_by_vector")
        s_dv = sem("vector_steps")
        s_cls = sem("class_token_vector"); s_cls_t = sem("class_token_tensor"); s_cls_p = sem("class_token_gpsimd")
        s_t = [sem(f"toeplitz_loaded_{q}") for q in range(2)]
        s_tz = sem("toeplitz_blocks_zeroed"); s_con = sem("constants_ready")
        s_ya = sem("part_a_ready"); s_yr = sem("rest_ready"); s_yb = sem("part_b_ready"); s_yc = sem("part_c_ready")
        s_cv = sem("convolved"); s_y = sem("stage_output_ready")

        block = ctx.enter_context(nc.Block())

        x_src = x.rearrange("b c (h r) w -> b c r h w", r=PATCH)
        N_SMALL = 7
        V_EPS, V_MEAN, V_FZERO, V_SELECT, V_HC, V_TWO, V_FP0, V_CLS, V_POS, V_MID, V_WPLO, V_FREST, V_FC = (
            1, 2, 3, 4, 5, 11, 12, 13, 14, 15, 16, 17, 18)
        A_WPHI, A_FA, A_FB = 1, 2, 3
        T_POS, T_MEAN, T_F, T_FT, T_F0 = 1, 2, 3, 4, 5
        WT_BANKS = 3
        MEAN_BANK, F_BANK, FT_BANK, F0_BANK, POS_BANK = 3, 4, 5, 6, 7
        BATCHES = NG + 1
        PR_BANKS = [0, 1, 4, 7]
        CLS_BANK = PR_BANKS[3]

        def load_images(eng, g, slot):
            for i in range(GI):
                for c in range(C):
                    eng.dma_start(
                        x_raw[c * PATCH:(c + 1) * PATCH, slot, i * XI:(i + 1) * XI].rearrange("p (h w) -> p h w", h=NP),
                        x_src[g * GI + i, c]).then_inc(s_x[slot], 16)

        X_LOADED = GI * C * 16

        def load_toeplitz(eng, i, pair, half):
            for w in range(TOK // COPIES):
                s0 = half * TOK + w * COPIES
                src = toep_copies[i, half, 2 * pair]
                eng.dma_start(
                    toep[s0:s0 + COPIES, 2 * pair:2 * pair + 2, half * TOK * 3 * CQ:(half + 1) * TOK * 3 * CQ],
                    bass.AP(src.tensor, offset=src.offset + (TOK - 1 - w * COPIES) * 3 * CQ,
                            ap=[[(RHO - 1) * 3 * CQ, COPIES], [COPIES * RHO * 3 * CQ, 2], [1, TOK * 3 * CQ]])
                ).then_inc(s_t[pair], 16)

        T_LOADED = 2 * (TOK // COPIES) * 16

        x_chunk = x_raw.rearrange("p s (t j) -> p s t j", j=PATCH)
        hi_chunk = ring_hi[:].rearrange("p r (j t) -> p r t j", j=CK)
        lo_chunk = ring_lo[:].rearrange("p r (j t) -> p r t j", j=CK)
        h_b = h[:, 0:NG * GT].rearrange("p (n t) -> p n t", t=GT)
        h_cls = h[:, NG * GT:]
        f_view = wf_raw.rearrange("p (v i) -> p i v", i=ST)
        f_sums = ps[0:TOK, F_BANK, 0:ST * HID].rearrange("p (n c) -> p n c", c=CQ)
        f_rest_n = f_rest.rearrange("p (n c) -> p n c", c=CQ)
        w_view = w_raw.rearrange("p (r j) -> p r j", j=PATCH)
        TR_BANKS = [2, 3]
        EW_BANKS = [2, 3, 4, 7]

        def by_vector(n, k):
            return k == 1 or (k == 3 and n % 2 == 0)

        def moved(n, k):
            v = sum(by_vector((i // NB) + 1, i % NB) for i in range((n - 1) * NB + k))
            return v + 1, (n - 1) * NB + k - v

        def tokens_of(n):
            return h_b[:, n - 1] if n else h_cls

        LAST = NG * NCK

        bs = stat[:, 0:30].rearrange("p (k n) -> p k n", n=6)
        mv = stat[:, 30:40].rearrange("p (k n) -> p k n", n=2)
        std, tt = stat[:, 40:45], stat[:, 45:50]
        rs = stat[:, 50:58].rearrange("p (r k) -> p r k", r=2)
        CLS_X, CLS_Y3, CLS_TWO, CLS_COL, CLS_F = 1, 6, 9, 10, 16

        def pool_parts_c(pool, n0, n1):
            for n in range(n0, n1):
                pool.wait_ge(s_yb, n + 1)
                pool.tensor_tensor(parts[:, 2, n % PARTS], xs_m[:, n], parts[:, 1, n % PARTS], ALU.subtract).then_inc(s_yc, 1)

        def pool_carry(pool):
            pool.wait_ge(s_cls, CLS_F)
            pool.memset(carry[3 * VB:P], 0.0).then_inc(s_cls_p, 1)
            pool.wait_ge(s_cls_p, 1)
            yield
            pool.tensor_copy(cls_a, cls_f).then_inc(s_cls_p, 1)
            pool.wait_ge(s_cls_p, 2)
            yield
            pool.tensor_copy(carry[0:VB, :, 0], cls_a[0:VB]).then_inc(s_cls_p, 1)
            pool.wait_ge(s_cls_p, 3)
            yield
            pool.tensor_copy(carry[0:VB, :, 1], cls_a[VB:2 * VB]).then_inc(s_cls_p, 1)
            pool.wait_ge(s_cls_p, 4)
            yield
            pool.tensor_tensor(cls_f, cls_f, cls_a, ALU.subtract).then_inc(s_cls_p, 1)
            pool.wait_ge(s_cls_p, 5)
            yield
            pool.tensor_copy(cls_a, cls_f).then_inc(s_cls_p, 1)
            pool.wait_ge(s_cls_p, 6)
            yield
            pool.tensor_copy(carry[VB:2 * VB, :, 0], cls_a[0:VB]).then_inc(s_cls_p, 1)
            pool.wait_ge(s_cls_p, 7)
            yield
            pool.tensor_copy(carry[VB:2 * VB, :, 1], cls_a[VB:2 * VB]).then_inc(s_cls_p, 1)
            pool.wait_ge(s_cls_p, 8)
            yield
            pool.tensor_tensor(carry[2 * VB:3 * VB, :, 0], cls_f[HV:HV + VB], cls_a[HV:HV + VB], ALU.subtract).then_inc(s_cls_p, 1)
            pool.wait_ge(s_cls_p, 9)
            yield
            pool.tensor_tensor(carry[2 * VB:3 * VB, :, 1], cls_f[HV + VB:P], cls_a[HV + VB:P], ALU.subtract).then_inc(s_cls_p, 1)
            pool.wait_ge(s_cls_p, 10)
            yield
            pool.wait_ge(s_const, 16)
            pool.wait_ge(s_ew_t, 5)
            pool.memset(ones_bf, 1.0).then_inc(s_con, 1)
            yield
            pool.tensor_copy(before_bf, c_("before")).then_inc(s_con, 1)
            yield
            pool.tensor_copy(ident_bf, ident).then_inc(s_con, 1)

        def tile0(n):
            return 0 if n == 0 else 1 + (n - 1) * NB

        def tiles(n):
            return 1 if n == 0 else NB

        def rank(i):
            return 1 - i if i < 2 else i

        def span(n):
            return slice(tile0(n), tile0(n) + tiles(n))

        def h_tiles(n):
            a = (NT - 1) * HID if n == 0 else (n - 1) * GT
            return h[:, a:a + tiles(n) * HID].rearrange("p (k v) -> p k v", v=HID)

        def wide(col, n):
            return col[:, span(n)].unsqueeze(2).to_broadcast([P, tiles(n), HID])

        SEL = 8
        PAD = 32
        a0 = 0

        def by_tile(width, dt=F32):
            nonlocal a0
            cols_ = NT * width if dt == F32 else NT * width // 2
            v = arena[:, a0:a0 + cols_]
            a0 += cols_
            v = v if dt == F32 else v.bitcast(dt)
            return v.rearrange("p (j e) -> p j e", e=width)

        xf, total, gated = by_tile(HID), by_tile(HID), by_tile(HID)
        picked = arena[:, a0:a0 + SEL * EG * HID].rearrange("p (s i f) -> p s i f", s=SEL, i=EG)
        a0 += SEL * EG * HID
        logit, below, expo, key, chosen, counts, chosen_count = (by_tile(E) for _ in range(7))
        eb_raw, eb_rest = gated[:, 0:EG], gated[:, EG:2 * EG]
        chosen_bf = by_tile(PAD, BF16)
        chosen_t = arena[:, a0:a0 + (NG + 1) * P // 2].bitcast(BF16).rearrange("p (n m) -> p n m", m=P)
        a0 += (NG + 1) * P // 2
        assert a0 <= X3
        a0 = PO
        cls_share = arena[:, a0:a0 + (NT - 1) * E].rearrange("p (j e) -> p j e", e=E); a0 += (NT - 1) * E
        eb = arena[:, a0:a0 + 3 * NB * HID // 2].bitcast(BF16).rearrange("p (k n) -> p k n", k=3)
        a0 += 3 * NB * HID // 2
        sum_before = arena[:, a0:a0 + (NG + 1) * PAD // 2].bitcast(BF16).rearrange("p (n e) -> p n e", e=PAD)
        a0 += (NG + 1) * PAD // 2
        sum_two = arena[:, a0:a0 + PAD].bitcast(BF16).rearrange("p (k e) -> p k e", k=2); a0 += PAD
        sum_one = arena[:, a0:a0 + PAD // 2].bitcast(BF16); a0 += PAD // 2
        bs2 = arena[:, a0:a0 + NT * 6].rearrange("p (j n) -> p j n", n=6); a0 += NT * 6
        mv2 = arena[:, a0:a0 + NT * 2].rearrange("p (j n) -> p j n", n=2); a0 += NT * 2
        std2, rs2, tt2, shift2, top, key_top, denom, prob, place, p_keep, p_drop, as_cls = (
            arena[:, a0 + k * NT:a0 + (k + 1) * NT] for k in range(12))
        a0 += 12 * NT
        cls_seen = arena[:, a0:a0 + 2]; a0 += 2
        assert a0 <= arena.shape[1]
        swb = stat[:, 64:64 + E]
        TR4, OHT_BANK, LG_BANK, BI_BANK = 4, 5, 6, 7
        CNT0 = P
        ROUNDS = [(0, 2), (2, 4), (4, NG + 1)]
        CLS0 = GT

        s_h1 = sem("residual_sums_by_gpsimd"); s_eb = sem("expert_bias_steps"); s_ebl = sem("expert_bias_loaded")
        s_l2 = sem("second_norm_steps"); s_var = sem("second_variances_ready"); s_dev = sem("second_deviations_ready")
        s_norm = sem("second_norm_ready"); s_xf = sem("normed_tokens_ready"); s_tr = sem("normed_tokens_turned")
        s_eh = sem("normed_high_ready"); s_el = sem("normed_low_ready"); s_lg = sem("logits_ready")
        s_rt = sem("routing_steps"); s_bel = sem("logits_below_top_ready"); s_ex = sem("exponentials_ready")
        s_oh = sem("experts_chosen"); s_cnt = sem("counts_ready"); s_gate = sem("gates_ready")
        s_oht = sem("chosen_turned_stored"); s_sum = sem("chosen_summed"); s_bi = sem("biases_ready")
        s_e = sem("expert_groups_computed"); s_p0 = sem("first_group_picked"); s_pk = sem("later_groups_picked")
        s_tot = sem("picked_summed"); s_bt = sem("biases_added"); s_g = sem("dropped_shares_ready"); s_fin = sem("batches_finished")
        s_ps = sem("gpsimd_sum_steps"); s_cs = sem("class_seen"); s_cc = sem("class_counts_ready"); s_out = sem("outputs_stored")
        s_xv = sem("normed_tokens_by_vector"); s_last = sem("last_biases_added"); s_lf = sem("last_tiles_finished")
        s_ac = sem("compared_with_the_class"); s_cv2 = sem("class_seen_stored")

        def turned(n):
            return ps[:, OHT_BANK, 2 * P:3 * P] if n == 0 else ps[:, TR4, :]

        def ring_of(ring, n, k0, k1):
            return ring[:, 0, CLS0:CLS0 + P] if n == 0 else ring[:, n % 2, k0 * P:k1 * P]

        def round_tiles(r):
            a, b = ROUNDS[r]
            return slice(tile0(a), tile0(b - 1) + tiles(b - 1))

        def experts_sync(sp):
            sp.wait_ge(s_eb, 2)
            for k in range(NB):
                sp.dma_start(eb_raw[PAD * k:PAD * k + E, k], expert_b).then_inc(s_ebl, 16)
            def store(n, k0, k1):
                for par in range(2):
                    sp.dma_start(
                        out[(n - 1) * GI + 2 * k0:(n - 1) * GI + 2 * k1, 1:SEQ].rearrange("(k u) t v -> u t k v", u=2)[par],
                        h_tiles(n)[par * TOK:(par + 1) * TOK, k0:k1]).then_inc(s_out, 16)

            for n in range(1, NG):
                sp.wait_ge(s_fin, n)
                store(n, 0, NB)
            sp.wait_ge(s_fin, NG)
            sp.dma_start(out[:, 0], h_tiles(0)[0:B, 0]).then_inc(s_out, 16)
            for k0, k1 in ((0, NB - 1), (NB - 1, NB)):
                sp.wait_ge(s_lf, k1)
                store(NG, k0, k1)
            sp.wait_ge(s_out, 16 * (2 * NG + 3))

        def experts_pool(pool):
            pool.wait_ge(s_y, ST * NS8)
            pool.memset(chosen_bf, 0.0).then_inc(s_eb, 1)
            pool.memset(eb_raw, 0.0).then_inc(s_eb, 1)
            for g in range(1, NG):
                pool.tensor_tensor(h_b[:, g], h_b[:, g], x3[:, g * NB:(g + 1) * NB].rearrange("p j v -> p (j v)"), ALU.add
                                   ).then_inc(s_h1, 1)
            flat = eb_raw.rearrange("p k f -> p (k f)")
            rest_ = eb_rest.rearrange("p k f -> p (k f)")
            pool.wait_ge(s_ebl, 16 * NB)
            pool.tensor_copy(eb[:, 0], flat).then_inc(s_eb, 1)
            pool.wait_ge(s_eb, 3)
            pool.tensor_tensor(rest_, flat, eb[:, 0], ALU.subtract).then_inc(s_eb, 1)
            pool.wait_ge(s_eb, 4)
            pool.tensor_copy(eb[:, 1], rest_).then_inc(s_eb, 1)
            pool.wait_ge(s_eb, 5)
            pool.tensor_tensor(eb[:, 2], rest_, eb[:, 1], ALU.subtract).then_inc(s_eb, 1)
            pool.wait_ge(s_eb, 3)

            def summed(n):
                pool.wait_ge(s_oh, rank(n) + 1)
                o = chosen_bf[:, span(n)]
                b = 3 * (n - 1)
                if n > 1:
                    pool.wait_ge(s_sum, b)
                pool.tensor_tensor(sum_two, o[:, 0:2], o[:, 2:4], ALU.add).then_inc(s_sum, 1)
                pool.wait_ge(s_sum, b + 1)
                pool.tensor_tensor(sum_one, sum_two[:, 0], sum_two[:, 1], ALU.add).then_inc(s_sum, 1)
                pool.wait_ge(s_sum, b + 2)
                if n == 1:
                    pool.tensor_copy(sum_before[:, n + 1], sum_one).then_inc(s_sum, 1)
                else:
                    pool.tensor_tensor(sum_before[:, n + 1], sum_before[:, n], sum_one, ALU.add).then_inc(s_sum, 1)

            ps_steps = 0

            def dropped(n):
                nonlocal ps_steps
                if n == 1:
                    pool.wait_ge(s_xv, 1)
                pool.wait_ge(s_gate, n if n else NG + 1)
                pool.tensor_tensor(gated[:, span(n)], xf[:, span(n)], wide(p_drop, n), ALU.mult).then_inc(s_ps, 1)
                ps_steps += 1
                pool.wait_ge(s_ps, ps_steps)
                pool.tensor_tensor(gated[:, span(n)], gated[:, span(n)], h_tiles(n), ALU.add).then_inc(s_g, 1)

            def sum_picked(t):
                nonlocal ps_steps
                s = picked[:, t % SEL]
                pool.wait_ge(s_pk, (EG - 1) * (rank(t) + 1))
                pool.tensor_tensor(s[:, 0:2], s[:, 0:2], s[:, 2:4], ALU.add).then_inc(s_ps, 1)
                ps_steps += 1
                pool.wait_ge(s_ps, ps_steps)
                pool.tensor_tensor(total[:, t], s[:, 0], s[:, 1], ALU.add).then_inc(s_tot, 1)

            def finish(n, done):
                nonlocal ps_steps
                pool.wait_ge(s_bt, n + 1)
                pool.wait_ge(s_g, done)
                pool.tensor_tensor(total[:, span(n)], total[:, span(n)], wide(p_keep, n), ALU.mult).then_inc(s_ps, 1)
                ps_steps += 1
                pool.wait_ge(s_ps, ps_steps)
                pool.tensor_tensor(h_tiles(n), total[:, span(n)], gated[:, span(n)], ALU.add).then_inc(s_fin, 1)

            for n in range(1, NG + 1):
                if n > 1:
                    dropped(n)
                for k in range(NB):
                    sum_picked(tile0(n) + k)
                    if k == 0 and n == 1:
                        sum_picked(0)
                        dropped(1)
                    if k == 0 and n < NG:
                        summed(n)
                    if k == 1 and n > 1:
                        finish(n - 1, n - 1)
                    if k == 2 and n == NG:
                        dropped(0)
                        finish(0, NG + 1)

        def experts_scalar(act):
            def second_deviations(r):
                act.wait_ge(s_var, r + 1)
                act.activation(std2[:, round_tiles(r)], mv2[:, round_tiles(r), 1], ACT.Sqrt, bias=eps_col).then_inc(s_dev, 1)

            def normed(n):
                for r, (a, b) in enumerate(ROUNDS):
                    if n == a:
                        act.wait_ge(s_norm, r + 1)
                if n >= 2:
                    act.wait_ge(s_h1, n - 1)
                for k in range(2 if n == 1 else tiles(n)):
                    t = tile0(n) + k
                    ins = act.activation(xf[:, t], h_tiles(n)[:, k], ACT.Identity, bias=shift2[:, t:t + 1], scale=rs2[:, t:t + 1])
                ins.then_inc(s_xf, 1)

            def high(n):
                act.wait_ge(s_tr, rank(n) + 1)
                if n >= 3:
                    act.wait_ge(s_e, EG * tile0(n - 1))
                act.activation(ring_of(ring_hi, n, 0, NB), turned(n), ACT.Copy).then_inc(s_eh, 1)

            def exponentials(n):
                act.wait_ge(s_bel, rank(n) + 1)
                act.activation(expo[:, span(n)], below[:, span(n)], ACT.Exp).then_inc(s_ex, 1)

            def store_turned(n):
                act.wait_ge(s_cnt, rank(n) + 1)
                w = tiles(n) * PAD
                act.activation(chosen_t[0:w, n], turned_bf[0:w], ACT.Copy).then_inc(s_oht, 1)

            def first_group(t):
                if t >= SEL:
                    act.wait_ge(s_tot, rank(t - SEL) + 1)
                act.wait_ge(s_e, EG * rank(t) + 1)
                for e in range(EG):
                    ins = act.activation(picked[:, t % SEL, e], ps[:, 0, e * HID:(e + 1) * HID], ACT.Copy,
                                         scale=chosen[:, t, e:e + 1])
                ins.then_inc(s_p0, 1)

            second_deviations(0)
            act.wait_ge(s_norm, 1)
            normed(1)
            normed(0)
            high(1)
            high(0)
            second_deviations(1)
            exponentials(1)
            exponentials(0)
            for n in range(1, NG + 1):
                act.wait_ge(s_oh, rank(n) + 1)
                for k in range(NB):
                    first_group(tile0(n) + k)
                    if n == 1 and k == 0:
                        store_turned(1)
                        normed(2)
                        act.wait_ge(s_oh, rank(0) + 1)
                        first_group(0)
                        store_turned(0)
                    if n < NG:
                        if k == 0:
                            high(n + 1)
                            if n == 2:
                                second_deviations(2)
                        if k == 2 and n + 2 <= NG:
                            normed(n + 2)
                        if k == 1:
                            exponentials(n + 1)
                        if k == 2:
                            store_turned(n + 1)

        def experts_vector(dve):
            dve.wait_ge(s_y, ST * NS8)
            l2 = 0
            dve.tensor_tensor(h_b[:, 0], h_b[:, 0], x3[:, 0:NB].rearrange("p j v -> p (j v)"), ALU.add).then_inc(s_l2, 1)
            dve.tensor_tensor(h_cls, h_cls, x3[:, NT - 1], ALU.add).then_inc(s_l2, 1)
            l2 += 2

            def statistics(n):
                nonlocal l2
                if n >= 2:
                    dve.wait_ge(s_h1, n - 1)
                else:
                    dve.wait_ge(s_l2, rank(n) + 1)
                for k in range(tiles(n)):
                    dve.bn_stats(bs2[:, tile0(n) + k], h_tiles(n)[:, k]).then_inc(s_l2, 1)
                l2 += tiles(n)
                dve.wait_ge(s_l2, l2)
                for k in range(tiles(n)):
                    ins = dve.bn_aggr(mv2[:, tile0(n) + k], bs2[:, tile0(n) + k])
                if n in (0, 3, NG):
                    ins.then_inc(s_var, 1)
                else:
                    ins.then_inc(s_l2, 1)
                    l2 += 1

            def second_scales(r):
                nonlocal l2
                t = round_tiles(r)
                dve.wait_ge(s_var, r + 1)
                dve.wait_ge(s_dev, r + 1)
                dve.reciprocal(rs2[:, t], std2[:, t]).then_inc(s_l2, 1)
                dve.wait_ge(s_l2, l2 + 1)
                dve.scalar_tensor_tensor(out=tt2[:, t], in0=mv2[:, t, 1], scalar=EPS, in1=rs2[:, t],
                                         op0=ALU.add, op1=ALU.mult).then_inc(s_l2, 1)
                dve.wait_ge(s_l2, l2 + 2)
                dve.scalar_tensor_tensor(out=tt2[:, t], in0=tt2[:, t], scalar=-0.5, in1=rs2[:, t],
                                         op0=ALU.mult, op1=ALU.mult).then_inc(s_l2, 1)
                dve.wait_ge(s_l2, l2 + 3)
                dve.scalar_tensor_tensor(out=rs2[:, t], in0=tt2[:, t], scalar=1.5, in1=rs2[:, t],
                                         op0=ALU.add, op1=ALU.mult).then_inc(s_l2, 1)
                dve.wait_ge(s_l2, l2 + 4)
                l2 += 4
                dve.scalar_tensor_tensor(out=shift2[:, t], in0=mv2[:, t, 0], scalar=-1.0, in1=rs2[:, t],
                                         op0=ALU.mult, op1=ALU.mult).then_inc(s_norm, 1)

            def low_parts(n):
                dve.wait_ge(s_eh, rank(n) + 1)
                dve.tensor_tensor(ring_of(ring_lo, n, 0, NB), turned(n), ring_of(ring_hi, n, 0, NB).bitcast(F32),
                                  ALU.subtract).then_inc(s_el, 1)

            steps = 0

            def choose(n):
                nonlocal steps
                nt, s = tiles(n), span(n)
                by = lambda col: col[:, s].unsqueeze(2).to_broadcast([P, nt, E])
                dve.wait_ge(s_lg, rank(n) + 1)
                dve.tensor_tensor(logit[:, s], ps[:, lg_bank(n), 0:nt * E].rearrange("p (k e) -> p k e", e=E),
                                  swb.unsqueeze(1).to_broadcast([P, nt, E]), ALU.add).then_inc(s_rt, 1)
                dve.wait_ge(s_rt, steps + 1)
                dve.tensor_reduce(top[:, s], logit[:, s], AX.X, ALU.max).then_inc(s_rt, 1)
                dve.wait_ge(s_rt, steps + 2)
                dve.tensor_tensor(below[:, s], logit[:, s], by(top), ALU.subtract).then_inc(s_bel, 1)
                dve.wait_ge(s_bel, rank(n) + 1)
                dve.scalar_tensor_tensor(out=key[:, s], in0=below[:, s], scalar=0.0,
                                         in1=c_("priority").unsqueeze(1).to_broadcast([P, nt, E]),
                                         op0=ALU.is_ge, op1=ALU.mult).then_inc(s_rt, 1)
                dve.wait_ge(s_rt, steps + 3)
                dve.tensor_reduce(key_top[:, s], key[:, s], AX.X, ALU.max).then_inc(s_rt, 1)
                dve.wait_ge(s_rt, steps + 4)
                dve.tensor_tensor(chosen[:, s], key[:, s], by(key_top), ALU.is_equal).then_inc(s_rt, 1)
                if n == 1:
                    dve.wait_ge(s_eb, 1)
                dve.tensor_tensor(chosen_bf[:, s, 0:E], key[:, s], by(key_top), ALU.is_equal).then_inc(s_oh, 1)
                dve.wait_ge(s_rt, steps + 5)
                steps += 5
                if n == 0:
                    dve.tensor_tensor(cls_share, c_("classes_before").unsqueeze(2).to_broadcast([P, NT - 1, E]),
                                      chosen[:, 0:1].to_broadcast([P, NT - 1, E]), ALU.mult).then_inc(s_rt, 1)
                    steps += 1
                dve.wait_ge(s_ex, rank(n) + 1)
                dve.tensor_reduce(denom[:, s], expo[:, s], AX.X, ALU.add).then_inc(s_rt, 1)
                steps += 1
                dve.wait_ge(s_rt, steps)
                dve.reciprocal(prob[:, s], denom[:, s]).then_inc(s_rt, 1)
                steps += 1
                dve.wait_ge(s_rt, steps)

            def as_class(n):
                nonlocal steps
                s = span(n)
                dve.tensor_tensor(chosen_count[:, s], chosen[:, s], chosen[:, 0:1].to_broadcast([P, NB, E]), ALU.mult
                                  ).then_inc(s_rt, 1)
                dve.wait_ge(s_rt, steps + 1)
                dve.tensor_reduce(as_cls[:, s], chosen_count[:, s], AX.X, ALU.add).then_inc(s_ac, 1)
                steps += 1

            def gates(n):
                nonlocal steps
                s = span(n)
                dve.wait_ge(s_cnt, rank(n) + 1)
                dve.tensor_tensor(
                    counts[:, s], ps[:, LG_BANK, CNT0:CNT0 + NB * PAD].rearrange("p (k e) -> p k e", e=PAD)[:, :, 0:E],
                    cls_share[:, (n - 1) * NB:n * NB], ALU.add).then_inc(s_rt, 1)
                dve.wait_ge(s_rt, steps + 1)
                dve.tensor_tensor(counts[:, s], counts[:, s], chosen[:, s], ALU.mult).then_inc(s_rt, 1)
                dve.wait_ge(s_rt, steps + 2)
                dve.tensor_reduce(place[:, s], counts[:, s], AX.X, ALU.add).then_inc(s_rt, 1)
                dve.wait_ge(s_rt, steps + 3)
                steps += 3
                split(s)

            def split(s):
                nonlocal steps
                dve.scalar_tensor_tensor(out=p_keep[:, s], in0=place[:, s], scalar=float(CAP), in1=prob[:, s],
                                         op0=ALU.is_lt, op1=ALU.mult).then_inc(s_rt, 1)
                dve.wait_ge(s_rt, steps + 1)
                steps += 1
                dve.tensor_tensor(p_drop[:, s], prob[:, s], p_keep[:, s], ALU.subtract).then_inc(s_gate, 1)

            def later_groups(t):
                for g in range(1, EG):
                    dve.wait_ge(s_e, EG * rank(t) + g + 1)
                    if g == 1:
                        dve.wait_ge(s_p0, rank(t) + 1)
                    else:
                        dve.wait_ge(s_pk, (EG - 1) * rank(t) + g - 1)
                    dve.copy_predicated(
                        picked[:, t % SEL], chosen[:, t, g * EG:(g + 1) * EG].bitcast(I32).unsqueeze(2).to_broadcast([P, EG, HID]),
                        ps[:, g, :].rearrange("p (e f) -> p e f", e=EG)).then_inc(s_pk, 1)

            def add_bias(n):
                dve.wait_ge(s_bi, n + 1)
                dve.wait_ge(s_tot, tile0(n) + tiles(n) if n else rank(0) + 1)
                dve.tensor_tensor(total[:, span(n)], total[:, span(n)],
                                  ps[:, BI_BANK, 0:tiles(n) * HID].rearrange("p (k f) -> p k f", f=HID), ALU.add
                                  ).then_inc(s_bt, 1)

            def store_seen():
                dve.wait_ge(s_cs, 1)
                dve.tensor_copy(cls_seen[0:NT - 1], ps[0:NT - 1, OHT_BANK, P:P + 2]).then_inc(s_cv2, 1)

            def class_gates():
                nonlocal steps
                dve.wait_ge(s_cc, 1)
                dve.tensor_tensor(place[:, 0:1], ps[:, OHT_BANK, P + 4:P + 5], c_("row"), ALU.add).then_inc(s_rt, 1)
                dve.wait_ge(s_rt, steps + 1)
                steps += 1
                split(slice(0, 1))

            def finish_last(k):
                t = tile0(NG) + k
                dve.wait_ge(s_tot, t + 1)
                if k == 0:
                    dve.wait_ge(s_bi, NG + 1)
                    dve.wait_ge(s_g, NG)
                dve.tensor_tensor(total[:, t], total[:, t], ps[:, BI_BANK, k * HID:(k + 1) * HID], ALU.add
                                  ).then_inc(s_last, 1)
                dve.wait_ge(s_last, k + 1)
                dve.scalar_tensor_tensor(out=h_tiles(NG)[:, k], in0=total[:, t], scalar=p_keep[:, t:t + 1],
                                         in1=gated[:, t], op0=ALU.mult, op1=ALU.add).then_inc(s_lf, 1)

            def normed_by_vector():
                dve.wait_ge(s_norm, 1)
                for k in range(2, NB):
                    t = tile0(1) + k
                    ins = dve.tensor_scalar(xf[:, t], h_tiles(1)[:, k], rs2[:, t:t + 1], shift2[:, t:t + 1], ALU.mult, ALU.add)
                ins.then_inc(s_xv, 1)

            statistics(1)
            statistics(0)
            second_scales(0)
            normed_by_vector()
            statistics(2)
            statistics(3)
            low_parts(1)
            low_parts(0)
            choose(1)
            choose(0)
            as_class(1)
            second_scales(1)
            for n in range(1, NG + 1):
                for k in range(NB):
                    later_groups(tile0(n) + k)
                    if n == 1:
                        if k == 0:
                            gates(1)
                            later_groups(0)
                        else:
                            for m in {1: (4,), 2: (5, 6), 3: (7, 8)}[k]:
                                statistics(m)
                    if n < NG:
                        if k == 0:
                            low_parts(n + 1)
                            if n > 1:
                                add_bias(n - 1)
                        if k == 1:
                            choose(n + 1)
                            as_class(n + 1)
                            if n == 1:
                                add_bias(0)
                            if n == 2:
                                second_scales(2)
                        if k == 3:
                            gates(n + 1)
                    else:
                        if k == 0:
                            store_seen()
                            add_bias(n - 1)
                        if k == 1:
                            class_gates()
                        if k:
                            finish_last(k - 1)
            finish_last(NB - 1)

        def experts_tensor(pe):
            def turn(n):
                pe.wait_ge(s_xf, rank(n) + 1)
                if n >= 2:
                    pe.wait_ge(s_eh, rank(n))
                    pe.wait_ge(s_el, rank(n))
                for k in range(tiles(n)):
                    if n == 1 and k == 2:
                        pe.wait_ge(s_xv, 1)
                    ins = pe.transpose(turned(n)[:, k * P:(k + 1) * P], xf[:, tile0(n) + k], ident)
                ins.then_inc(s_tr, 1)

            def logits(n):
                pe.wait_ge(s_eh, rank(n) + 1)
                pe.wait_ge(s_el, rank(n) + 1)
                if n >= 2:
                    pe.wait_ge(s_gate, n - 1)
                a = E * HID
                for k in range(tiles(n)):
                    x_h, x_l = (ring_of(q, n, k, k + 1) for q in (ring_hi, ring_lo))
                    o = ps[:, lg_bank(n), k * E:(k + 1) * E]
                    pe.matmul(o, x_h, w_hi[:, a:a + E], start=True, stop=False)
                    pe.matmul(o, x_h, w_lo[:, a:a + E], start=False, stop=False)
                    ins = pe.matmul(o, x_l, w_hi[:, a:a + E], start=False, stop=True)
                ins.then_inc(s_lg, 1)

            turned_in = ps[:, OHT_BANK, 0:HV].bitcast(BF16)

            def count(n):
                pe.wait_ge(s_oh, rank(n) + 1)
                if rank(n):
                    pe.wait_ge(s_oht, rank(n))
                w = tiles(n) * PAD
                ins = pe.transpose(turned_in[0:w], chosen_bf[:, span(n)].rearrange("p k e -> p (k e)"), ident_bf)
                if n:
                    cnt = lambda k: ps[:, LG_BANK, CNT0 + k * PAD:CNT0 + NB * PAD]
                    pe.matmul(cnt(0), before_bf, chosen_bf[:, span(n)].rearrange("p k e -> p (k e)"), start=True, stop=False,
                              skip_group_check=True)
                    if n > 1:
                        pe.wait_ge(s_sum, 3 * (n - 1))
                        pe.matmul(cnt(0).rearrange("p (k e) -> p k e", e=PAD), ones_bf,
                                  sum_before[:, n:n + 1].to_broadcast([P, NB, PAD]), start=False, stop=False,
                                  skip_group_check=True)
                    for k in range(NB - 1):
                        ins = pe.matmul(cnt(k + 1).rearrange("p (k e) -> p k e", e=PAD), ones_bf,
                                        chosen_bf[:, tile0(n) + k:tile0(n) + k + 1].to_broadcast([P, NB - 1 - k, PAD]),
                                        start=False, stop=(k == NB - 2), skip_group_check=True)
                ins.then_inc(s_cnt, 1)

            def bias(n):
                pe.wait_ge(s_oht, rank(n) + 1)
                if n:
                    pe.wait_ge(s_bt, n)
                w, f = tiles(n) * PAD, tiles(n) * HID
                for k in range(3):
                    ins = pe.matmul(ps[:, BI_BANK, 0:f], chosen_t[0:w, n], eb[0:w, k, 0:f], start=(k == 0), stop=(k == 2))
                ins.then_inc(s_bi, 1)

            def experts(n, k):
                t = tile0(n) + k
                r = rank(t)
                x_h, x_l = (ring_of(q, n, k, k + 1) for q in (ring_hi, ring_lo))
                for g in range(EG):
                    if r:
                        if g == 0:
                            pe.wait_ge(s_p0, r)
                        else:
                            pe.wait_ge(s_pk, (EG - 1) * (r - 1) + g)
                    o, a = ps[:, g, :], g * EG * HID
                    pe.matmul(o, x_h, w_hi[:, a:a + EG * HID], start=True, stop=False)
                    pe.matmul(o, x_h, w_lo[:, a:a + EG * HID], start=False, stop=False)
                    pe.matmul(o, x_l, w_hi[:, a:a + EG * HID], start=False, stop=True).then_inc(s_e, 1)

            def class_seen():
                pe.wait_ge(s_ac, NG)
                pe.wait_ge(s_oht, NG + 1)
                pe.matmul(ps[0:NT - 1, OHT_BANK, P:P + 2], as_cls[:, 1:NT], c_("image_half"), start=True, stop=True
                          ).then_inc(s_cs, 1)

            def class_counts():
                pe.wait_ge(s_cv2, 1)
                for k, name in enumerate(("even_before", "odd_before")):
                    ins = pe.matmul(ps[:, OHT_BANK, P + 4:P + 5], c_(name)[0:NT - 1], cls_seen[0:NT - 1, k:k + 1],
                                    start=(k == 0), stop=(k == 1))
                ins.then_inc(s_cc, 1)

            pe.wait_ge(s_y, ST * NS8)
            turn(1)
            turn(0)
            logits(1)
            logits(0)
            pe.wait_ge(s_con, 3)
            for n in range(1, NG + 1):
                for k in range(NB):
                    experts(n, k)
                    if n == 1 and k == 0:
                        count(1)
                        experts(0, 0)
                        count(0)
                    if k == 0 and n < NG:
                        turn(n + 1)
                    if k == 1:
                        if n < NG:
                            logits(n + 1)
                        if n == 1:
                            pe.wait_ge(s_eb, 6)
                            bias(0)
                        else:
                            bias(n)
                    if k == 2:
                        if n == 1:
                            bias(1)
                        if n < NG:
                            count(n + 1)
                    if k == 0 and n == NG:
                        class_seen()
                    if k == 1 and n == NG:
                        class_counts()

        def lg_bank(n):
            return LG_BANK if n else BI_BANK

        turned_bf = ps[:, OHT_BANK, 0:HV].bitcast(BF16)

        @block.sync
        def _(sp):
            sp.dma_start(con[:], consts).then_inc(s_const, 16)
            sp.dma_start(w_raw, tok_w).then_inc(s_wraw, 16)
            load_images(sp, 0, 0)
            sp.wait_ge(s_prep, V_FC)
            sp.wait_ge(s_prep_a, A_FB)
            with nc.allow_non_contiguous_dma(reason="padded filter rows of 16 channels"):
                sp.dma_start(toep_rows.rearrange("i a q r k c -> (i a q) (r k c)")[:, 0:(TOK - 1) * 3 * CQ], f_zero
                             ).then_inc(s_rows, 16)
                for i in range(ST):
                    sp.dma_start(
                        toep_rows[i, :, :, TOK - 1:2 * TOK - 1].rearrange("a q r k c -> r (a q) (k c)"),
                        f_parts[:, i * 2 * NQ:(i + 1) * 2 * NQ].rearrange("p n k c -> p n (k c)")).then_inc(s_rows, 16)
            sp.wait_ge(s_prep_t, T_F0)
            sp.wait_ge(s_wt_lo, NCK)
            sp.wait_ge(s_rows, 16 * (1 + ST))
            load_images(sp, 1, 1)
            sp.dma_start(ew_raw.rearrange("p (e d) -> p e d", e=E), expert_w.rearrange("e f d -> f e d")).then_inc(s_exp, 16)
            sp.dma_start(sw_raw, switch_w).then_inc(s_exp, 16)
            sp.dma_start(stat[:, 64:64 + E], bass.AP(switch_b.tensor, offset=switch_b.offset, ap=[[0, P], [1, E]])
                         ).then_inc(s_exp, 16)
            with sp.Fori(1, NG // 2) as i:
                for u in range(2):
                    sp.wait_ge(s_lo, (i * 2 + u - 1) * NCK)
                    load_images(sp, i * 2 + u, u)
            used = (RHO - 1) * 3 * CQ
            sp.dma_start(
                toep_copies.rearrange("i a q z r k c -> (i a q) z (r k c)")[:, :, 0:used],
                toep_rows.rearrange("i a q r k c -> (i a q) (r k c)")[:, 0:used].unsqueeze(1).to_broadcast(
                    [ST * 2 * NQ, COPIES, used])).then_inc(s_copies, 16)
            sp.wait_ge(s_copies, 16)
            sp.wait_ge(s_tz, 2 * NQ - 1)
            for pair, half in ((0, 0), (0, 1), (1, 0)):
                load_toeplitz(sp, 0, pair, half)
            sp.wait_ge(s_yc, 2)
            load_toeplitz(sp, 0, 1, 1)
            for i in range(1, ST):
                for pair in range(2):
                    sp.wait_ge(s_cv, NS8 * (i - 1) + 4 * pair + 4)
                    for half in range(2):
                        load_toeplitz(sp, i, pair, half)
            experts_sync(sp)

        @block.gpsimd
        def _(pool):
            pool.memset(w_lo[HV:P, 0:WP0].bitcast(F32), 0.0).then_inc(s_zero, 1)
            for ring in (ring_hi, ring_lo):
                for r in range(2):
                    pool.memset(ring[HV:P, r].bitcast(F32), 0.0).then_inc(s_zero, 1)
            def zero_slot(q, half):
                other = 1 - half
                pool.memset(toep[half * TOK:(half + 1) * TOK, q, other * TOK * 3 * CQ:(other + 1) * TOK * 3 * CQ
                                 ].bitcast(F32), 0.0).then_inc(s_tz, 1)

            pool.wait_ge(s_zero, 6)
            pool.wait_ge(s_lo, (NG - 1) * NCK)
            for half in (1, 0):
                for q in range(NQ if half else NQ - 1):
                    zero_slot(q, half)
            pool.wait_ge(s_tz, 2 * NQ - 1)
            for n in range(NG + 1):
                src = tokens_of(n)
                w = src.shape[1]
                pool.wait_ge(s_n_hi, n + 1)
                pool.tensor_tensor(ring_lo[:, n % 2, 0:w], src, ring_hi[:, n % 2, 0:w].bitcast(F32), ALU.subtract
                                   ).then_inc(s_n_lo, 1)
                if n == 4:
                    work = pool_carry(pool)
                if n >= 4:
                    pool.wait_ge(s_n_lo, n + 1)
                    for _ in range(3):
                        next(work, None)
            pool_parts_c(pool, 0, 2)
            pool.wait_ge(s_yc, 2)
            zero_slot(NQ - 1, 0)
            pool.wait_ge(s_tz, 2 * NQ)
            pool_parts_c(pool, 2, ST * NS8)
            experts_pool(pool)

        @block.scalar
        def _(act):
            for dst, src in ((fp_t, filt_pos_t), (wp_raw, w_proj.rearrange("w v s -> w (v s)")),
                             (wf_raw, w_filt.rearrange("w v s -> w (v s)")), (pos_raw, pos_embed[1:SEQ]),
                             (b_col, tok_b.rearrange("(p o) -> p o", o=1)),
                             (ct_col, class_token.rearrange("o p -> p o")),
                             (p0_col, pos_embed[0:1].rearrange("o p -> p o"))):
                act.dma_start(dst, src).then_inc(s_small, 16)

            act.wait_ge(s_prep, V_EPS)
            act.activation(cols[:, 5:6], eps_col, ACT.Sqrt)
            act.wait_ge(s_zero, 6)
            for b in range(NCK):
                act.wait_ge(s_wt, b + 1)
                act.activation(w_hi[0:ROWS, b * GT:(b + 1) * GT], ps[0:ROWS, b % WT_BANKS, :], ACT.Copy
                               ).then_inc(s_wt_hi, 1)

            act.wait_ge(s_prep, V_MID)
            act.activation(w_hi[:, WP0:], wp_mid, ACT.Copy).then_inc(s_prep_a, 1)
            act.wait_ge(s_prep_t, T_F)
            act.activation(f_parts[:, :, 0], f_sums, ACT.Copy).then_inc(s_prep_a, 1)
            act.wait_ge(s_prep, V_FREST)
            act.activation(f_parts[:, :, 1], f_rest_n, ACT.Copy).then_inc(s_prep_a, 1)
            for u in range(2):
                for k in range(NCK):
                    n = u * NCK + k
                    if k == 0:
                        act.wait_ge(s_x[u], X_LOADED)
                    if n >= 2:
                        act.wait_ge(s_hi_used, n - 1)
                        act.wait_ge(s_lo, n - 1)
                    act.activation(hi_chunk[0:ROWS, n % 2], x_chunk[0:ROWS, u, :, k * CK:(k + 1) * CK], ACT.Copy
                                   ).then_inc(s_hi, 1)
            with act.Fori(1, NG // 2) as i:
                for u in range(2):
                    for k in range(NCK):
                        n0 = i * (2 * NCK) + (u * NCK + k)
                        r = (u * NCK + k) % 2
                        if k == 0:
                            act.wait_ge(s_x[u], i * X_LOADED + X_LOADED)
                        act.wait_ge(s_hi_used, n0 - 1)
                        act.wait_ge(s_lo, n0 - 1)
                        act.activation(hi_chunk[0:ROWS, r], x_chunk[0:ROWS, u, :, k * CK:(k + 1) * CK], ACT.Copy
                                       ).then_inc(s_hi, 1)

            for k in range(4):
                act.wait_ge(s_ew_t, k + 1)
                act.wait_ge(s_hi_used, LAST - NCK + k + 1)
                act.wait_ge(s_lo_used, LAST - NCK + k + 1)
                act.activation(w_hi[:, k * GT:(k + 1) * GT], ps[:, EW_BANKS[k], :], ACT.Copy).then_inc(s_ew_hi, 1)
            act.wait_ge(s_lo_used, LAST - NCK + 5)
            act.wait_ge(s_ew_t, 5)
            act.activation(w_hi[:, E * HID:E * HID + E], ps[:, EW_BANKS[3], 0:E], ACT.Copy).then_inc(s_ew_hi, 1)

            act.wait_ge(s_hi_used, LAST)
            act.wait_ge(s_lo_used, LAST)

            def high(n):
                src = tokens_of(n)
                if n >= 2:
                    act.wait_ge(s_n_pr, 1 if n == 2 else (n - 2) * NB + 1)
                act.activation(ring_hi[:, n % 2, 0:src.shape[1]], src, ACT.Copy).then_inc(s_n_hi, 1)

            def by_row(n):
                src = tokens_of(n)
                act.wait_ge(s_n_tr, n + 1)
                act.wait_ge(s_n_lo, n + 1)
                act.activation(src, ps[:, TR_BANKS[n % 2], 0:src.shape[1]], ACT.Copy).then_inc(s_n_nat, 1)

            def deviations(n):
                act.wait_ge(s_n_var, n + 1)
                nt = tokens_of(n).shape[1] // P
                k = NB if n == 0 else 0
                act.activation(std[:, k:k + nt], mv[:, k:k + nt, 1], ACT.Sqrt, bias=eps_col).then_inc(s_n_std, 1)

            def move(n, k):
                if k == 0:
                    act.wait_ge(s_n_r, n + 1)
                j = (n - 1) * NB + k
                act.wait_ge(s_n_pr, j + 2)
                src = ps[:, PR_BANKS[k], :].rearrange("p (s v) -> p s v", s=4)
                sc = rs[:, n % 2, k:k + 1]
                for par in range(2):
                    rows = slice(par * TOK, (par + 1) * TOK)
                    for half in range(2):
                        act.activation(xs_q[half * HV:(half + 1) * HV, :, :, 2 * j + par:2 * j + par + 1],
                                       src[rows, 0:ST, half * HV:(half + 1) * HV].unsqueeze(3), ACT.Copy, scale=sc[rows])
                act.activation(x3[:, j:j + 1, :], src[:, ST:ST + 1, :], ACT.Copy, scale=sc).then_inc(s_n_pa, 1)

            act.wait_ge(s_prep, V_CLS)
            high(0)
            act.wait_ge(s_tok, NG)
            high(1)
            by_row(0)
            by_row(1)
            deviations(0)
            deviations(1)
            high(2)
            for n in range(1, NG + 1):
                move(n, 0)
                if n < NG:
                    by_row(n + 1)
                move(n, 2)
                if n + 2 <= NG:
                    high(n + 2)
                if n < NG:
                    deviations(n + 1)
                if not by_vector(n, 3):
                    move(n, 3)

            act.wait_ge(s_n_pv, moved(NG, NB)[0])
            act.wait_ge(s_n_pa, moved(NG, NB)[1])
            for st in range(ST):
                for g in range(NS8 + 1):
                    n = st * NS8 + g
                    if g < NS8:
                        if st:
                            act.wait_ge(s_y, n - NS8 + 1)
                        elif g == 0:
                            act.wait_ge(s_cls_p, 10)
                        if n >= PARTS:
                            act.wait_ge(s_cv, n - PARTS + 1)
                        act.activation(parts[:, 0, n % PARTS], xs_m[:, n], ACT.Copy).then_inc(s_ya, 1)
                    if g:
                        act.wait_ge(s_yr, n)
                        act.activation(parts[:, 1, (n - 1) % PARTS], xs_m[:, n - 1], ACT.Copy).then_inc(s_yb, 1)
            experts_scalar(act)

        @block.vector
        def _(dve):
            def prep(ins):
                ins.then_inc(s_prep, 1)

            prep(dve.memset(eps_col, EPS))
            dve.memset(w_hi[HV:P, 0:WP0].bitcast(F32), 0.0).then_inc(s_zero, 1)
            prep(dve.memset(mean_w, 1.0 / HID))
            prep(dve.memset(f_zero, 0.0))
            dve.wait_ge(s_zero, 6)
            for b in range(NCK):
                dve.wait_ge(s_wt_hi, b + 1)
                dve.tensor_tensor(w_lo[0:ROWS, b * GT:(b + 1) * GT], ps[0:ROWS, b % WT_BANKS, :],
                                  w_hi[0:ROWS, b * GT:(b + 1) * GT].bitcast(F32), ALU.subtract).then_inc(s_wt_lo, 1)
            dve.wait_ge(s_small, 16 * N_SMALL)
            dve.wait_ge(s_const, 16)
            prep(dve.tensor_copy(select[:], c_("select")))
            prep(dve.tensor_tensor(hc_col, ct_col, p0_col, ALU.mult))
            two = wf_two.rearrange("p (i a d v) -> p i a d v", i=ST, a=2, d=2)
            for i in range(ST):
                for d in range(2):
                    prep(dve.tensor_copy(two[:, i, :, d], f_view[:, i].rearrange("p (a v) -> p a v", a=2)))
            prep(dve.tensor_copy(fp0, fp_t[:, 0:1].to_broadcast([P, P])))
            dve.wait_ge(s_prep, V_HC)
            prep(dve.tensor_copy(h_cls, hc_col.to_broadcast([P, P])))
            dve.wait_ge(s_prep_t, T_POS)
            prep(dve.tensor_copy(pos_t[:], ps[:, POS_BANK, 0:TOK]))
            dve.wait_ge(s_prep_t, T_MEAN)
            prep(dve.tensor_tensor(
                wp_mid.rearrange("p (s v) -> p s v", s=4), wp_raw.rearrange("p (v s) -> p s v", s=4),
                ps[:, MEAN_BANK, :].rearrange("p (v s) -> p s v", s=4), ALU.subtract))
            dve.wait_ge(s_prep, V_MID)
            dve.wait_ge(s_prep_a, A_WPHI)
            prep(dve.tensor_tensor(w_lo[:, WP0:], wp_mid, w_hi[:, WP0:].bitcast(F32), ALU.subtract))
            dve.wait_ge(s_prep_a, A_FA)
            prep(dve.tensor_tensor(f_rest_n, f_sums, f_parts[:, :, 0], ALU.subtract))
            dve.wait_ge(s_prep_a, A_FB)
            dve.wait_ge(s_prep, V_FREST)
            prep(dve.tensor_tensor(f_parts[:, :, 2], f_rest_n, f_parts[:, :, 1], ALU.subtract))
            def low(u, k):
                r = (u * NCK + k) % 2
                dve.tensor_tensor(lo_chunk[0:ROWS, r], x_chunk[0:ROWS, u, :, k * CK:(k + 1) * CK],
                                  hi_chunk[0:ROWS, r].bitcast(F32), ALU.subtract).then_inc(s_lo, 1)

            def tokens(g, bank):
                dve.wait_ge(s_lo_used, g * NCK + NCK)
                dve.scalar_tensor_tensor(
                    out=h_b[:, g].rearrange("p (b t) -> p b t", b=GI), in0=ps[:, bank, :].rearrange("p (b t) -> p b t", b=GI),
                    scalar=b_col, in1=pos_t[:].unsqueeze(1).to_broadcast([P, GI, TOK]),
                    op0=ALU.add, op1=ALU.mult).then_inc(s_tok, 1)

            dve.wait_ge(s_prep, V_POS)
            for u in range(2):
                for k in range(NCK):
                    n = u * NCK + k
                    dve.wait_ge(s_hi, n + 1)
                    if n >= 2:
                        dve.wait_ge(s_lo_used, n - 1)
                    low(u, k)
                    if u and k == 1:
                        tokens(0, 0)
            with dve.Fori(1, NG // 2) as i:
                for u in range(2):
                    for k in range(NCK):
                        n = i * (2 * NCK) + (u * NCK + k)
                        dve.wait_ge(s_hi, n + 1)
                        dve.wait_ge(s_lo_used, n - 1)
                        low(u, k)
                        if k == 1:
                            tokens(i * 2 + (u - 1), 1 - u)

            for k in range(5):
                dve.wait_ge(s_ew_hi, k + 1)
                a, w, bank = (k * GT, GT, EW_BANKS[k]) if k < 4 else (E * HID, E, EW_BANKS[3])
                dve.tensor_tensor(w_lo[:, a:a + w], ps[:, bank, 0:w], w_hi[:, a:a + w].bitcast(F32), ALU.subtract
                                  ).then_inc(s_ew_lo, 1)
                if k == 3:
                    tokens(NG - 1, 1)

            dv = 0

            def variances(n):
                nonlocal dv
                src = tokens_of(n)
                nt = src.shape[1] // P
                k0 = 0 if n else NB
                dve.wait_ge(s_n_nat, n + 1)
                for k in range(nt):
                    dve.bn_stats(bs[:, k0 + k], src[:, k * P:(k + 1) * P]).then_inc(s_dv, 1)
                dv += nt
                dve.wait_ge(s_dv, dv)
                for k in range(nt):
                    ins = dve.bn_aggr(mv[:, k0 + k], bs[:, k0 + k])
                ins.then_inc(s_n_var, 1)

            def scales(n):
                nonlocal dv
                nt = tokens_of(n).shape[1] // P
                k = slice(0, nt) if n else slice(NB, NB + 1)
                r_ = rs[:, n % 2, 0:nt]
                dve.wait_ge(s_n_var, n + 1)
                dve.wait_ge(s_n_std, n + 1)
                dve.reciprocal(r_, std[:, k]).then_inc(s_dv, 1)
                dve.wait_ge(s_dv, dv + 1)
                dve.scalar_tensor_tensor(out=tt[:, k], in0=mv[:, k, 1], scalar=EPS, in1=r_,
                                         op0=ALU.add, op1=ALU.mult).then_inc(s_dv, 1)
                dve.wait_ge(s_dv, dv + 2)
                dve.scalar_tensor_tensor(out=tt[:, k], in0=tt[:, k], scalar=-0.5, in1=r_,
                                         op0=ALU.mult, op1=ALU.mult).then_inc(s_dv, 1)
                dve.wait_ge(s_dv, dv + 3)
                dv += 3
                dve.scalar_tensor_tensor(out=r_, in0=tt[:, k], scalar=1.5, in1=r_,
                                         op0=ALU.add, op1=ALU.mult).then_inc(s_n_r, 1)
                dve.wait_ge(s_n_r, n + 1)

            def move(n, k):
                j = (n - 1) * NB + k
                dve.wait_ge(s_n_pr, j + 2)
                src = ps[:, PR_BANKS[k], :].rearrange("p (s v) -> p s v", s=4)
                sc = rs[:, n % 2, k:k + 1]
                for par in range(2):
                    rows = slice(par * TOK, (par + 1) * TOK)
                    for half in range(2):
                        dve.tensor_scalar(xs_q[half * HV:(half + 1) * HV, :, :, 2 * j + par:2 * j + par + 1],
                                          src[rows, 0:ST, half * HV:(half + 1) * HV].unsqueeze(3), sc[rows], None, ALU.mult)
                dve.tensor_scalar(x3[:, j:j + 1, :], src[:, ST:ST + 1, :], sc, None, ALU.mult).then_inc(s_n_pv, 1)

            variances(0)
            variances(1)
            scales(0)
            scales(1)
            dve.wait_ge(s_n_pr, 1)
            dve.tensor_scalar(cls_x.rearrange("p s v -> p (s v)"), ps[:, CLS_BANK, :], rs[:, 0, 0:1], None, ALU.mult
                              ).then_inc(s_n_pv, 1)
            for n in range(1, NG + 1):
                move(n, 1)
                if n < NG:
                    variances(n + 1)
                if by_vector(n, 3):
                    move(n, 3)
                if n < NG:
                    scales(n + 1)
                if n == 1:
                    dve.wait_ge(s_n_pv, 1)
                    y = cls_x[:, 0]
                    for i in range(ST):
                        dve.tensor_tensor(cls_t, y, ps[:, F0_BANK, i * HID:(i + 1) * HID], ALU.mult).then_inc(s_cls, 1)
                        dve.wait_ge(s_cls, 2 * i + 1)
                        to = x3[:, NT - 1] if i == ST - 1 else cls_y[:, i + 1]
                        dve.tensor_tensor(to, cls_t, cls_x[:, i + 1], ALU.mult).then_inc(s_cls, 1)
                        dve.wait_ge(s_cls, 2 * i + 2)
                        y = to
                    for i in range(ST):
                        src = (cls_x[:, 0] if i == 0 else cls_y[:, i]).rearrange("p (a v) -> p a v", a=2)
                        dve.tensor_copy(cls_two[:, i], src.unsqueeze(2).to_broadcast([P, 2, 2, HV])).then_inc(s_cls, 1)
                if n == 2:
                    dve.wait_ge(s_cls_t, 1)
                    dve.tensor_copy(cls_col, ps[:, F0_BANK, ST * HID:ST * HID + 6]).then_inc(s_cls, 1)
                    dve.wait_ge(s_cls, 10)
                    for i in range(ST):
                        for a in range(2):
                            dve.tensor_scalar(cls_f[:, i, a * TOK:(a + 1) * TOK],
                                              ps[:, FT_BANK, (2 * i + a) * TOK:(2 * i + a + 1) * TOK],
                                              cls_col[:, 2 * i + a:2 * i + a + 1], None, ALU.mult).then_inc(s_cls, 1)

            x3_q = x3[:, 0:NT - 1].rearrange("p j v -> p v j")

            def rest(n):
                if n >= NS8:
                    dve.wait_ge(s_y, n - NS8 + 1)
                dve.wait_ge(s_ya, n + 1)
                dve.tensor_tensor(xs_m[:, n], xs_m[:, n], parts[:, 0, n % PARTS], ALU.subtract).then_inc(s_yr, 1)

            def multiply(n):
                g = n % NS8
                dve.wait_ge(s_cv, n + 1)
                if n < (ST - 1) * NS8:
                    m = n + NS8
                    dve.tensor_tensor(xs_m[:, m], ps[:, g, :], xs_m[:, m], ALU.mult).then_inc(s_y, 1)
                    return
                src = ps[:, g, :].rearrange("p (v j u) -> p v j u", v=G8, u=2)
                for half in range(2):
                    for par in range(2):
                        to = x3_q[par * TOK:(par + 1) * TOK, half * HV + g * G8:half * HV + (g + 1) * G8]
                        ins = dve.tensor_tensor(to, src[half * HV:(half + 1) * HV, :, :, par], to, ALU.mult)
                ins.then_inc(s_y, 1)

            dve.wait_ge(s_n_pv, moved(NG, NB)[0])
            dve.wait_ge(s_n_pa, moved(NG, NB)[1])
            for n in range(PARTS):
                rest(n)
            for n in range(ST * NS8):
                multiply(n)
                if n + PARTS < ST * NS8:
                    rest(n + PARTS)
            experts_vector(dve)

        @block.tensor
        def _(pe):
            pe.wait_ge(s_const, 16)
            pe.wait_ge(s_wraw, 16)
            for b in range(NCK):
                if b >= WT_BANKS:
                    pe.wait_ge(s_wt_lo, b - WT_BANKS + 1)
                for k in range(CK):
                    ins = pe.transpose(ps[0:ROWS, b % WT_BANKS, k * HID:(k + 1) * HID], w_view[:, :, b * CK + k], ident)
                ins.then_inc(s_wt, 1)
            pe.wait_ge(s_small, 16 * N_SMALL)
            pe.transpose(ps[:, POS_BANK, 0:TOK], pos_raw, ident[0:TOK, 0:TOK]).then_inc(s_prep_t, 1)
            pe.wait_ge(s_prep, V_MEAN)
            pe.matmul(ps[:, MEAN_BANK, :], mean_w, wp_raw, start=True, stop=True).then_inc(s_prep_t, 1)
            pe.matmul(ps[0:TOK, F_BANK, 0:ST * HID], fp_t[:, 0:TOK], f_view, start=True, stop=True).then_inc(s_prep_t, 1)
            pe.wait_ge(s_prep, V_FP0)
            for k in range(2 * ST):
                ins = pe.matmul(ps[:, FT_BANK, k * TOK:(k + 1) * TOK], wf_two[:, k * P:(k + 1) * P], fp_t[:, 1:SEQ],
                                start=True, stop=True)
            ins.then_inc(s_prep_t, 1)
            pe.matmul(ps[:, F0_BANK, 0:ST * HID], fp0, f_view, start=True, stop=True).then_inc(s_prep_t, 1)

            pe.wait_ge(s_wt_lo, NCK)
            pe.wait_ge(s_wt_hi, NCK)
            def two_groups(i):
                for u in range(2):
                    for k in range(NCK):
                        r = (u * NCK + k) % 2
                        n = i * (2 * NCK) + (u * NCK + k)
                        pe.wait_ge(s_hi, n + 1)
                        for j in range(CK):
                            for w in (w_hi, w_lo):
                                a = (k * CK + j) * HID
                                ins = pe.matmul(ps[:, u, :], w[:, a:a + HID], ring_hi[:, r, j * GT:(j + 1) * GT],
                                                start=(k == 0 and j == 0 and w is w_hi), stop=False)
                        ins.then_inc(s_hi_used, 1)
                        pe.wait_ge(s_lo, n + 1)
                        for j in range(CK):
                            a = (k * CK + j) * HID
                            ins = pe.matmul(ps[:, u, :], w_hi[:, a:a + HID], ring_lo[:, r, j * GT:(j + 1) * GT],
                                            start=False, stop=(k == NCK - 1 and j == CK - 1))
                        ins.then_inc(s_lo_used, 1)

            with pe.Fori(0, NG // 2 - 1) as i:
                two_groups(i)
            pe.wait_ge(s_exp, 48)
            pe.wait_ge(s_prep, V_MID)
            pe.wait_ge(s_prep_a, A_FB)
            for k in range(4):
                for j in range(EG):
                    e = k * EG + j
                    ins = pe.transpose(ps[:, EW_BANKS[k], j * HID:(j + 1) * HID], ew_raw[:, e * HID:(e + 1) * HID], ident)
                ins.then_inc(s_ew_t, 1)
            two_groups(NG // 2 - 1)
            pe.wait_ge(s_ew_lo, 4)
            pe.transpose(ps[:, EW_BANKS[3], 0:E], sw_raw, ident[0:E, 0:E]).then_inc(s_ew_t, 1)

            def turn(n):
                src = tokens_of(n)
                if n >= 2:
                    pe.wait_ge(s_n_nat, n - 1)
                for k in range(src.shape[1] // P):
                    ins = pe.transpose(ps[:, TR_BANKS[n % 2], k * P:(k + 1) * P], src[:, k * P:(k + 1) * P], ident)
                ins.then_inc(s_n_tr, 1)

            def project(n, k):
                x_h, x_l = (q[:, n % 2, k * P:(k + 1) * P] for q in (ring_hi, ring_lo))
                out_ = ps[:, PR_BANKS[k] if n else CLS_BANK, :]
                pe.matmul(out_, x_h, w_hi[:, WP0:], start=True, stop=False)
                pe.matmul(out_, x_h, w_lo[:, WP0:], start=False, stop=False)
                pe.matmul(out_, x_l, w_hi[:, WP0:], start=False, stop=True).then_inc(s_n_pr, 1)

            pe.wait_ge(s_prep, V_WPLO)
            turn(0)
            turn(1)
            pe.wait_ge(s_n_hi, 1)
            pe.wait_ge(s_n_lo, 1)
            pe.wait_ge(s_ew_lo, 5)
            project(0, 0)
            pe.wait_ge(s_tok, NG)
            for n in range(1, NG + 1):
                if n < NG:
                    turn(n + 1)
                pe.wait_ge(s_n_hi, n + 1)
                pe.wait_ge(s_n_lo, n + 1)
                for k in range(NB):
                    if n > 1:
                        pe.wait_ge(*((s_n_pv, moved(n - 1, k + 1)[0]) if by_vector(n - 1, k) else
                                     (s_n_pa, moved(n - 1, k + 1)[1])))
                    elif PR_BANKS[k] == CLS_BANK:
                        pe.wait_ge(s_n_pv, 1)
                    project(n, k)
                if n == 2:
                    pe.wait_ge(s_cls, 9)
                    for k in range(6):
                        ins = pe.matmul(ps[:, F0_BANK, ST * HID + k:ST * HID + k + 1],
                                        cls_two[:, k // 2, k % 2].rearrange("p d v -> p (d v)"), ident[:, 0:1],
                                        start=True, stop=True)
                    ins.then_inc(s_cls_t, 1)

            pe.wait_ge(s_cls_p, 10)
            pe.wait_ge(s_n_pv, moved(NG, NB)[0])
            pe.wait_ge(s_n_pa, moved(NG, NB)[1])
            pe.wait_ge(s_prep, V_SELECT)
            toep_v = toep.rearrange("p q (t k c) -> p q t k c", k=3, c=CQ)
            with pe.Fori(0, ST) as st:
                for g in range(NS8):
                    q = g // 2
                    if g == 4:
                        pe.wait_ge(s_tz, 2 * NQ)
                    if g % 4 == 0:
                        pe.wait_ge(s_t[g // 4], st * T_LOADED + T_LOADED)
                    pe.wait_ge(s_ya, st * NS8 + (g + 1))
                    b, v0 = g * G8 // VB, g * G8 % VB
                    rows = select[:, v0:v0 + G8].unsqueeze(2).to_broadcast([P, G8, B])
                    bank = ps[:, g, :].rearrange("p (c b) -> p c b", c=G8)
                    pe.matmul(bank, carry[:, bass.ds(st, 1), b, :].rearrange("p o n -> p (o n)"), rows, start=True, stop=False,
                              skip_group_check=True)
                    for j, ready in enumerate((s_ya, s_yb, s_yc)):
                        if j:
                            pe.wait_ge(ready, st * NS8 + (g + 1))
                        for c in range(G8):
                            for k in range(3 - j):
                                ins = pe.matmul(ps[:, g, c * B:(c + 1) * B], toep_v[:, q, :, k, (g % 2) * G8 + c],
                                                parts[:, j, g % PARTS, c * B:(c + 1) * B], start=False,
                                                stop=(c == G8 - 1 and j == 2), skip_group_check=True)
                    ins.then_inc(s_cv, 1)
            experts_tensor(pe)


_INS = ["x", "L0_tok_W", "L0_tok_b", "L0_tok_class_token", "L0_tok_pos_embed", "L0_attn_W_proj", "L0_attn_W_filt",
        "L0_ffn_switch_w", "L0_ffn_switch_b", "L0_ffn_expert_w", "L0_ffn_expert_b"]
_OUTS = [((B, SEQ, HID), "float32")]


def kernel(**inputs):
    import numpy as _np
    import concourse.bacc as _bacc
    from concourse import mybir as _mybir
    from concourse.bass_utils import run_bass_kernel_spmd as _run

    nc = _bacc.Bacc("TRN2", target_bir_lowering=False, num_devices=1)
    arrays, args = {}, []
    given = {name: _np.ascontiguousarray(inputs[name]) for name in _INS}
    given["constants"] = CONSTS
    given["filter_positions"] = positions_t()
    for name, a in given.items():
        arrays[f"in_{name}_dram"] = a
        args.append(nc.dram_tensor(f"in_{name}_dram", a.shape, _mybir.dt.from_np(a.dtype), kind="ExternalInput").ap())
    for i, (shape, dtype) in enumerate(_OUTS):
        args.append(nc.dram_tensor(f"out_{i}_dram", shape, _mybir.dt.from_np(_np.dtype(dtype)), kind="ExternalOutput").ap())
    build(nc, *args)
    r = _run(nc, [arrays], core_ids=[0])
    return r.results[0]["out_0_dram"]
```

```python
from contextlib import ExitStack

import numpy as np

import concourse.bass as bass
from concourse import mybir

P = 128
B, C, IMG, PATCH, HID = 64, 3, 224, 28, 128
NP = IMG // PATCH
TOK = NP * NP
SEQ = TOK + 1
ROWS = C * PATCH
GI = 8
GT = GI * TOK
NG = B // GI
XI = NP * IMG
XG = GI * XI
CK = 4
NCK = PATCH // CK
NB = GT // P
NT = B * TOK // P + 1
ST = 3
HV = HID // 2
VB = 32
CQ = 16
NQ = HV // CQ
G8 = 8
NS8 = HV // G8
PARTS = 4
E = 16
EG = 4
CAP = int(1.2 * (B * SEQ) / E)
EPS = 1e-5
COPIES = 16
RHO = 128

F32 = mybir.dt.float32
F32R = mybir.dt.float32r
BF16 = mybir.dt.bfloat16
I32 = mybir.dt.int32
ALU = mybir.AluOpType
ACT = mybir.ActivationFunctionType
AX = mybir.AxisListType

CONST_COLS = {}


def constants():
    p = np.arange(P)
    parts = [
        ("ident", np.eye(P)),
        ("select", (p[:, None] % VB == np.arange(VB)[None, :])),
        ("before", (p[:, None] < p[None, :])),
        ("image_half", (p[:, None] // TOK == np.arange(2)[None, :])),
        ("even_before", (2 * p[:, None] < p[None, :]) & (p[:, None] < B // 2)),
        ("odd_before", (2 * p[:, None] + 1 < p[None, :]) & (p[:, None] < B // 2)),
        ("priority", np.broadcast_to(E - np.arange(E)[None, :], (P, E))),
        ("classes_before", 2 * np.arange(B // 2)[None, :] + p[:, None] // TOK + 1),
        ("row", p[:, None]),
    ]
    at = 0
    for name, a in parts:
        CONST_COLS[name] = (at, at + a.shape[1])
        at += a.shape[1]
    return np.concatenate([a.astype(np.float32) for _, a in parts], axis=1)


def positions_t():
    half = HID // 2
    freqs = np.power(np.float32(10000.0), -np.arange(half, dtype=np.float32) / np.float32(half)).astype(np.float32)
    phi = np.arange(SEQ, dtype=np.float32)[:, None] * freqs[None, :]
    return np.ascontiguousarray(np.concatenate([np.sin(phi), np.cos(phi)], axis=-1).astype(np.float32).T)


CONSTS = constants()


def build(nc, x, tok_w, tok_b, class_token, pos_embed, w_proj, w_filt, switch_w, switch_b, expert_w, expert_b,
          consts, filt_pos_t, out):
    with ExitStack() as ctx:
        def sb(name, shape, dt=F32):
            return ctx.enter_context(nc.sbuf_tensor(name, shape, dt))

        def sem(name):
            return ctx.enter_context(nc.semaphore(name))

        ps = ctx.enter_context(nc.psum_tensor("ps", [P, 8, 512], F32))

        arena = sb("arena", [P, 2 * XG + E * HID + HID])
        ring_hi = sb("ring_hi", [P, 2, CK * GT], F32R)
        ring_lo = sb("ring_lo", [P, 2, CK * GT], F32R)
        w_hi = sb("w_hi", [P, PATCH * HID + 4 * HID], F32R)
        w_lo = sb("w_lo", [P, PATCH * HID + 4 * HID], F32R)
        h = sb("h", [P, NT * HID])
        con = sb("con", [P, CONSTS.shape[1]])
        pos_t = sb("pos_t", [P, TOK])
        select = sb("select", [P, VB], BF16)
        carry = sb("carry", [P, ST, HV // VB, P], BF16)
        ident_bf, before_bf, ones_bf = (sb(name, [P, P], BF16)[:] for name in ("ident_bf", "before_bf", "ones_bf"))
        cols = sb("cols", [P, 8])
        stat = sb("stat", [P, 176])

        def c_(name):
            a, b = CONST_COLS[name]
            return con[:, a:b]

        ident = c_("ident")
        b_col, ct_col, p0_col, hc_col, eps_col = (cols[:, i:i + 1] for i in range(5))
        WP0 = PATCH * HID

        x_raw = arena[:, 0:2 * XG].rearrange("p (s n) -> p s n", s=2)
        a0 = XG
        w_raw = arena[:, a0:a0 + ROWS * PATCH]; a0 += ROWS * PATCH
        wp_raw = arena[:, a0:a0 + 4 * HID]; a0 += 4 * HID
        wp_mid = arena[:, a0:a0 + 4 * HID]; a0 += 4 * HID
        wf_raw = arena[:, a0:a0 + ST * HID]; a0 += ST * HID
        wf_two = arena[:, a0:a0 + ST * 2 * HID]; a0 += ST * 2 * HID
        fp_t = arena[:, a0:a0 + SEQ]; a0 += SEQ
        fp0 = arena[:, a0:a0 + P]; a0 += P
        mean_w = arena[:, a0:a0 + P]; a0 += P
        pos_raw = arena[0:TOK, a0:a0 + HID]; a0 += HID
        f_rest = arena[0:TOK, a0:a0 + ST * HID]; a0 += ST * HID
        f_parts = arena[0:TOK, a0:a0 + ST * 3 * HID // 2].bitcast(BF16).rearrange("p (n k c) -> p n k c", k=3, c=CQ)
        a0 += ST * 3 * HID // 2
        f_zero = arena[0:ST * 2 * NQ, a0:a0 + (TOK - 1) * 3 * CQ // 2].bitcast(BF16); a0 += (TOK - 1) * 3 * CQ // 2
        assert a0 <= 2 * XG
        ew_raw = arena[:, 2 * XG:2 * XG + E * HID]
        sw_raw = arena[0:E, 2 * XG + E * HID:2 * XG + E * HID + HID]
        TW = 3 * P * CQ
        toep = arena[:, 0:NQ * TW // 2].bitcast(BF16).rearrange("p (q n) -> p q n", q=NQ)
        XO = NQ * TW // 2 - 2 * G8 * B
        xs = arena[:, XO:XO + ST * HV * B]
        xs_q = xs.rearrange("p (s v b) -> p s v b", s=ST, v=HV)
        xs_m = xs.rearrange("p (m n) -> p m n", n=G8 * B)
        X3 = XO + ST * HV * B
        x3 = arena[:, X3:X3 + NT * HID].rearrange("p (j v) -> p j v", v=HID)
        PO = X3 + NT * HID
        parts = arena[:, PO:PO + 3 * PARTS * G8 * B // 2].bitcast(BF16).rearrange("p (k g n) -> p k g n", k=3, g=PARTS)
        assert PO + 3 * PARTS * G8 * B // 2 <= arena.shape[1]
        a0 = PO
        cls_x = arena[:, a0:a0 + 4 * HID].rearrange("p (s v) -> p s v", s=4); a0 += 4 * HID
        cls_y = arena[:, a0:a0 + 3 * HID].rearrange("p (s v) -> p s v", s=3); a0 += 3 * HID
        cls_t = arena[:, a0:a0 + HID]; a0 += HID
        cls_two = arena[:, a0:a0 + ST * 2 * HID].rearrange("p (i a d v) -> p i a d v", i=ST, a=2, d=2)
        a0 += ST * 2 * HID
        cls_col = arena[:, a0:a0 + 6]; a0 += 6
        cls_f = arena[:, a0:a0 + ST * P].rearrange("p (i n) -> p i n", i=ST); a0 += ST * P
        cls_a = arena[:, a0:a0 + ST * P // 2].bitcast(BF16).rearrange("p (i n) -> p i n", i=ST); a0 += ST * P // 2
        assert a0 <= PO + 3 * PARTS * G8 * B // 2

        toep_rows = nc.dram_tensor("toeplitz_rows", [ST, 2, NQ, RHO, 3, CQ], BF16, kind="Internal").ap()

        toep_copies = nc.dram_tensor("toeplitz_copies", [ST, 2, NQ, COPIES, RHO, 3, CQ], BF16, kind="Internal").ap()

        constants_loaded = sem("constants_loaded")
        small_loaded = sem("small_loaded")
        patch_weights_loaded = sem("patch_weights_loaded")
        expert_weights_loaded = sem("expert_weights_loaded")
        images_loaded = [sem("images_loaded_even"), sem("images_loaded_odd")]
        rings_zeroed = sem("rings_zeroed")
        prepared_by_vector = sem("prepared_by_vector")
        prepared_by_scalar = sem("prepared_by_scalar")
        prepared_by_tensor = sem("prepared_by_tensor")
        patch_weights_turned = sem("patch_weights_turned")
        patch_weights_high = sem("patch_weights_high")
        patch_weights_low = sem("patch_weights_low")
        toeplitz_rows_stored = sem("toeplitz_rows_stored")
        toeplitz_copies_stored = sem("toeplitz_copies_stored")
        high_parts_ready = sem("high_parts_ready")
        low_parts_ready = sem("low_parts_ready")
        high_parts_used = sem("high_parts_used")
        low_parts_used = sem("low_parts_used")
        tokens_ready = sem("tokens_ready")
        expert_weights_turned = sem("expert_weights_turned")
        expert_weights_high = sem("expert_weights_high")
        expert_weights_low = sem("expert_weights_low")
        token_high_ready = sem("token_high_ready")
        token_low_ready = sem("token_low_ready")
        tokens_turned = sem("tokens_turned")
        tokens_stored_by_row = sem("tokens_stored_by_row")
        variances_ready = sem("variances_ready")
        deviations_ready = sem("deviations_ready")
        scales_ready = sem("scales_ready")
        projected = sem("projected")
        projections_moved_by_scalar = sem("projections_moved_by_scalar")
        projections_moved_by_vector = sem("projections_moved_by_vector")
        vector_steps = sem("vector_steps")
        class_token_vector = sem("class_token_vector")
        class_token_tensor = sem("class_token_tensor")
        class_token_gpsimd = sem("class_token_gpsimd")
        toeplitz_loaded = [sem(f"toeplitz_loaded_{q}") for q in range(2)]
        toeplitz_blocks_zeroed = sem("toeplitz_blocks_zeroed")
        constants_ready = sem("constants_ready")
        part_a_ready = sem("part_a_ready")
        rest_ready = sem("rest_ready")
        part_b_ready = sem("part_b_ready")
        part_c_ready = sem("part_c_ready")
        convolved = sem("convolved")
        stage_output_ready = sem("stage_output_ready")

        block = ctx.enter_context(nc.Block())

        x_src = x.rearrange("b c (h r) w -> b c r h w", r=PATCH)
        N_SMALL = 7
        V_EPS, V_MEAN, V_FZERO, V_SELECT, V_HC, V_TWO, V_FP0, V_CLS, V_POS, V_MID, V_WPLO, V_FREST, V_FC = (
            1, 2, 3, 4, 5, 11, 12, 13, 14, 15, 16, 17, 18)
        A_WPHI, A_FA, A_FB = 1, 2, 3
        T_POS, T_MEAN, T_F, T_F0 = 1, 2, 3, 5
        WT_BANKS = 3
        MEAN_BANK, F_BANK, FT_BANK, F0_BANK, POS_BANK = 3, 4, 5, 6, 7
        PR_BANKS = [0, 1, 4, 7]
        CLS_BANK = PR_BANKS[3]

        def load_images(eng, g, slot):
            for i in range(GI):
                for c in range(C):
                    eng.dma_start(
                        x_raw[c * PATCH:(c + 1) * PATCH, slot, i * XI:(i + 1) * XI].rearrange("p (h w) -> p h w", h=NP),
                        x_src[g * GI + i, c]).then_inc(images_loaded[slot], 16)

        X_LOADED = GI * C * 16

        def load_toeplitz(eng, i, pair, half):
            for w in range(TOK // COPIES):
                s0 = half * TOK + w * COPIES
                src = toep_copies[i, half, 2 * pair]
                eng.dma_start(
                    toep[s0:s0 + COPIES, 2 * pair:2 * pair + 2, half * TOK * 3 * CQ:(half + 1) * TOK * 3 * CQ],
                    bass.AP(src.tensor, offset=src.offset + (TOK - 1 - w * COPIES) * 3 * CQ,
                            ap=[[(RHO - 1) * 3 * CQ, COPIES], [COPIES * RHO * 3 * CQ, 2], [1, TOK * 3 * CQ]])
                ).then_inc(toeplitz_loaded[pair], 16)

        T_LOADED = 2 * (TOK // COPIES) * 16

        x_chunk = x_raw.rearrange("p s (t j) -> p s t j", j=PATCH)
        hi_chunk = ring_hi[:].rearrange("p r (j t) -> p r t j", j=CK)
        lo_chunk = ring_lo[:].rearrange("p r (j t) -> p r t j", j=CK)
        h_b = h[:, 0:NG * GT].rearrange("p (n t) -> p n t", t=GT)
        h_cls = h[:, NG * GT:]
        f_view = wf_raw.rearrange("p (v i) -> p i v", i=ST)
        f_sums = ps[0:TOK, F_BANK, 0:ST * HID].rearrange("p (n c) -> p n c", c=CQ)
        f_rest_n = f_rest.rearrange("p (n c) -> p n c", c=CQ)
        w_view = w_raw.rearrange("p (r j) -> p r j", j=PATCH)
        TR_BANKS = [2, 3]
        EW_BANKS = [2, 3, 4, 7]

        def by_vector(n, k):
            return k == 1 or (k == 3 and n % 2 == 0)

        def moved(n, k):
            v = sum(by_vector((i // NB) + 1, i % NB) for i in range((n - 1) * NB + k))
            return v + 1, (n - 1) * NB + k - v

        def tokens_of(n):
            return h_b[:, n - 1] if n else h_cls

        LAST = NG * NCK

        bs = stat[:, 0:30].rearrange("p (k n) -> p k n", n=6)
        mv = stat[:, 30:40].rearrange("p (k n) -> p k n", n=2)
        std, tt = stat[:, 40:45], stat[:, 45:50]
        rs = stat[:, 50:58].rearrange("p (r k) -> p r k", r=2)
        CLS_F = 16

        def pool_parts_c(pool, n0, n1):
            for n in range(n0, n1):
                pool.wait_ge(part_b_ready, n + 1)
                pool.tensor_tensor(parts[:, 2, n % PARTS], xs_m[:, n], parts[:, 1, n % PARTS], ALU.subtract).then_inc(part_c_ready, 1)

        def pool_carry(pool):
            pool.wait_ge(class_token_vector, CLS_F)
            pool.memset(carry[3 * VB:P], 0.0).then_inc(class_token_gpsimd, 1)
            pool.wait_ge(class_token_gpsimd, 1)
            yield
            pool.tensor_copy(cls_a, cls_f).then_inc(class_token_gpsimd, 1)
            pool.wait_ge(class_token_gpsimd, 2)
            yield
            pool.tensor_copy(carry[0:VB, :, 0], cls_a[0:VB]).then_inc(class_token_gpsimd, 1)
            pool.wait_ge(class_token_gpsimd, 3)
            yield
            pool.tensor_copy(carry[0:VB, :, 1], cls_a[VB:2 * VB]).then_inc(class_token_gpsimd, 1)
            pool.wait_ge(class_token_gpsimd, 4)
            yield
            pool.tensor_tensor(cls_f, cls_f, cls_a, ALU.subtract).then_inc(class_token_gpsimd, 1)
            pool.wait_ge(class_token_gpsimd, 5)
            yield
            pool.tensor_copy(cls_a, cls_f).then_inc(class_token_gpsimd, 1)
            pool.wait_ge(class_token_gpsimd, 6)
            yield
            pool.tensor_copy(carry[VB:2 * VB, :, 0], cls_a[0:VB]).then_inc(class_token_gpsimd, 1)
            pool.wait_ge(class_token_gpsimd, 7)
            yield
            pool.tensor_copy(carry[VB:2 * VB, :, 1], cls_a[VB:2 * VB]).then_inc(class_token_gpsimd, 1)
            pool.wait_ge(class_token_gpsimd, 8)
            yield
            pool.tensor_tensor(carry[2 * VB:3 * VB, :, 0], cls_f[HV:HV + VB], cls_a[HV:HV + VB], ALU.subtract).then_inc(class_token_gpsimd, 1)
            pool.wait_ge(class_token_gpsimd, 9)
            yield
            pool.tensor_tensor(carry[2 * VB:3 * VB, :, 1], cls_f[HV + VB:P], cls_a[HV + VB:P], ALU.subtract).then_inc(class_token_gpsimd, 1)
            pool.wait_ge(class_token_gpsimd, 10)
            yield
            pool.wait_ge(constants_loaded, 16)
            pool.wait_ge(expert_weights_turned, 5)
            pool.memset(ones_bf, 1.0).then_inc(constants_ready, 1)
            yield
            pool.tensor_copy(before_bf, c_("before")).then_inc(constants_ready, 1)
            yield
            pool.tensor_copy(ident_bf, ident).then_inc(constants_ready, 1)

        def tile0(n):
            return 0 if n == 0 else 1 + (n - 1) * NB

        def tiles(n):
            return 1 if n == 0 else NB

        def rank(i):
            return 1 - i if i < 2 else i

        def span(n):
            return slice(tile0(n), tile0(n) + tiles(n))

        def h_tiles(n):
            a = (NT - 1) * HID if n == 0 else (n - 1) * GT
            return h[:, a:a + tiles(n) * HID].rearrange("p (k v) -> p k v", v=HID)

        def wide(col, n):
            return col[:, span(n)].unsqueeze(2).to_broadcast([P, tiles(n), HID])

        SEL = 8
        PAD = 32
        a0 = 0

        def by_tile(width, dt=F32):
            nonlocal a0
            cols_ = NT * width if dt == F32 else NT * width // 2
            v = arena[:, a0:a0 + cols_]
            a0 += cols_
            v = v if dt == F32 else v.bitcast(dt)
            return v.rearrange("p (j e) -> p j e", e=width)

        xf, total, gated = by_tile(HID), by_tile(HID), by_tile(HID)
        picked = arena[:, a0:a0 + SEL * EG * HID].rearrange("p (s i f) -> p s i f", s=SEL, i=EG)
        a0 += SEL * EG * HID
        logit, below, expo, key, chosen, counts, chosen_count = (by_tile(E) for _ in range(7))
        eb_raw, eb_rest = gated[:, 0:EG], gated[:, EG:2 * EG]
        chosen_bf = by_tile(PAD, BF16)
        chosen_t = arena[:, a0:a0 + (NG + 1) * P // 2].bitcast(BF16).rearrange("p (n m) -> p n m", m=P)
        a0 += (NG + 1) * P // 2
        assert a0 <= X3
        a0 = PO
        cls_share = arena[:, a0:a0 + (NT - 1) * E].rearrange("p (j e) -> p j e", e=E); a0 += (NT - 1) * E
        eb = arena[:, a0:a0 + 3 * NB * HID // 2].bitcast(BF16).rearrange("p (k n) -> p k n", k=3)
        a0 += 3 * NB * HID // 2
        sum_before = arena[:, a0:a0 + (NG + 1) * PAD // 2].bitcast(BF16).rearrange("p (n e) -> p n e", e=PAD)
        a0 += (NG + 1) * PAD // 2
        sum_two = arena[:, a0:a0 + PAD].bitcast(BF16).rearrange("p (k e) -> p k e", k=2); a0 += PAD
        sum_one = arena[:, a0:a0 + PAD // 2].bitcast(BF16); a0 += PAD // 2
        bs2 = arena[:, a0:a0 + NT * 6].rearrange("p (j n) -> p j n", n=6); a0 += NT * 6
        mv2 = arena[:, a0:a0 + NT * 2].rearrange("p (j n) -> p j n", n=2); a0 += NT * 2
        std2, rs2, tt2, shift2, top, key_top, denom, prob, place, p_keep, p_drop, as_cls = (
            arena[:, a0 + k * NT:a0 + (k + 1) * NT] for k in range(12))
        a0 += 12 * NT
        cls_seen = arena[:, a0:a0 + 2]; a0 += 2
        assert a0 <= arena.shape[1]
        swb = stat[:, 64:64 + E]
        TR4, OHT_BANK, LG_BANK, BI_BANK = 4, 5, 6, 7
        CNT0 = P
        ROUNDS = [(0, 2), (2, 4), (4, NG + 1)]
        CLS0 = GT

        residual_sums_by_gpsimd = sem("residual_sums_by_gpsimd")
        expert_bias_steps = sem("expert_bias_steps")
        expert_bias_loaded = sem("expert_bias_loaded")
        second_norm_steps = sem("second_norm_steps")
        second_variances_ready = sem("second_variances_ready")
        second_deviations_ready = sem("second_deviations_ready")
        second_norm_ready = sem("second_norm_ready")
        normed_tokens_ready = sem("normed_tokens_ready")
        normed_tokens_turned = sem("normed_tokens_turned")
        normed_high_ready = sem("normed_high_ready")
        normed_low_ready = sem("normed_low_ready")
        logits_ready = sem("logits_ready")
        routing_steps = sem("routing_steps")
        logits_below_top_ready = sem("logits_below_top_ready")
        exponentials_ready = sem("exponentials_ready")
        experts_chosen = sem("experts_chosen")
        counts_ready = sem("counts_ready")
        gates_ready = sem("gates_ready")
        chosen_turned_stored = sem("chosen_turned_stored")
        chosen_summed = sem("chosen_summed")
        biases_ready = sem("biases_ready")
        expert_groups_computed = sem("expert_groups_computed")
        first_group_picked = sem("first_group_picked")
        later_groups_picked = sem("later_groups_picked")
        picked_summed = sem("picked_summed")
        biases_added = sem("biases_added")
        dropped_shares_ready = sem("dropped_shares_ready")
        batches_finished = sem("batches_finished")
        gpsimd_sum_steps = sem("gpsimd_sum_steps")
        class_seen = sem("class_seen")
        class_counts_ready = sem("class_counts_ready")
        outputs_stored = sem("outputs_stored")
        normed_tokens_by_vector = sem("normed_tokens_by_vector")
        last_biases_added = sem("last_biases_added")
        last_tiles_finished = sem("last_tiles_finished")
        compared_with_the_class = sem("compared_with_the_class")
        class_seen_stored = sem("class_seen_stored")

        def turned(n):
            return ps[:, OHT_BANK, 2 * P:3 * P] if n == 0 else ps[:, TR4, :]

        def ring_of(ring, n, k0, k1):
            return ring[:, 0, CLS0:CLS0 + P] if n == 0 else ring[:, n % 2, k0 * P:k1 * P]

        def round_tiles(r):
            a, b = ROUNDS[r]
            return slice(tile0(a), tile0(b - 1) + tiles(b - 1))

        def experts_sync(sp):
            sp.wait_ge(expert_bias_steps, 2)
            for k in range(NB):
                sp.dma_start(eb_raw[PAD * k:PAD * k + E, k], expert_b).then_inc(expert_bias_loaded, 16)

            def store(n, k0, k1):
                for par in range(2):
                    sp.dma_start(
                        out[(n - 1) * GI + 2 * k0:(n - 1) * GI + 2 * k1, 1:SEQ].rearrange("(k u) t v -> u t k v", u=2)[par],
                        h_tiles(n)[par * TOK:(par + 1) * TOK, k0:k1]).then_inc(outputs_stored, 16)

            for n in range(1, NG):
                sp.wait_ge(batches_finished, n)
                store(n, 0, NB)
            sp.wait_ge(batches_finished, NG)
            sp.dma_start(out[:, 0], h_tiles(0)[0:B, 0]).then_inc(outputs_stored, 16)
            for k0, k1 in ((0, NB - 1), (NB - 1, NB)):
                sp.wait_ge(last_tiles_finished, k1)
                store(NG, k0, k1)
            sp.wait_ge(outputs_stored, 16 * (2 * NG + 3))

        def experts_pool(pool):
            pool.wait_ge(stage_output_ready, ST * NS8)
            pool.memset(chosen_bf, 0.0).then_inc(expert_bias_steps, 1)
            pool.memset(eb_raw, 0.0).then_inc(expert_bias_steps, 1)
            for g in range(1, NG):
                pool.tensor_tensor(h_b[:, g], h_b[:, g], x3[:, g * NB:(g + 1) * NB].rearrange("p j v -> p (j v)"), ALU.add
                                   ).then_inc(residual_sums_by_gpsimd, 1)
            flat = eb_raw.rearrange("p k f -> p (k f)")
            rest_ = eb_rest.rearrange("p k f -> p (k f)")
            pool.wait_ge(expert_bias_loaded, 16 * NB)
            pool.tensor_copy(eb[:, 0], flat).then_inc(expert_bias_steps, 1)
            pool.wait_ge(expert_bias_steps, 3)
            pool.tensor_tensor(rest_, flat, eb[:, 0], ALU.subtract).then_inc(expert_bias_steps, 1)
            pool.wait_ge(expert_bias_steps, 4)
            pool.tensor_copy(eb[:, 1], rest_).then_inc(expert_bias_steps, 1)
            pool.wait_ge(expert_bias_steps, 5)
            pool.tensor_tensor(eb[:, 2], rest_, eb[:, 1], ALU.subtract).then_inc(expert_bias_steps, 1)
            pool.wait_ge(expert_bias_steps, 3)

            def summed(n):
                pool.wait_ge(experts_chosen, rank(n) + 1)
                o = chosen_bf[:, span(n)]
                b = 3 * (n - 1)
                if n > 1:
                    pool.wait_ge(chosen_summed, b)
                pool.tensor_tensor(sum_two, o[:, 0:2], o[:, 2:4], ALU.add).then_inc(chosen_summed, 1)
                pool.wait_ge(chosen_summed, b + 1)
                pool.tensor_tensor(sum_one, sum_two[:, 0], sum_two[:, 1], ALU.add).then_inc(chosen_summed, 1)
                pool.wait_ge(chosen_summed, b + 2)
                if n == 1:
                    pool.tensor_copy(sum_before[:, n + 1], sum_one).then_inc(chosen_summed, 1)
                else:
                    pool.tensor_tensor(sum_before[:, n + 1], sum_before[:, n], sum_one, ALU.add).then_inc(chosen_summed, 1)

            ps_steps = 0

            def dropped(n):
                nonlocal ps_steps
                if n == 1:
                    pool.wait_ge(normed_tokens_by_vector, 1)
                pool.wait_ge(gates_ready, n if n else NG + 1)
                pool.tensor_tensor(gated[:, span(n)], xf[:, span(n)], wide(p_drop, n), ALU.mult).then_inc(gpsimd_sum_steps, 1)
                ps_steps += 1
                pool.wait_ge(gpsimd_sum_steps, ps_steps)
                pool.tensor_tensor(gated[:, span(n)], gated[:, span(n)], h_tiles(n), ALU.add).then_inc(dropped_shares_ready, 1)

            def sum_picked(t):
                nonlocal ps_steps
                s = picked[:, t % SEL]
                pool.wait_ge(later_groups_picked, (EG - 1) * (rank(t) + 1))
                pool.tensor_tensor(s[:, 0:2], s[:, 0:2], s[:, 2:4], ALU.add).then_inc(gpsimd_sum_steps, 1)
                ps_steps += 1
                pool.wait_ge(gpsimd_sum_steps, ps_steps)
                pool.tensor_tensor(total[:, t], s[:, 0], s[:, 1], ALU.add).then_inc(picked_summed, 1)

            def finish(n, done):
                nonlocal ps_steps
                pool.wait_ge(biases_added, n + 1)
                pool.wait_ge(dropped_shares_ready, done)
                pool.tensor_tensor(total[:, span(n)], total[:, span(n)], wide(p_keep, n), ALU.mult).then_inc(gpsimd_sum_steps, 1)
                ps_steps += 1
                pool.wait_ge(gpsimd_sum_steps, ps_steps)
                pool.tensor_tensor(h_tiles(n), total[:, span(n)], gated[:, span(n)], ALU.add).then_inc(batches_finished, 1)

            for n in range(1, NG + 1):
                if n > 1:
                    dropped(n)
                for k in range(NB):
                    sum_picked(tile0(n) + k)
                    if k == 0 and n == 1:
                        sum_picked(0)
                        dropped(1)
                    if k == 0 and n < NG:
                        summed(n)
                    if k == 1 and n > 1:
                        finish(n - 1, n - 1)
                    if k == 2 and n == NG:
                        dropped(0)
                        finish(0, NG + 1)

        def experts_scalar(act):
            def second_deviations(r):
                act.wait_ge(second_variances_ready, r + 1)
                act.activation(std2[:, round_tiles(r)], mv2[:, round_tiles(r), 1], ACT.Sqrt, bias=eps_col).then_inc(second_deviations_ready, 1)

            def normed(n):
                for r, (a, b) in enumerate(ROUNDS):
                    if n == a:
                        act.wait_ge(second_norm_ready, r + 1)
                if n >= 2:
                    act.wait_ge(residual_sums_by_gpsimd, n - 1)
                for k in range(2 if n == 1 else tiles(n)):
                    t = tile0(n) + k
                    ins = act.activation(xf[:, t], h_tiles(n)[:, k], ACT.Identity, bias=shift2[:, t:t + 1], scale=rs2[:, t:t + 1])
                ins.then_inc(normed_tokens_ready, 1)

            def high(n):
                act.wait_ge(normed_tokens_turned, rank(n) + 1)
                if n >= 3:
                    act.wait_ge(expert_groups_computed, EG * tile0(n - 1))
                act.activation(ring_of(ring_hi, n, 0, NB), turned(n), ACT.Copy).then_inc(normed_high_ready, 1)

            def exponentials(n):
                act.wait_ge(logits_below_top_ready, rank(n) + 1)
                act.activation(expo[:, span(n)], below[:, span(n)], ACT.Exp).then_inc(exponentials_ready, 1)

            def store_turned(n):
                act.wait_ge(counts_ready, rank(n) + 1)
                w = tiles(n) * PAD
                act.activation(chosen_t[0:w, n], turned_bf[0:w], ACT.Copy).then_inc(chosen_turned_stored, 1)

            def first_group(t):
                if t >= SEL:
                    act.wait_ge(picked_summed, rank(t - SEL) + 1)
                act.wait_ge(expert_groups_computed, EG * rank(t) + 1)
                for e in range(EG):
                    ins = act.activation(picked[:, t % SEL, e], ps[:, 0, e * HID:(e + 1) * HID], ACT.Copy,
                                         scale=chosen[:, t, e:e + 1])
                ins.then_inc(first_group_picked, 1)

            second_deviations(0)
            act.wait_ge(second_norm_ready, 1)
            normed(1)
            normed(0)
            high(1)
            high(0)
            second_deviations(1)
            exponentials(1)
            exponentials(0)
            for n in range(1, NG + 1):
                act.wait_ge(experts_chosen, rank(n) + 1)
                for k in range(NB):
                    first_group(tile0(n) + k)
                    if n == 1 and k == 0:
                        store_turned(1)
                        normed(2)
                        act.wait_ge(experts_chosen, rank(0) + 1)
                        first_group(0)
                        store_turned(0)
                    if n < NG:
                        if k == 0:
                            high(n + 1)
                            if n == 2:
                                second_deviations(2)
                        if k == 2 and n + 2 <= NG:
                            normed(n + 2)
                        if k == 1:
                            exponentials(n + 1)
                        if k == 2:
                            store_turned(n + 1)

        def experts_vector(dve):
            dve.wait_ge(stage_output_ready, ST * NS8)
            l2 = 0
            dve.tensor_tensor(h_b[:, 0], h_b[:, 0], x3[:, 0:NB].rearrange("p j v -> p (j v)"), ALU.add).then_inc(second_norm_steps, 1)
            dve.tensor_tensor(h_cls, h_cls, x3[:, NT - 1], ALU.add).then_inc(second_norm_steps, 1)
            l2 += 2

            def statistics(n):
                nonlocal l2
                if n >= 2:
                    dve.wait_ge(residual_sums_by_gpsimd, n - 1)
                else:
                    dve.wait_ge(second_norm_steps, rank(n) + 1)
                for k in range(tiles(n)):
                    dve.bn_stats(bs2[:, tile0(n) + k], h_tiles(n)[:, k]).then_inc(second_norm_steps, 1)
                l2 += tiles(n)
                dve.wait_ge(second_norm_steps, l2)
                for k in range(tiles(n)):
                    ins = dve.bn_aggr(mv2[:, tile0(n) + k], bs2[:, tile0(n) + k])
                if n in (0, 3, NG):
                    ins.then_inc(second_variances_ready, 1)
                else:
                    ins.then_inc(second_norm_steps, 1)
                    l2 += 1

            def second_scales(r):
                nonlocal l2
                t = round_tiles(r)
                dve.wait_ge(second_variances_ready, r + 1)
                dve.wait_ge(second_deviations_ready, r + 1)
                dve.reciprocal(rs2[:, t], std2[:, t]).then_inc(second_norm_steps, 1)
                dve.wait_ge(second_norm_steps, l2 + 1)
                dve.scalar_tensor_tensor(out=tt2[:, t], in0=mv2[:, t, 1], scalar=EPS, in1=rs2[:, t],
                                         op0=ALU.add, op1=ALU.mult).then_inc(second_norm_steps, 1)
                dve.wait_ge(second_norm_steps, l2 + 2)
                dve.scalar_tensor_tensor(out=tt2[:, t], in0=tt2[:, t], scalar=-0.5, in1=rs2[:, t],
                                         op0=ALU.mult, op1=ALU.mult).then_inc(second_norm_steps, 1)
                dve.wait_ge(second_norm_steps, l2 + 3)
                dve.scalar_tensor_tensor(out=rs2[:, t], in0=tt2[:, t], scalar=1.5, in1=rs2[:, t],
                                         op0=ALU.add, op1=ALU.mult).then_inc(second_norm_steps, 1)
                dve.wait_ge(second_norm_steps, l2 + 4)
                l2 += 4
                dve.scalar_tensor_tensor(out=shift2[:, t], in0=mv2[:, t, 0], scalar=-1.0, in1=rs2[:, t],
                                         op0=ALU.mult, op1=ALU.mult).then_inc(second_norm_ready, 1)

            def low_parts(n):
                dve.wait_ge(normed_high_ready, rank(n) + 1)
                dve.tensor_tensor(ring_of(ring_lo, n, 0, NB), turned(n), ring_of(ring_hi, n, 0, NB).bitcast(F32),
                                  ALU.subtract).then_inc(normed_low_ready, 1)

            steps = 0

            def choose(n):
                nonlocal steps
                nt, s = tiles(n), span(n)
                by = lambda col: col[:, s].unsqueeze(2).to_broadcast([P, nt, E])
                dve.wait_ge(logits_ready, rank(n) + 1)
                dve.tensor_tensor(logit[:, s], ps[:, lg_bank(n), 0:nt * E].rearrange("p (k e) -> p k e", e=E),
                                  swb.unsqueeze(1).to_broadcast([P, nt, E]), ALU.add).then_inc(routing_steps, 1)
                dve.wait_ge(routing_steps, steps + 1)
                dve.tensor_reduce(top[:, s], logit[:, s], AX.X, ALU.max).then_inc(routing_steps, 1)
                dve.wait_ge(routing_steps, steps + 2)
                dve.tensor_tensor(below[:, s], logit[:, s], by(top), ALU.subtract).then_inc(logits_below_top_ready, 1)
                dve.wait_ge(logits_below_top_ready, rank(n) + 1)
                dve.scalar_tensor_tensor(out=key[:, s], in0=below[:, s], scalar=0.0,
                                         in1=c_("priority").unsqueeze(1).to_broadcast([P, nt, E]),
                                         op0=ALU.is_ge, op1=ALU.mult).then_inc(routing_steps, 1)
                dve.wait_ge(routing_steps, steps + 3)
                dve.tensor_reduce(key_top[:, s], key[:, s], AX.X, ALU.max).then_inc(routing_steps, 1)
                dve.wait_ge(routing_steps, steps + 4)
                dve.tensor_tensor(chosen[:, s], key[:, s], by(key_top), ALU.is_equal).then_inc(routing_steps, 1)
                if n == 1:
                    dve.wait_ge(expert_bias_steps, 1)
                dve.tensor_tensor(chosen_bf[:, s, 0:E], key[:, s], by(key_top), ALU.is_equal).then_inc(experts_chosen, 1)
                dve.wait_ge(routing_steps, steps + 5)
                steps += 5
                if n == 0:
                    dve.tensor_tensor(cls_share, c_("classes_before").unsqueeze(2).to_broadcast([P, NT - 1, E]),
                                      chosen[:, 0:1].to_broadcast([P, NT - 1, E]), ALU.mult).then_inc(routing_steps, 1)
                    steps += 1
                dve.wait_ge(exponentials_ready, rank(n) + 1)
                dve.tensor_reduce(denom[:, s], expo[:, s], AX.X, ALU.add).then_inc(routing_steps, 1)
                steps += 1
                dve.wait_ge(routing_steps, steps)
                dve.reciprocal(prob[:, s], denom[:, s]).then_inc(routing_steps, 1)
                steps += 1
                dve.wait_ge(routing_steps, steps)

            def as_class(n):
                nonlocal steps
                s = span(n)
                dve.tensor_tensor(chosen_count[:, s], chosen[:, s], chosen[:, 0:1].to_broadcast([P, NB, E]), ALU.mult
                                  ).then_inc(routing_steps, 1)
                dve.wait_ge(routing_steps, steps + 1)
                dve.tensor_reduce(as_cls[:, s], chosen_count[:, s], AX.X, ALU.add).then_inc(compared_with_the_class, 1)
                steps += 1

            def gates(n):
                nonlocal steps
                s = span(n)
                dve.wait_ge(counts_ready, rank(n) + 1)
                dve.tensor_tensor(
                    counts[:, s], ps[:, LG_BANK, CNT0:CNT0 + NB * PAD].rearrange("p (k e) -> p k e", e=PAD)[:, :, 0:E],
                    cls_share[:, (n - 1) * NB:n * NB], ALU.add).then_inc(routing_steps, 1)
                dve.wait_ge(routing_steps, steps + 1)
                dve.tensor_tensor(counts[:, s], counts[:, s], chosen[:, s], ALU.mult).then_inc(routing_steps, 1)
                dve.wait_ge(routing_steps, steps + 2)
                dve.tensor_reduce(place[:, s], counts[:, s], AX.X, ALU.add).then_inc(routing_steps, 1)
                dve.wait_ge(routing_steps, steps + 3)
                steps += 3
                split(s)

            def split(s):
                nonlocal steps
                dve.scalar_tensor_tensor(out=p_keep[:, s], in0=place[:, s], scalar=float(CAP), in1=prob[:, s],
                                         op0=ALU.is_lt, op1=ALU.mult).then_inc(routing_steps, 1)
                dve.wait_ge(routing_steps, steps + 1)
                steps += 1
                dve.tensor_tensor(p_drop[:, s], prob[:, s], p_keep[:, s], ALU.subtract).then_inc(gates_ready, 1)

            def later_groups(t):
                for g in range(1, EG):
                    dve.wait_ge(expert_groups_computed, EG * rank(t) + g + 1)
                    if g == 1:
                        dve.wait_ge(first_group_picked, rank(t) + 1)
                    else:
                        dve.wait_ge(later_groups_picked, (EG - 1) * rank(t) + g - 1)
                    dve.copy_predicated(
                        picked[:, t % SEL], chosen[:, t, g * EG:(g + 1) * EG].bitcast(I32).unsqueeze(2).to_broadcast([P, EG, HID]),
                        ps[:, g, :].rearrange("p (e f) -> p e f", e=EG)).then_inc(later_groups_picked, 1)

            def add_bias(n):
                dve.wait_ge(biases_ready, n + 1)
                dve.wait_ge(picked_summed, tile0(n) + tiles(n) if n else rank(0) + 1)
                dve.tensor_tensor(total[:, span(n)], total[:, span(n)],
                                  ps[:, BI_BANK, 0:tiles(n) * HID].rearrange("p (k f) -> p k f", f=HID), ALU.add
                                  ).then_inc(biases_added, 1)

            def store_seen():
                dve.wait_ge(class_seen, 1)
                dve.tensor_copy(cls_seen[0:NT - 1], ps[0:NT - 1, OHT_BANK, P:P + 2]).then_inc(class_seen_stored, 1)

            def class_gates():
                nonlocal steps
                dve.wait_ge(class_counts_ready, 1)
                dve.tensor_tensor(place[:, 0:1], ps[:, OHT_BANK, P + 4:P + 5], c_("row"), ALU.add).then_inc(routing_steps, 1)
                dve.wait_ge(routing_steps, steps + 1)
                steps += 1
                split(slice(0, 1))

            def finish_last(k):
                t = tile0(NG) + k
                dve.wait_ge(picked_summed, t + 1)
                if k == 0:
                    dve.wait_ge(biases_ready, NG + 1)
                    dve.wait_ge(dropped_shares_ready, NG)
                dve.tensor_tensor(total[:, t], total[:, t], ps[:, BI_BANK, k * HID:(k + 1) * HID], ALU.add
                                  ).then_inc(last_biases_added, 1)
                dve.wait_ge(last_biases_added, k + 1)
                dve.scalar_tensor_tensor(out=h_tiles(NG)[:, k], in0=total[:, t], scalar=p_keep[:, t:t + 1],
                                         in1=gated[:, t], op0=ALU.mult, op1=ALU.add).then_inc(last_tiles_finished, 1)

            def normed_by_vector():
                dve.wait_ge(second_norm_ready, 1)
                for k in range(2, NB):
                    t = tile0(1) + k
                    ins = dve.tensor_scalar(xf[:, t], h_tiles(1)[:, k], rs2[:, t:t + 1], shift2[:, t:t + 1], ALU.mult, ALU.add)
                ins.then_inc(normed_tokens_by_vector, 1)

            statistics(1)
            statistics(0)
            second_scales(0)
            normed_by_vector()
            statistics(2)
            statistics(3)
            low_parts(1)
            low_parts(0)
            statistics(4)
            statistics(5)
            choose(1)
            choose(0)
            as_class(1)
            second_scales(1)
            for n in range(1, NG + 1):
                for k in range(NB):
                    later_groups(tile0(n) + k)
                    if n == 1:
                        if k == 0:
                            gates(1)
                            later_groups(0)
                        else:
                            for m in {1: (6,), 2: (7,), 3: (8,)}[k]:
                                statistics(m)
                    if n < NG:
                        if k == 0:
                            low_parts(n + 1)
                            if n > 1:
                                add_bias(n - 1)
                        if k == 1:
                            choose(n + 1)
                            as_class(n + 1)
                            if n == 1:
                                add_bias(0)
                            if n == 2:
                                second_scales(2)
                        if k == 3:
                            gates(n + 1)
                    else:
                        if k == 0:
                            store_seen()
                            add_bias(n - 1)
                        if k == 1:
                            class_gates()
                        if k:
                            finish_last(k - 1)
            finish_last(NB - 1)

        def experts_tensor(pe):
            def turn(n):
                pe.wait_ge(normed_tokens_ready, rank(n) + 1)
                if n >= 2:
                    pe.wait_ge(normed_high_ready, rank(n))
                    pe.wait_ge(normed_low_ready, rank(n))
                for k in range(tiles(n)):
                    if n == 1 and k == 2:
                        pe.wait_ge(normed_tokens_by_vector, 1)
                    ins = pe.transpose(turned(n)[:, k * P:(k + 1) * P], xf[:, tile0(n) + k], ident)
                ins.then_inc(normed_tokens_turned, 1)

            def logits(n):
                pe.wait_ge(normed_high_ready, rank(n) + 1)
                pe.wait_ge(normed_low_ready, rank(n) + 1)
                if n >= 2:
                    pe.wait_ge(gates_ready, n - 1)
                a = E * HID
                for k in range(tiles(n)):
                    x_h, x_l = (ring_of(q, n, k, k + 1) for q in (ring_hi, ring_lo))
                    o = ps[:, lg_bank(n), k * E:(k + 1) * E]
                    pe.matmul(o, x_h, w_hi[:, a:a + E], start=True, stop=False)
                    pe.matmul(o, x_h, w_lo[:, a:a + E], start=False, stop=False)
                    ins = pe.matmul(o, x_l, w_hi[:, a:a + E], start=False, stop=True)
                ins.then_inc(logits_ready, 1)

            turned_in = ps[:, OHT_BANK, 0:HV].bitcast(BF16)

            def count(n):
                pe.wait_ge(experts_chosen, rank(n) + 1)
                if rank(n):
                    pe.wait_ge(chosen_turned_stored, rank(n))
                w = tiles(n) * PAD
                ins = pe.transpose(turned_in[0:w], chosen_bf[:, span(n)].rearrange("p k e -> p (k e)"), ident_bf)
                if n:
                    cnt = lambda k: ps[:, LG_BANK, CNT0 + k * PAD:CNT0 + NB * PAD]
                    pe.matmul(cnt(0), before_bf, chosen_bf[:, span(n)].rearrange("p k e -> p (k e)"), start=True, stop=False,
                              skip_group_check=True)
                    if n > 1:
                        pe.wait_ge(chosen_summed, 3 * (n - 1))
                        pe.matmul(cnt(0).rearrange("p (k e) -> p k e", e=PAD), ones_bf,
                                  sum_before[:, n:n + 1].to_broadcast([P, NB, PAD]), start=False, stop=False,
                                  skip_group_check=True)
                    for k in range(NB - 1):
                        ins = pe.matmul(cnt(k + 1).rearrange("p (k e) -> p k e", e=PAD), ones_bf,
                                        chosen_bf[:, tile0(n) + k:tile0(n) + k + 1].to_broadcast([P, NB - 1 - k, PAD]),
                                        start=False, stop=(k == NB - 2), skip_group_check=True)
                ins.then_inc(counts_ready, 1)

            def bias(n):
                pe.wait_ge(chosen_turned_stored, rank(n) + 1)
                if n:
                    pe.wait_ge(biases_added, n)
                w, f = tiles(n) * PAD, tiles(n) * HID
                for k in range(3):
                    ins = pe.matmul(ps[:, BI_BANK, 0:f], chosen_t[0:w, n], eb[0:w, k, 0:f], start=(k == 0), stop=(k == 2))
                ins.then_inc(biases_ready, 1)

            def experts(n, k):
                t = tile0(n) + k
                r = rank(t)
                x_h, x_l = (ring_of(q, n, k, k + 1) for q in (ring_hi, ring_lo))
                for g in range(EG):
                    if r:
                        if g == 0:
                            pe.wait_ge(first_group_picked, r)
                        else:
                            pe.wait_ge(later_groups_picked, (EG - 1) * (r - 1) + g)
                    o, a = ps[:, g, :], g * EG * HID
                    pe.matmul(o, x_h, w_hi[:, a:a + EG * HID], start=True, stop=False)
                    pe.matmul(o, x_h, w_lo[:, a:a + EG * HID], start=False, stop=False)
                    pe.matmul(o, x_l, w_hi[:, a:a + EG * HID], start=False, stop=True).then_inc(expert_groups_computed, 1)

            def see_class():
                pe.wait_ge(compared_with_the_class, NG)
                pe.wait_ge(chosen_turned_stored, NG + 1)
                pe.matmul(ps[0:NT - 1, OHT_BANK, P:P + 2], as_cls[:, 1:NT], c_("image_half"), start=True, stop=True
                          ).then_inc(class_seen, 1)

            def class_counts():
                pe.wait_ge(class_seen_stored, 1)
                for k, name in enumerate(("even_before", "odd_before")):
                    ins = pe.matmul(ps[:, OHT_BANK, P + 4:P + 5], c_(name)[0:NT - 1], cls_seen[0:NT - 1, k:k + 1],
                                    start=(k == 0), stop=(k == 1))
                ins.then_inc(class_counts_ready, 1)

            pe.wait_ge(stage_output_ready, ST * NS8)
            turn(1)
            turn(0)
            logits(1)
            logits(0)
            pe.wait_ge(constants_ready, 3)
            for n in range(1, NG + 1):
                for k in range(NB):
                    experts(n, k)
                    if n == 1 and k == 0:
                        count(1)
                        experts(0, 0)
                        count(0)
                    if k == 0 and n < NG:
                        turn(n + 1)
                    if k == 1:
                        if n < NG:
                            logits(n + 1)
                        if n == 1:
                            pe.wait_ge(expert_bias_steps, 6)
                            bias(0)
                        else:
                            bias(n)
                    if k == 2:
                        if n == 1:
                            bias(1)
                        if n < NG:
                            count(n + 1)
                    if k == 0 and n == NG:
                        see_class()
                    if k == 1 and n == NG:
                        class_counts()

        def lg_bank(n):
            return LG_BANK if n else BI_BANK

        turned_bf = ps[:, OHT_BANK, 0:HV].bitcast(BF16)

        @block.sync
        def _(sp):
            sp.dma_start(con[:], consts).then_inc(constants_loaded, 16)
            sp.dma_start(w_raw, tok_w).then_inc(patch_weights_loaded, 16)
            load_images(sp, 0, 0)
            sp.wait_ge(prepared_by_vector, V_FC)
            sp.wait_ge(prepared_by_scalar, A_FB)
            with nc.allow_non_contiguous_dma(reason="padded filter rows of 16 channels"):
                sp.dma_start(toep_rows.rearrange("i a q r k c -> (i a q) (r k c)")[:, 0:(TOK - 1) * 3 * CQ], f_zero
                             ).then_inc(toeplitz_rows_stored, 16)
                for i in range(ST):
                    sp.dma_start(
                        toep_rows[i, :, :, TOK - 1:2 * TOK - 1].rearrange("a q r k c -> r (a q) (k c)"),
                        f_parts[:, i * 2 * NQ:(i + 1) * 2 * NQ].rearrange("p n k c -> p n (k c)")).then_inc(toeplitz_rows_stored, 16)
            sp.wait_ge(prepared_by_tensor, T_F0)
            sp.wait_ge(patch_weights_low, NCK)
            sp.wait_ge(toeplitz_rows_stored, 16 * (1 + ST))
            load_images(sp, 1, 1)
            sp.dma_start(ew_raw.rearrange("p (e d) -> p e d", e=E), expert_w.rearrange("e f d -> f e d")).then_inc(expert_weights_loaded, 16)
            sp.dma_start(sw_raw, switch_w).then_inc(expert_weights_loaded, 16)
            sp.dma_start(stat[:, 64:64 + E], bass.AP(switch_b.tensor, offset=switch_b.offset, ap=[[0, P], [1, E]])
                         ).then_inc(expert_weights_loaded, 16)
            with sp.Fori(1, NG // 2) as i:
                for u in range(2):
                    sp.wait_ge(low_parts_ready, (i * 2 + u - 1) * NCK)
                    load_images(sp, i * 2 + u, u)
            used = (RHO - 1) * 3 * CQ
            sp.dma_start(
                toep_copies.rearrange("i a q z r k c -> (i a q) z (r k c)")[:, :, 0:used],
                toep_rows.rearrange("i a q r k c -> (i a q) (r k c)")[:, 0:used].unsqueeze(1).to_broadcast(
                    [ST * 2 * NQ, COPIES, used])).then_inc(toeplitz_copies_stored, 16)
            sp.wait_ge(toeplitz_copies_stored, 16)
            sp.wait_ge(toeplitz_blocks_zeroed, 2 * NQ - 1)
            for pair, half in ((0, 0), (0, 1), (1, 0)):
                load_toeplitz(sp, 0, pair, half)
            sp.wait_ge(part_c_ready, 2)
            load_toeplitz(sp, 0, 1, 1)
            for i in range(1, ST):
                for pair in range(2):
                    sp.wait_ge(convolved, NS8 * (i - 1) + 4 * pair + 4)
                    for half in range(2):
                        load_toeplitz(sp, i, pair, half)
            experts_sync(sp)

        @block.gpsimd
        def _(pool):
            pool.memset(w_lo[HV:P, 0:WP0].bitcast(F32), 0.0).then_inc(rings_zeroed, 1)
            for ring in (ring_hi, ring_lo):
                for r in range(2):
                    pool.memset(ring[HV:P, r].bitcast(F32), 0.0).then_inc(rings_zeroed, 1)
            def zero_slot(q, half):
                other = 1 - half
                pool.memset(toep[half * TOK:(half + 1) * TOK, q, other * TOK * 3 * CQ:(other + 1) * TOK * 3 * CQ
                                 ].bitcast(F32), 0.0).then_inc(toeplitz_blocks_zeroed, 1)

            pool.wait_ge(rings_zeroed, 6)
            pool.wait_ge(low_parts_ready, (NG - 1) * NCK)
            for half in (1, 0):
                for q in range(NQ if half else NQ - 1):
                    zero_slot(q, half)
            pool.wait_ge(toeplitz_blocks_zeroed, 2 * NQ - 1)
            for n in range(NG + 1):
                src = tokens_of(n)
                w = src.shape[1]
                pool.wait_ge(token_high_ready, n + 1)
                pool.tensor_tensor(ring_lo[:, n % 2, 0:w], src, ring_hi[:, n % 2, 0:w].bitcast(F32), ALU.subtract
                                   ).then_inc(token_low_ready, 1)
                if n == 4:
                    work = pool_carry(pool)
                if n >= 4:
                    pool.wait_ge(token_low_ready, n + 1)
                    for _ in range(3):
                        next(work, None)
            pool_parts_c(pool, 0, 2)
            pool.wait_ge(part_c_ready, 2)
            zero_slot(NQ - 1, 0)
            pool.wait_ge(toeplitz_blocks_zeroed, 2 * NQ)
            pool_parts_c(pool, 2, ST * NS8)
            experts_pool(pool)

        @block.scalar
        def _(act):
            for dst, src in ((fp_t, filt_pos_t), (wp_raw, w_proj.rearrange("w v s -> w (v s)")),
                             (wf_raw, w_filt.rearrange("w v s -> w (v s)")), (pos_raw, pos_embed[1:SEQ]),
                             (b_col, tok_b.rearrange("(p o) -> p o", o=1)),
                             (ct_col, class_token.rearrange("o p -> p o")),
                             (p0_col, pos_embed[0:1].rearrange("o p -> p o"))):
                act.dma_start(dst, src).then_inc(small_loaded, 16)

            act.wait_ge(prepared_by_vector, V_EPS)
            act.activation(cols[:, 5:6], eps_col, ACT.Sqrt)
            act.wait_ge(rings_zeroed, 6)
            for b in range(NCK):
                act.wait_ge(patch_weights_turned, b + 1)
                act.activation(w_hi[0:ROWS, b * GT:(b + 1) * GT], ps[0:ROWS, b % WT_BANKS, :], ACT.Copy
                               ).then_inc(patch_weights_high, 1)

            act.wait_ge(prepared_by_vector, V_MID)
            act.activation(w_hi[:, WP0:], wp_mid, ACT.Copy).then_inc(prepared_by_scalar, 1)
            act.wait_ge(prepared_by_tensor, T_F)
            act.activation(f_parts[:, :, 0], f_sums, ACT.Copy).then_inc(prepared_by_scalar, 1)
            act.wait_ge(prepared_by_vector, V_FREST)
            act.activation(f_parts[:, :, 1], f_rest_n, ACT.Copy).then_inc(prepared_by_scalar, 1)
            for u in range(2):
                for k in range(NCK):
                    n = u * NCK + k
                    if k == 0:
                        act.wait_ge(images_loaded[u], X_LOADED)
                    if n >= 2:
                        act.wait_ge(high_parts_used, n - 1)
                        act.wait_ge(low_parts_ready, n - 1)
                    act.activation(hi_chunk[0:ROWS, n % 2], x_chunk[0:ROWS, u, :, k * CK:(k + 1) * CK], ACT.Copy
                                   ).then_inc(high_parts_ready, 1)
            with act.Fori(1, NG // 2) as i:
                for u in range(2):
                    for k in range(NCK):
                        n0 = i * (2 * NCK) + (u * NCK + k)
                        r = (u * NCK + k) % 2
                        if k == 0:
                            act.wait_ge(images_loaded[u], i * X_LOADED + X_LOADED)
                        act.wait_ge(high_parts_used, n0 - 1)
                        act.wait_ge(low_parts_ready, n0 - 1)
                        act.activation(hi_chunk[0:ROWS, r], x_chunk[0:ROWS, u, :, k * CK:(k + 1) * CK], ACT.Copy
                                       ).then_inc(high_parts_ready, 1)

            for k in range(4):
                act.wait_ge(expert_weights_turned, k + 1)
                act.wait_ge(high_parts_used, LAST - NCK + k + 1)
                act.wait_ge(low_parts_used, LAST - NCK + k + 1)
                act.activation(w_hi[:, k * GT:(k + 1) * GT], ps[:, EW_BANKS[k], :], ACT.Copy).then_inc(expert_weights_high, 1)
            act.wait_ge(low_parts_used, LAST - NCK + 5)
            act.wait_ge(expert_weights_turned, 5)
            act.activation(w_hi[:, E * HID:E * HID + E], ps[:, EW_BANKS[3], 0:E], ACT.Copy).then_inc(expert_weights_high, 1)

            act.wait_ge(high_parts_used, LAST)
            act.wait_ge(low_parts_used, LAST)

            def high(n):
                src = tokens_of(n)
                if n >= 2:
                    act.wait_ge(projected, 1 if n == 2 else (n - 2) * NB + 1)
                act.activation(ring_hi[:, n % 2, 0:src.shape[1]], src, ACT.Copy).then_inc(token_high_ready, 1)

            def by_row(n):
                src = tokens_of(n)
                act.wait_ge(tokens_turned, n + 1)
                act.wait_ge(token_low_ready, n + 1)
                act.activation(src, ps[:, TR_BANKS[n % 2], 0:src.shape[1]], ACT.Copy).then_inc(tokens_stored_by_row, 1)

            def deviations(n):
                act.wait_ge(variances_ready, n + 1)
                nt = tokens_of(n).shape[1] // P
                k = NB if n == 0 else 0
                act.activation(std[:, k:k + nt], mv[:, k:k + nt, 1], ACT.Sqrt, bias=eps_col).then_inc(deviations_ready, 1)

            def move(n, k):
                if k == 0:
                    act.wait_ge(scales_ready, n + 1)
                j = (n - 1) * NB + k
                act.wait_ge(projected, j + 2)
                src = ps[:, PR_BANKS[k], :].rearrange("p (s v) -> p s v", s=4)
                sc = rs[:, n % 2, k:k + 1]
                for par in range(2):
                    rows = slice(par * TOK, (par + 1) * TOK)
                    for half in range(2):
                        act.activation(xs_q[half * HV:(half + 1) * HV, :, :, 2 * j + par:2 * j + par + 1],
                                       src[rows, 0:ST, half * HV:(half + 1) * HV].unsqueeze(3), ACT.Copy, scale=sc[rows])
                act.activation(x3[:, j:j + 1, :], src[:, ST:ST + 1, :], ACT.Copy, scale=sc).then_inc(projections_moved_by_scalar, 1)

            act.wait_ge(prepared_by_vector, V_CLS)
            high(0)
            act.wait_ge(tokens_ready, NG)
            high(1)
            by_row(0)
            by_row(1)
            deviations(0)
            deviations(1)
            high(2)
            for n in range(1, NG + 1):
                move(n, 0)
                if n < NG:
                    by_row(n + 1)
                move(n, 2)
                if n + 2 <= NG:
                    high(n + 2)
                if n < NG:
                    deviations(n + 1)
                if not by_vector(n, 3):
                    move(n, 3)

            act.wait_ge(projections_moved_by_vector, moved(NG, NB)[0])
            act.wait_ge(projections_moved_by_scalar, moved(NG, NB)[1])
            for st in range(ST):
                for g in range(NS8 + 1):
                    n = st * NS8 + g
                    if g < NS8:
                        if st:
                            act.wait_ge(stage_output_ready, n - NS8 + 1)
                        elif g == 0:
                            act.wait_ge(class_token_gpsimd, 10)
                        if n >= PARTS:
                            act.wait_ge(convolved, n - PARTS + 1)
                        act.activation(parts[:, 0, n % PARTS], xs_m[:, n], ACT.Copy).then_inc(part_a_ready, 1)
                    if g:
                        act.wait_ge(rest_ready, n)
                        act.activation(parts[:, 1, (n - 1) % PARTS], xs_m[:, n - 1], ACT.Copy).then_inc(part_b_ready, 1)
            experts_scalar(act)

        @block.vector
        def _(dve):
            def prep(ins):
                ins.then_inc(prepared_by_vector, 1)

            prep(dve.memset(eps_col, EPS))
            dve.memset(w_hi[HV:P, 0:WP0].bitcast(F32), 0.0).then_inc(rings_zeroed, 1)
            prep(dve.memset(mean_w, 1.0 / HID))
            prep(dve.memset(f_zero, 0.0))
            dve.wait_ge(rings_zeroed, 6)
            for b in range(NCK):
                dve.wait_ge(patch_weights_high, b + 1)
                dve.tensor_tensor(w_lo[0:ROWS, b * GT:(b + 1) * GT], ps[0:ROWS, b % WT_BANKS, :],
                                  w_hi[0:ROWS, b * GT:(b + 1) * GT].bitcast(F32), ALU.subtract).then_inc(patch_weights_low, 1)
            dve.wait_ge(small_loaded, 16 * N_SMALL)
            dve.wait_ge(constants_loaded, 16)
            prep(dve.tensor_copy(select[:], c_("select")))
            prep(dve.tensor_tensor(hc_col, ct_col, p0_col, ALU.mult))
            two = wf_two.rearrange("p (i a d v) -> p i a d v", i=ST, a=2, d=2)
            for i in range(ST):
                for d in range(2):
                    prep(dve.tensor_copy(two[:, i, :, d], f_view[:, i].rearrange("p (a v) -> p a v", a=2)))
            prep(dve.tensor_copy(fp0, fp_t[:, 0:1].to_broadcast([P, P])))
            dve.wait_ge(prepared_by_vector, V_HC)
            prep(dve.tensor_copy(h_cls, hc_col.to_broadcast([P, P])))
            dve.wait_ge(prepared_by_tensor, T_POS)
            prep(dve.tensor_copy(pos_t[:], ps[:, POS_BANK, 0:TOK]))
            dve.wait_ge(prepared_by_tensor, T_MEAN)
            prep(dve.tensor_tensor(
                wp_mid.rearrange("p (s v) -> p s v", s=4), wp_raw.rearrange("p (v s) -> p s v", s=4),
                ps[:, MEAN_BANK, :].rearrange("p (v s) -> p s v", s=4), ALU.subtract))
            dve.wait_ge(prepared_by_vector, V_MID)
            dve.wait_ge(prepared_by_scalar, A_WPHI)
            prep(dve.tensor_tensor(w_lo[:, WP0:], wp_mid, w_hi[:, WP0:].bitcast(F32), ALU.subtract))
            dve.wait_ge(prepared_by_scalar, A_FA)
            prep(dve.tensor_tensor(f_rest_n, f_sums, f_parts[:, :, 0], ALU.subtract))
            dve.wait_ge(prepared_by_scalar, A_FB)
            dve.wait_ge(prepared_by_vector, V_FREST)
            prep(dve.tensor_tensor(f_parts[:, :, 2], f_rest_n, f_parts[:, :, 1], ALU.subtract))
            def low(u, k):
                r = (u * NCK + k) % 2
                dve.tensor_tensor(lo_chunk[0:ROWS, r], x_chunk[0:ROWS, u, :, k * CK:(k + 1) * CK],
                                  hi_chunk[0:ROWS, r].bitcast(F32), ALU.subtract).then_inc(low_parts_ready, 1)

            def tokens(g, bank):
                dve.wait_ge(low_parts_used, g * NCK + NCK)
                dve.scalar_tensor_tensor(
                    out=h_b[:, g].rearrange("p (b t) -> p b t", b=GI), in0=ps[:, bank, :].rearrange("p (b t) -> p b t", b=GI),
                    scalar=b_col, in1=pos_t[:].unsqueeze(1).to_broadcast([P, GI, TOK]),
                    op0=ALU.add, op1=ALU.mult).then_inc(tokens_ready, 1)

            dve.wait_ge(prepared_by_vector, V_POS)
            for u in range(2):
                for k in range(NCK):
                    n = u * NCK + k
                    dve.wait_ge(high_parts_ready, n + 1)
                    if n >= 2:
                        dve.wait_ge(low_parts_used, n - 1)
                    low(u, k)
                    if u and k == 1:
                        tokens(0, 0)
            with dve.Fori(1, NG // 2) as i:
                for u in range(2):
                    for k in range(NCK):
                        n = i * (2 * NCK) + (u * NCK + k)
                        dve.wait_ge(high_parts_ready, n + 1)
                        dve.wait_ge(low_parts_used, n - 1)
                        low(u, k)
                        if k == 1:
                            tokens(i * 2 + (u - 1), 1 - u)

            for k in range(5):
                dve.wait_ge(expert_weights_high, k + 1)
                a, w, bank = (k * GT, GT, EW_BANKS[k]) if k < 4 else (E * HID, E, EW_BANKS[3])
                dve.tensor_tensor(w_lo[:, a:a + w], ps[:, bank, 0:w], w_hi[:, a:a + w].bitcast(F32), ALU.subtract
                                  ).then_inc(expert_weights_low, 1)
                if k == 3:
                    tokens(NG - 1, 1)

            dv = 0

            def variances(n):
                nonlocal dv
                src = tokens_of(n)
                nt = src.shape[1] // P
                k0 = 0 if n else NB
                dve.wait_ge(tokens_stored_by_row, n + 1)
                for k in range(nt):
                    dve.bn_stats(bs[:, k0 + k], src[:, k * P:(k + 1) * P]).then_inc(vector_steps, 1)
                dv += nt
                dve.wait_ge(vector_steps, dv)
                for k in range(nt):
                    ins = dve.bn_aggr(mv[:, k0 + k], bs[:, k0 + k])
                ins.then_inc(variances_ready, 1)

            def scales(n):
                nonlocal dv
                nt = tokens_of(n).shape[1] // P
                k = slice(0, nt) if n else slice(NB, NB + 1)
                r_ = rs[:, n % 2, 0:nt]
                dve.wait_ge(variances_ready, n + 1)
                dve.wait_ge(deviations_ready, n + 1)
                dve.reciprocal(r_, std[:, k]).then_inc(vector_steps, 1)
                dve.wait_ge(vector_steps, dv + 1)
                dve.scalar_tensor_tensor(out=tt[:, k], in0=mv[:, k, 1], scalar=EPS, in1=r_,
                                         op0=ALU.add, op1=ALU.mult).then_inc(vector_steps, 1)
                dve.wait_ge(vector_steps, dv + 2)
                dve.scalar_tensor_tensor(out=tt[:, k], in0=tt[:, k], scalar=-0.5, in1=r_,
                                         op0=ALU.mult, op1=ALU.mult).then_inc(vector_steps, 1)
                dve.wait_ge(vector_steps, dv + 3)
                dv += 3
                dve.scalar_tensor_tensor(out=r_, in0=tt[:, k], scalar=1.5, in1=r_,
                                         op0=ALU.add, op1=ALU.mult).then_inc(scales_ready, 1)
                dve.wait_ge(scales_ready, n + 1)

            def move(n, k):
                j = (n - 1) * NB + k
                dve.wait_ge(projected, j + 2)
                src = ps[:, PR_BANKS[k], :].rearrange("p (s v) -> p s v", s=4)
                sc = rs[:, n % 2, k:k + 1]
                for par in range(2):
                    rows = slice(par * TOK, (par + 1) * TOK)
                    for half in range(2):
                        dve.tensor_scalar(xs_q[half * HV:(half + 1) * HV, :, :, 2 * j + par:2 * j + par + 1],
                                          src[rows, 0:ST, half * HV:(half + 1) * HV].unsqueeze(3), sc[rows], None, ALU.mult)
                dve.tensor_scalar(x3[:, j:j + 1, :], src[:, ST:ST + 1, :], sc, None, ALU.mult).then_inc(projections_moved_by_vector, 1)

            variances(0)
            variances(1)
            scales(0)
            scales(1)
            dve.wait_ge(projected, 1)
            dve.tensor_scalar(cls_x.rearrange("p s v -> p (s v)"), ps[:, CLS_BANK, :], rs[:, 0, 0:1], None, ALU.mult
                              ).then_inc(projections_moved_by_vector, 1)
            for n in range(1, NG + 1):
                move(n, 1)
                if n < NG:
                    variances(n + 1)
                if by_vector(n, 3):
                    move(n, 3)
                if n < NG:
                    scales(n + 1)
                if n == 1:
                    dve.wait_ge(projections_moved_by_vector, 1)
                    y = cls_x[:, 0]
                    for i in range(ST):
                        dve.tensor_tensor(cls_t, y, ps[:, F0_BANK, i * HID:(i + 1) * HID], ALU.mult).then_inc(class_token_vector, 1)
                        dve.wait_ge(class_token_vector, 2 * i + 1)
                        to = x3[:, NT - 1] if i == ST - 1 else cls_y[:, i + 1]
                        dve.tensor_tensor(to, cls_t, cls_x[:, i + 1], ALU.mult).then_inc(class_token_vector, 1)
                        dve.wait_ge(class_token_vector, 2 * i + 2)
                        y = to
                    for i in range(ST):
                        src = (cls_x[:, 0] if i == 0 else cls_y[:, i]).rearrange("p (a v) -> p a v", a=2)
                        dve.tensor_copy(cls_two[:, i], src.unsqueeze(2).to_broadcast([P, 2, 2, HV])).then_inc(class_token_vector, 1)
                if n == 2:
                    dve.wait_ge(class_token_tensor, 1)
                    dve.tensor_copy(cls_col, ps[:, F0_BANK, ST * HID:ST * HID + 6]).then_inc(class_token_vector, 1)
                    dve.wait_ge(class_token_vector, 10)
                    for i in range(ST):
                        for a in range(2):
                            dve.tensor_scalar(cls_f[:, i, a * TOK:(a + 1) * TOK],
                                              ps[:, FT_BANK, (2 * i + a) * TOK:(2 * i + a + 1) * TOK],
                                              cls_col[:, 2 * i + a:2 * i + a + 1], None, ALU.mult).then_inc(class_token_vector, 1)

            x3_q = x3[:, 0:NT - 1].rearrange("p j v -> p v j")

            def rest(n):
                if n >= NS8:
                    dve.wait_ge(stage_output_ready, n - NS8 + 1)
                dve.wait_ge(part_a_ready, n + 1)
                dve.tensor_tensor(xs_m[:, n], xs_m[:, n], parts[:, 0, n % PARTS], ALU.subtract).then_inc(rest_ready, 1)

            def multiply(n):
                g = n % NS8
                dve.wait_ge(convolved, n + 1)
                if n < (ST - 1) * NS8:
                    m = n + NS8
                    dve.tensor_tensor(xs_m[:, m], ps[:, g, :], xs_m[:, m], ALU.mult).then_inc(stage_output_ready, 1)
                    return
                src = ps[:, g, :].rearrange("p (v j u) -> p v j u", v=G8, u=2)
                for half in range(2):
                    for par in range(2):
                        to = x3_q[par * TOK:(par + 1) * TOK, half * HV + g * G8:half * HV + (g + 1) * G8]
                        ins = dve.tensor_tensor(to, src[half * HV:(half + 1) * HV, :, :, par], to, ALU.mult)
                ins.then_inc(stage_output_ready, 1)

            dve.wait_ge(projections_moved_by_vector, moved(NG, NB)[0])
            dve.wait_ge(projections_moved_by_scalar, moved(NG, NB)[1])
            for n in range(PARTS):
                rest(n)
            for n in range(ST * NS8):
                multiply(n)
                if n + PARTS < ST * NS8:
                    rest(n + PARTS)
            experts_vector(dve)

        @block.tensor
        def _(pe):
            pe.wait_ge(constants_loaded, 16)
            pe.wait_ge(patch_weights_loaded, 16)
            for b in range(NCK):
                if b >= WT_BANKS:
                    pe.wait_ge(patch_weights_low, b - WT_BANKS + 1)
                for k in range(CK):
                    ins = pe.transpose(ps[0:ROWS, b % WT_BANKS, k * HID:(k + 1) * HID], w_view[:, :, b * CK + k], ident)
                ins.then_inc(patch_weights_turned, 1)
            pe.wait_ge(small_loaded, 16 * N_SMALL)
            pe.transpose(ps[:, POS_BANK, 0:TOK], pos_raw, ident[0:TOK, 0:TOK]).then_inc(prepared_by_tensor, 1)
            pe.wait_ge(prepared_by_vector, V_MEAN)
            pe.matmul(ps[:, MEAN_BANK, :], mean_w, wp_raw, start=True, stop=True).then_inc(prepared_by_tensor, 1)
            pe.matmul(ps[0:TOK, F_BANK, 0:ST * HID], fp_t[:, 0:TOK], f_view, start=True, stop=True).then_inc(prepared_by_tensor, 1)
            pe.wait_ge(prepared_by_vector, V_FP0)
            for k in range(2 * ST):
                ins = pe.matmul(ps[:, FT_BANK, k * TOK:(k + 1) * TOK], wf_two[:, k * P:(k + 1) * P], fp_t[:, 1:SEQ],
                                start=True, stop=True)
            ins.then_inc(prepared_by_tensor, 1)
            pe.matmul(ps[:, F0_BANK, 0:ST * HID], fp0, f_view, start=True, stop=True).then_inc(prepared_by_tensor, 1)

            pe.wait_ge(patch_weights_low, NCK)
            pe.wait_ge(patch_weights_high, NCK)
            def two_groups(i):
                for u in range(2):
                    for k in range(NCK):
                        r = (u * NCK + k) % 2
                        n = i * (2 * NCK) + (u * NCK + k)
                        pe.wait_ge(high_parts_ready, n + 1)
                        for j in range(CK):
                            for w in (w_hi, w_lo):
                                a = (k * CK + j) * HID
                                ins = pe.matmul(ps[:, u, :], w[:, a:a + HID], ring_hi[:, r, j * GT:(j + 1) * GT],
                                                start=(k == 0 and j == 0 and w is w_hi), stop=False)
                        ins.then_inc(high_parts_used, 1)
                        pe.wait_ge(low_parts_ready, n + 1)
                        for j in range(CK):
                            a = (k * CK + j) * HID
                            ins = pe.matmul(ps[:, u, :], w_hi[:, a:a + HID], ring_lo[:, r, j * GT:(j + 1) * GT],
                                            start=False, stop=(k == NCK - 1 and j == CK - 1))
                        ins.then_inc(low_parts_used, 1)

            with pe.Fori(0, NG // 2 - 1) as i:
                two_groups(i)
            pe.wait_ge(expert_weights_loaded, 48)
            pe.wait_ge(prepared_by_vector, V_MID)
            pe.wait_ge(prepared_by_scalar, A_FB)
            for k in range(4):
                for j in range(EG):
                    e = k * EG + j
                    ins = pe.transpose(ps[:, EW_BANKS[k], j * HID:(j + 1) * HID], ew_raw[:, e * HID:(e + 1) * HID], ident)
                ins.then_inc(expert_weights_turned, 1)
            two_groups(NG // 2 - 1)
            pe.wait_ge(expert_weights_low, 4)
            pe.transpose(ps[:, EW_BANKS[3], 0:E], sw_raw, ident[0:E, 0:E]).then_inc(expert_weights_turned, 1)

            def turn(n):
                src = tokens_of(n)
                if n >= 2:
                    pe.wait_ge(tokens_stored_by_row, n - 1)
                for k in range(src.shape[1] // P):
                    ins = pe.transpose(ps[:, TR_BANKS[n % 2], k * P:(k + 1) * P], src[:, k * P:(k + 1) * P], ident)
                ins.then_inc(tokens_turned, 1)

            def project(n, k):
                x_h, x_l = (q[:, n % 2, k * P:(k + 1) * P] for q in (ring_hi, ring_lo))
                out_ = ps[:, PR_BANKS[k] if n else CLS_BANK, :]
                pe.matmul(out_, x_h, w_hi[:, WP0:], start=True, stop=False)
                pe.matmul(out_, x_h, w_lo[:, WP0:], start=False, stop=False)
                pe.matmul(out_, x_l, w_hi[:, WP0:], start=False, stop=True).then_inc(projected, 1)

            pe.wait_ge(prepared_by_vector, V_WPLO)
            turn(0)
            turn(1)
            pe.wait_ge(token_high_ready, 1)
            pe.wait_ge(token_low_ready, 1)
            pe.wait_ge(expert_weights_low, 5)
            project(0, 0)
            pe.wait_ge(tokens_ready, NG)
            for n in range(1, NG + 1):
                if n < NG:
                    turn(n + 1)
                pe.wait_ge(token_high_ready, n + 1)
                pe.wait_ge(token_low_ready, n + 1)
                for k in range(NB):
                    if n > 1:
                        pe.wait_ge(*((projections_moved_by_vector, moved(n - 1, k + 1)[0]) if by_vector(n - 1, k) else
                                     (projections_moved_by_scalar, moved(n - 1, k + 1)[1])))
                    elif PR_BANKS[k] == CLS_BANK:
                        pe.wait_ge(projections_moved_by_vector, 1)
                    project(n, k)
                if n == 2:
                    pe.wait_ge(class_token_vector, 9)
                    for k in range(6):
                        ins = pe.matmul(ps[:, F0_BANK, ST * HID + k:ST * HID + k + 1],
                                        cls_two[:, k // 2, k % 2].rearrange("p d v -> p (d v)"), ident[:, 0:1],
                                        start=True, stop=True)
                    ins.then_inc(class_token_tensor, 1)

            pe.wait_ge(class_token_gpsimd, 10)
            pe.wait_ge(projections_moved_by_vector, moved(NG, NB)[0])
            pe.wait_ge(projections_moved_by_scalar, moved(NG, NB)[1])
            pe.wait_ge(prepared_by_vector, V_SELECT)
            toep_v = toep.rearrange("p q (t k c) -> p q t k c", k=3, c=CQ)
            with pe.Fori(0, ST) as st:
                for g in range(NS8):
                    q = g // 2
                    if g == 4:
                        pe.wait_ge(toeplitz_blocks_zeroed, 2 * NQ)
                    if g % 4 == 0:
                        pe.wait_ge(toeplitz_loaded[g // 4], st * T_LOADED + T_LOADED)
                    pe.wait_ge(part_a_ready, st * NS8 + (g + 1))
                    b, v0 = g * G8 // VB, g * G8 % VB
                    rows = select[:, v0:v0 + G8].unsqueeze(2).to_broadcast([P, G8, B])
                    bank = ps[:, g, :].rearrange("p (c b) -> p c b", c=G8)
                    pe.matmul(bank, carry[:, bass.ds(st, 1), b, :].rearrange("p o n -> p (o n)"), rows, start=True, stop=False,
                              skip_group_check=True)
                    for j, ready in enumerate((part_a_ready, part_b_ready, part_c_ready)):
                        if j:
                            pe.wait_ge(ready, st * NS8 + (g + 1))
                        for c in range(G8):
                            for k in range(3 - j):
                                ins = pe.matmul(ps[:, g, c * B:(c + 1) * B], toep_v[:, q, :, k, (g % 2) * G8 + c],
                                                parts[:, j, g % PARTS, c * B:(c + 1) * B], start=False,
                                                stop=(c == G8 - 1 and j == 2), skip_group_check=True)
                    ins.then_inc(convolved, 1)
            experts_tensor(pe)


_INS = ["x", "L0_tok_W", "L0_tok_b", "L0_tok_class_token", "L0_tok_pos_embed", "L0_attn_W_proj", "L0_attn_W_filt",
        "L0_ffn_switch_w", "L0_ffn_switch_b", "L0_ffn_expert_w", "L0_ffn_expert_b"]
_OUTS = [((B, SEQ, HID), "float32")]


def kernel(**inputs):
    import numpy as _np
    import concourse.bacc as _bacc
    from concourse import mybir as _mybir
    from concourse.bass_utils import run_bass_kernel_spmd as _run

    nc = _bacc.Bacc("TRN2", target_bir_lowering=False, num_devices=1)
    arrays, args = {}, []
    given = {name: _np.ascontiguousarray(inputs[name]) for name in _INS}
    given["constants"] = CONSTS
    given["filter_positions"] = positions_t()
    for name, a in given.items():
        arrays[f"in_{name}_dram"] = a
        args.append(nc.dram_tensor(f"in_{name}_dram", a.shape, _mybir.dt.from_np(a.dtype), kind="ExternalInput").ap())
    for i, (shape, dtype) in enumerate(_OUTS):
        args.append(nc.dram_tensor(f"out_{i}_dram", shape, _mybir.dt.from_np(_np.dtype(dtype)), kind="ExternalOutput").ap())
    build(nc, *args)
    r = _run(nc, [arrays], core_ids=[0])
    return r.results[0]["out_0_dram"]
```
